# Optimizing a Trainium2 kernel written in Bass

```python
import numpy as np
import jax
import jax.numpy as jnp

def _softmax(x, axis=-1):
    return jax.nn.softmax(x, axis=axis)

def _gelu(x):
    return jax.nn.gelu(x, approximate=True)

def _silu(x):
    return jax.nn.silu(x)

def _sigmoid(x):
    return jax.nn.sigmoid(x)

def _layernorm(x, axis=-1, eps=1e-05):
    m = jnp.mean(x, axis=axis, keepdims=True)
    v = jnp.var(x, axis=axis, keepdims=True)
    return (x - m) / jnp.sqrt(v + eps)

def _scatter_add(tgt, idx, src, axis=0):
    return tgt.at[idx].add(src)

def _segment_sum(src, seg, n):
    return jax.ops.segment_sum(src, seg, n)
kernel_name = 'mk_gnn_ffn_d1_gnn_r8_b77dbd'

def setup_inputs(seed: int=0):
    np.random.seed(seed)
    _w = jnp.asarray

    def _rec_inputs():
        import jax
        import jax.numpy as jnp
        _gk = jax.random.key(seed)
        x = -0.0003713 + 1 * jax.random.normal(jax.random.fold_in(_gk, 1), (6250, 256), jnp.float32)
        _s = jax.random.randint(jax.random.fold_in(_gk, 2), (100000,), 0, 6250, jnp.int32)
        _d = jax.random.randint(jax.random.fold_in(_gk, 3), (100000,), 0, 6250, jnp.int32)
        _loop = jnp.arange(6250, dtype=jnp.int32)
        src = jnp.concatenate([_s, _d, _loop])
        dst = jnp.concatenate([_d, _s, _loop])
        _o = jnp.argsort(dst, stable=True)
        src = src[_o]
        dst = dst[_o]
        edge_weight = jax.random.uniform(jax.random.fold_in(_gk, 12), (206250,), jnp.float32, 0.0, 1)
        return (x, src, dst, edge_weight)
    x, src, dst, edge_weight = _rec_inputs()

    def _L0_gnn_setup():
        import jax, jax.numpy as jnp
        import numpy as np
        N_NODES = 6250
        N_EDGES = 200000
        D_IN = 256
        D_OUT = 256
        K_HOPS = 2

        def spmm(edge_src, edge_dst, edge_val, h):
            msgs = edge_val[:, None] * h[edge_src]
            return jax.ops.segment_sum(msgs, edge_dst, num_segments=N_NODES)
        key = jax.random.key(seed)
        ks = jax.random.split(key, 6)
        x = jax.random.normal(ks[0], (N_NODES, D_IN), dtype=jnp.float32)
        edge_src = jax.random.randint(ks[1], (N_EDGES,), 0, N_NODES, dtype=jnp.int32)
        edge_dst = jax.random.randint(ks[2], (N_EDGES,), 0, N_NODES, dtype=jnp.int32)
        edge_val = jax.random.uniform(ks[3], (N_EDGES,), dtype=jnp.float32)
        stdv = 1.0 / np.sqrt(D_OUT)
        W = jax.random.uniform(ks[4], (K_HOPS, D_IN, D_OUT), dtype=jnp.float32, minval=-stdv, maxval=stdv)
        bias = jax.random.uniform(ks[5], (D_OUT,), dtype=jnp.float32, minval=-stdv, maxval=stdv)
        return {'x': x, 'edge_src': edge_src, 'edge_dst': edge_dst, 'edge_val': edge_val, 'W': W, 'bias': bias}
    _L0_gnn_all = _L0_gnn_setup()
    _L0_gnn_in = {k: v for k, v in _L0_gnn_all.items() if k in ('W', 'bias')}
    del _L0_gnn_all

    def _L0_ffn_setup():
        import jax, jax.numpy as jnp
        import numpy as np
        B, S, H, F, E, K = (8, 512, 256, 512, 16, 2)
        EPS = 1e-05
        key = jax.random.key(seed)
        ks = jax.random.split(key, 9)
        sc = 0.02
        return {'x': jax.random.normal(ks[0], (B, S, H), dtype=jnp.float32), 'gate_w': jax.random.normal(ks[1], (H, E), dtype=jnp.float32) * sc, 'gate_b': jnp.zeros((E,), dtype=jnp.float32), 'w1': jax.random.normal(ks[2], (E, H, F), dtype=jnp.float32) * sc, 'b1': jnp.zeros((E, F), dtype=jnp.float32), 'w2': jax.random.normal(ks[3], (E, F, H), dtype=jnp.float32) * sc, 'b2': jnp.zeros((E, H), dtype=jnp.float32), 'gamma': jnp.ones((H,), dtype=jnp.float32), 'beta': jnp.zeros((H,), dtype=jnp.float32)}
    _L0_ffn_all = _L0_ffn_setup()
    _L0_ffn_in = {k: v for k, v in _L0_ffn_all.items() if k in ('gate_w', 'gate_b', 'w1', 'b1', 'w2', 'b2', 'gamma', 'beta')}
    del _L0_ffn_all
    return {'x': x, 'src': src, 'dst': dst, 'edge_weight': edge_weight, 'L0_gnn_W': _L0_gnn_in['W'], 'L0_gnn_bias': _L0_gnn_in['bias'], 'L0_ffn_gate_w': _L0_ffn_in['gate_w'], 'L0_ffn_gate_b': _L0_ffn_in['gate_b'], 'L0_ffn_w1': _L0_ffn_in['w1'], 'L0_ffn_b1': _L0_ffn_in['b1'], 'L0_ffn_w2': _L0_ffn_in['w2'], 'L0_ffn_b2': _L0_ffn_in['b2'], 'L0_ffn_gamma': _L0_ffn_in['gamma'], 'L0_ffn_beta': _L0_ffn_in['beta']}

def reference(x, src, dst, edge_weight, L0_gnn_W, L0_gnn_bias, L0_ffn_gate_w, L0_ffn_gate_b, L0_ffn_w1, L0_ffn_b1, L0_ffn_w2, L0_ffn_b2, L0_ffn_gamma, L0_ffn_beta):
    import jax
    import jax.numpy as jnp

    def _L0_gnn_ref(x, edge_src, edge_dst, edge_val, W, bias):
        import jax, jax.numpy as jnp
        import numpy as np
        N_NODES = 6250
        N_EDGES = 200000
        D_IN = 256
        D_OUT = 256
        K_HOPS = 2

        def spmm(edge_src, edge_dst, edge_val, h):
            msgs = edge_val[:, None] * h[edge_src]
            return jax.ops.segment_sum(msgs, edge_dst, num_segments=N_NODES)
        h = x
        output = jnp.zeros((N_NODES, D_OUT), dtype=x.dtype)
        for k in range(K_HOPS):
            h = spmm(edge_src, edge_dst, edge_val, h)
            output = output + h @ W[k]
        return output + bias

    def _L0_ffn_ref(x, gate_w, gate_b, w1, b1, w2, b2, gamma, beta):
        import jax, jax.numpy as jnp
        import numpy as np
        B, S, H, F, E, K = (8, 512, 256, 512, 16, 2)
        EPS = 1e-05
        gate_logits = x @ gate_w + gate_b
        topk_vals, topk_idx = jax.lax.top_k(gate_logits, K)
        topk_w = jax.nn.softmax(topk_vals, axis=-1)
        h = jax.nn.relu(jnp.einsum('bsh,ehf->bsef', x, w1) + b1)
        expert_out = jnp.einsum('bsef,efh->bseh', h, w2) + b2
        sel = jnp.take_along_axis(expert_out, topk_idx[:, :, :, None], axis=2)
        moe = jnp.sum(topk_w[..., None] * sel, axis=2)
        y = x + moe
        mu = jnp.mean(y, axis=-1, keepdims=True)
        var = jnp.var(y, axis=-1, keepdims=True)
        return (y - mu) / jnp.sqrt(var + EPS) * gamma + beta
    x = x + _L0_gnn_ref(_layernorm(x, axis=-1), src, dst, edge_weight, L0_gnn_W, L0_gnn_bias)
    x = x + _L0_ffn_ref(_layernorm(x, axis=-1)[None], L0_ffn_gate_w, L0_ffn_gate_b, L0_ffn_w1, L0_ffn_b1, L0_ffn_w2, L0_ffn_b2, L0_ffn_gamma, L0_ffn_beta)[0]
    return x

_drawn_inputs = setup_inputs


def setup_inputs(seed=0):
    import zlib

    import numpy as np

    out = dict(_drawn_inputs(seed))
    spreads = {'L0_ffn_gate_b': (0.0, 0.8),
     'L0_ffn_b1': (0.0, 0.8),
     'L0_ffn_b2': (0.0, 2.0),
     'L0_ffn_gamma': (1.0, 0.6),
     'L0_ffn_beta': (0.0, 0.781)}
    factors = {'L0_gnn_bias': 8.0, 'L0_ffn_gate_w': 5.653, 'L0_ffn_w1': 8.0, 'L0_ffn_w2': 7.037}
    for name, (base, spread) in spreads.items():
        noise = np.random.default_rng([zlib.crc32(name.encode()), seed]).standard_normal(out[name].shape)
        drawn = base * np.exp(spread * noise) if base else spread * noise
        out[name] = jnp.asarray(drawn.astype(out[name].dtype))
    for name, factor in factors.items():
        out[name] = (out[name] * factor).astype(out[name].dtype)
    return out
```

```python
from contextlib import ExitStack

import concourse.bass as bass
from concourse import mybir

ALU = mybir.AluOpType
ACT = mybir.ActivationFunctionType
AX_X = mybir.AxisListType.X
F32 = mybir.dt.float32
I32 = mybir.dt.int32
U32 = mybir.dt.uint32

P = 128
N = 6250
D = 256
DH = D // P
NE = 206250
EPS = 1e-5

CT = 26
CH = 62
CE = CT * P
NEP = CH * CE
SR = CT // 2
NR = N + P + 22
assert NEP >= NE and CH % 2 == 0

LR = 6
LG = 8
LMAIN = P * LR * LG
LTAIL = N - LMAIN
assert 0 < LTAIL <= P

TR = 104
TT = -(-N // TR)
TLAST = N - (TT - 1) * TR
LAG = 4
assert TT % 4 == 1 and CH - LAG == TT - 3

X = 16
F = 512
FH = F // P
CAP = NR
STEPS = (2 * N + X * (P - 1)) // P
SPARE = STEPS - (-(-2 * N // P))
NSLOT = X * CAP + SPARE * P
assert STEPS <= P and STEPS % 4 == 1

ROUND = 8388608.0
FAR = 1000.0
OUT = 65536.0
ETILES = NEP // P


def wait(eng, sem, value):
    if isinstance(value, int) and value <= 0:
        return
    eng.wait_ge(sem, value)


def wait_apart(eng, always, sem, value):
    if not isinstance(value, int):
        value = eng.to_reg(value)
    eng.wait_ge(always, 1)
    wait(eng, sem, value)


def steps_of_four(eng, count, step):
    for r in range(4):
        step(r, r, 0)
    whole = (count - 3) // 4
    with eng.Fori(1, whole) as g:
        for r in range(4):
            step(4 * g + r, r, g)
    for s in range(4 * whole, count):
        step(s, s % 4, s // 4)


def pairs_of_tiles(eng, pair):
    pair(0, 0, 0, 2, TR)
    pair(1, 0, 1, 2, TR)
    with eng.Fori(1, TT // 4 - 1) as g:
        pair(2 * g, g, 0, 2, TR)
        pair(2 * g + 1, g, 1, 2, TR)
    pair(TT // 2 - 2, TT // 4 - 1, 0, 2, TR)
    pair(TT // 2 - 1, TT // 4 - 1, 1, 2, TR)
    pair(TT // 2, TT // 4, 0, 1, TLAST)


def build(nc, x, src, dst, edge_weight, gnn_w, gnn_bias, gate_w, gate_b, w1, b1, w2, b2, gamma, beta, out):
    ctx = ExitStack()
    with ctx:
        def sb(name, shape, dt=F32):
            return ctx.enter_context(nc.sbuf_tensor(name, shape, dt))

        def bank(name):
            return ctx.enter_context(nc.psum_tensor(name, [P, 512], F32))

        def sem(name):
            return ctx.enter_context(nc.semaphore(name))

        def sems(name, n):
            return [sem(f"{name}{i}") for i in range(n)]

        def dram(name, shape, dt=F32):
            return nc.dram_tensor(name, shape, dt).ap()

        xn_rows = dram("xn_rows", (N, D))
        h_rows = [dram("h1_rows", (NR, D)), dram("h2_rows", (NR, D))]
        t_rows = dram("t_rows", (N, D))
        res_rows = dram("res_rows", (N, D))
        src_pad = dram("src_pad", (NEP,), I32)
        dst_pad = dram("dst_pad", (NEP + NEP // P,), I32)
        w_pad = dram("w_pad", (NEP,))
        slot_in = dram("slot_in", (NSLOT, D))
        slot_out = dram("slot_out", (STEPS * P, D))
        bias_tab = dram("bias_tab", (X, F + D))
        step_tab = dram("step_tab", (P, 2), I32)

        w1_sb = sb("w1_sb", [P, X * DH, F])
        w2_sb = sb("w2_sb", [P, X * FH, D])
        scratch1 = w1_sb[:, 0:13, :].rearrange("p a b -> p (a b)")
        ln_in = [scratch1[:, b * LR * D:(b + 1) * LR * D].rearrange("p (r d) -> p r d", d=D) for b in range(2)]
        ln_out = [scratch1[:, (2 + b) * LR * D:(3 + b) * LR * D].rearrange("p (r d) -> p r d", d=D) for b in range(2)]
        tail_in = scratch1[:, 4 * LR * D:(4 * LR + 1) * D].unsqueeze(1)
        tail_out = scratch1[:, (4 * LR + 1) * D:(4 * LR + 2) * D].unsqueeze(1)
        PK = NEP // P
        scratch2 = w2_sb[:, 0:16, :].rearrange("p a b -> p (a b)")
        dst_all = scratch2[:, 0:PK + 1].bitcast(I32)
        unsorted = scratch2[:, PK + 1:2 * PK + 1]
        pad_i = sb("pad_i", [1, 3 * P], I32)

        rows = sb("rows", [P, CT, D])
        sel = sb("sel", [P, SR, P])
        kept = sb("kept", [P, 2, D])
        shift = sb("shift", [P, 2, P])
        src_t = [sb(f"src_t{b}", [P, CT], I32) for b in range(2)]
        dst_t = [sb(f"dst_t{b}", [P, CT], I32) for b in range(2)]
        w_t = [sb(f"w_t{b}", [P, CT]) for b in range(2)]
        dst_rel = [sb(f"dst_rel{b}", [P, CT]) for b in range(2)]

        col_id = sb("col_id", [P, P])
        diff_id = sb("diff_id", [P, P])
        ident = sb("ident", [P, P])
        below = sb("below", [P, P])
        ones = sb("ones", [P, P])
        zeros = sb("zeros", [P, D])
        tri_eye = sb("tri_eye", [X, 2 * X])
        row_id = sb("row_id", [P, 1])
        base_row = sb("base_row", [1, 64], I32)
        base_rowf = sb("base_rowf", [1, 64])
        base = sb("base", [P, 64])
        delta = sb("delta", [P, 64])
        need = sb("need", [P, 64])
        bad = sb("bad", [P, 3])
        bad_sum = sb("bad_sum", [P, 1])
        slow_i = sb("slow_i", [P, 1], I32)

        gnn_w_sb = sb("gnn_w_sb", [P, 2 * DH, D])
        bias_sb = sb("bias_sb", [P, D])
        gamma_sb = sb("gamma_sb", [P, D])
        beta_sb = sb("beta_sb", [P, D])
        gate_w_sb = sb("gate_w_sb", [P, DH, X])
        gate_b_sb = sb("gate_b_sb", [P, X])
        slot_base = sb("slot_base", [P, X])

        ln_stats = sb("ln_stats", [P, LR, 6])
        ln_mv = [sb(f"ln_mv{b}", [P, LR, 2]) for b in range(2)]
        ln_small = [sb(f"ln_small{b}", [P, 6, LR]) for b in range(2)]

        x_t = sb("x_t", [P, 2, D])
        h_t = sb("h_t", [P, 2, 2 * D])
        hT_t = sb("hT_t", [P, 2 * DH, TR])
        mid_t = sb("mid_t", [P, D])
        res_t = sb("res_t", [P, 2, D])
        t_t = sb("t_t", [P, 2, D])
        tT_t = sb("tT_t", [P, DH, TR])
        tok_stats = sb("tok_stats", [P, 2, 6])
        tok_mv = sb("tok_mv", [P, 2, 2])
        tok_small = sb("tok_small", [P, 6, 2])
        logits = sb("logits", [P, X])
        top_v = sb("top_v", [P, 8])
        top_i = sb("top_i", [P, 8], U32)
        top_f = sb("top_f", [P, 2])
        gap = sb("gap", [P, 1])
        gap_e = sb("gap_e", [P, 1])
        gap_d = sb("gap_d", [P, 1])
        gap_r = sb("gap_r", [P, 1])
        chosen = sb("chosen", [P, 2, X])
        both = sb("both", [P, X])
        routed = sb("routed", [P, X])
        place = sb("place", [P, X])
        placed = sb("placed", [P, 2, X])
        pos_f = sb("pos_f", [P, 2])
        pos_t = [sb(f"pos_t{b}", [P, 2], I32) for b in range(2)]
        pos_s = [sb(f"pos_s{b}", [P, 2], I32) for b in range(4)]
        pos_all = sb("pos_all", [P, 2 * TT])
        exp_all = sb("exp_all", [P, 2 * TT])
        pos_fix = sb("pos_fix", [P, 2 * TT])
        slot_fix = sb("slot_fix", [P, X])
        wts_all = sb("wts_all", [P, 2 * TT])

        tiles_T = sb("tiles_T", [X, P])
        tiles_C = sb("tiles_C", [P, 2 * X])
        step_cmp = sb("step_cmp", [P, X])
        step_cum = sb("step_cum", [P, X])
        step_f = sb("step_f", [P, 4])
        step_i = sb("step_i", [P, 2], I32)
        step_row = sb("step_row", [1, 2 * P], I32)
        zero_f = sb("zero_f", [P, X])
        zero_at = sb("zero_at", [P, X], I32)

        room = rows[:, :, :].rearrange("p a b -> p (a b)")
        room2 = sel[:, :, :].rearrange("p a b -> p (a b)")
        taken = [0, 0]

        def part(n):
            taken[0] += n
            return room[:, taken[0] - n:taken[0]]

        def part2(n):
            taken[1] += n
            return room2[:, taken[1] - n:taken[1]]

        xs = [part(D) for _ in range(4)]
        bias_t = [part(F + D) for _ in range(4)]
        hb = [part(F) for _ in range(2)]
        xsT = [part2(D).rearrange("p (k t) -> p k t", t=P) for _ in range(2)]
        ys = [part2(D) for _ in range(2)]
        hT = [part(F).rearrange("p (k t) -> p k t", t=P) for _ in range(2)]
        taken[0] = 0
        y_a = [part(D) for _ in range(4)]
        y_b = [part(D) for _ in range(4)]
        f_t = [part(D) for _ in range(4)]
        f_res = [part(D) for _ in range(4)]
        f_mix = [part(D) for _ in range(2)]
        f_sum = [part(D) for _ in range(2)]
        f_scaled = [part(D) for _ in range(2)]
        f_out = [part(D) for _ in range(2)]

        s_src = sb("s_src", [P, 1], I32)
        s_dst = sb("s_dst", [P, 1], I32)
        s_w = sb("s_w", [P, 1])
        s_dstf = sb("s_dstf", [P, 1])
        s_rep = sb("s_rep", [P, 1])
        s_repf = sb("s_repf", [P, 1])
        s_put = sb("s_put", [P, 1], I32)
        s_dst_row = sel[:, 0, :].bitcast(I32)
        s_dst_rowf = sel[:, 1, :]
        s_same_w = sel[:, 2, :]
        s_same_below = sel[:, 3, :]
        s_rows, s_old, s_new = rows[:, 0, :], rows[:, 1, :], rows[:, 2, :]

        win = [bank("win0"), bank("win1")]
        turn = bank("turn")
        turn2 = bank("turn2")
        proj = [bank("proj0"), bank("proj1")]
        small = bank("small")
        small2 = bank("small2")

        iotas = sem("iotas")
        fills = sem("fills")
        consts_ready = sem("consts_ready")
        params_in = sem("params_in")
        edges_copied = sem("edges_copied")
        pad_in = sem("pad_in")
        dst_in = sem("dst_in")
        base_in = sem("base_in")
        base_ready = sem("base_ready")
        base_spread = sem("base_spread")
        base_kept = sem("base_kept")
        bad_ready = sem("bad_ready")
        bad_summed = sem("bad_summed")
        slow_known = sem("slow_known")
        ln_loaded = sems("ln_loaded", 2)
        tail_loaded = sem("tail_loaded")
        ln_var = sem("ln_var")
        ln_sd = sem("ln_sd")
        ln_scaled = sem("ln_scaled")
        ln_applied = sem("ln_applied")
        ln_stored = sems("ln_stored", 2)
        tail_stored = sem("tail_stored")
        weights_in = sem("weights_in")

        edges_in = sems("edges_in", 2)
        rel_ready = sem("rel_ready")
        sel_built = sem("sel_built")
        shift_built = sem("shift_built")
        rows_in = sems("rows_in", CT)
        tile_summed = sem("tile_summed")
        window_summed = sem("window_summed")
        window_kept = sem("window_kept")
        window_out = sem("window_out")

        slow_zeroed = sem("slow_zeroed")
        slow_loaded = [sems(f"slow_loaded{h}_", 4) for h in range(2)]
        slow_sel = sem("slow_sel")
        slow_rows = [sems(f"slow_rows{h}_", 2) for h in range(2)]
        slow_summed = sem("slow_summed")
        slow_new = sem("slow_new")
        slow_stored = sems("slow_stored", 2)

        tok_in = sems("tok_in", 2)
        tok_turned = sem("tok_turned")
        tok_turned_kept = sem("tok_turned_kept")
        tok_projected = sem("tok_projected")
        tok_res = sem("tok_res")
        tok_var = sem("tok_var")
        tok_sd = sem("tok_sd")
        tok_t = sem("tok_t")
        tok_out = sems("tok_out", 2)
        t_turned = sem("t_turned")
        t_turned_kept = sem("t_turned_kept")
        tok_gated = sem("tok_gated")
        tok_chosen = sem("tok_chosen")
        tok_exp = sem("tok_exp")
        tok_ranked = sem("tok_ranked")
        tok_placed = sem("tok_placed")
        tok_scattered = sems("tok_scattered", 2)

        counted = sem("counted")
        tiles_ready = sem("tiles_ready")
        cumulated = sem("cumulated")
        steps_ready = sem("steps_ready")
        steps_out = sem("steps_out")
        steps_in = sem("steps_in")
        zeros_out = sem("zeros_out")
        spare_out = sem("spare_out")
        biases_out = sem("biases_out")
        xs_in = sems("xs_in", 4)
        bias_in = sems("bias_in", 4)
        xs_turned = sem("xs_turned")
        xs_kept = sem("xs_kept")
        up_done = sem("up_done")
        up_kept = sem("up_kept")
        h_turned = sem("h_turned")
        h_kept = sem("h_kept")
        down_done = sem("down_done")
        y_kept = sem("y_kept")
        y_out = sems("y_out", 2)

        pos_staged = sem("pos_staged")
        y_in = sems("y_in", 4)
        fin_t_in = sems("fin_t_in", 4)
        fin_res_in = sems("fin_res_in", 4)
        fin_var = sem("fin_var")
        fin_sd = sem("fin_sd")
        fin_ready = sem("fin_ready")
        out_stored = sems("out_stored", 2)

        block = ctx.enter_context(nc.Block())

        x_main = x[0:LMAIN, :].rearrange("(p r) d -> p r d", p=P)
        xn_main = xn_rows[0:LMAIN, :].rearrange("(p r) d -> p r d", p=P)
        hop_in = [xn_rows, h_rows[0][0:N, :]]
        gate_w_v = gate_w.rearrange("(k p) e -> p k e", p=P)
        gnn_w_v = gnn_w.rearrange("h (k p) d -> p (h k) d", p=P)

        def chunk_view(a, c):
            return a[bass.ds(c * CE, CE)].rearrange("(p j) -> p j", p=P)

        def as_row(a):
            return a.rearrange("(a n) -> a n", a=1)

        def tile_rows(i, r):
            return bass.ds(i * TR, r)

        @block.sync
        def _(sp):
            def load_ln(g, b, m):
                wait(sp, ln_applied, g - 1)
                sp.dma_start(ln_in[b], x_main[:, bass.ds(g * LR, LR), :]).then_inc(ln_loaded[b], 16)

            load_ln(0, 0, 0)
            load_ln(1, 1, 0)
            sp.dma_start(tail_in[0:LTAIL, 0, :], x[LMAIN:N, :]).then_inc(tail_loaded, 16)

            sp.dma_start(as_row(dst_pad[0:NE]), as_row(dst)).then_inc(edges_copied, 16)
            sp.dma_start(as_row(src_pad[0:NE]), as_row(src)).then_inc(edges_copied, 16)
            sp.dma_start(as_row(w_pad[0:NE]), as_row(edge_weight)).then_inc(edges_copied, 16)
            npad = NEP - NE
            sp.wait_ge(fills, 3)
            sp.dma_start(as_row(src_pad[NE:NEP]), pad_i[:, 0:npad]).then_inc(edges_copied, 16)
            sp.dma_start(as_row(w_pad[NE:NEP]), pad_i[:, 0:npad].bitcast(F32)).then_inc(edges_copied, 16)
            sp.dma_start(as_row(dst_pad[NE:NEP + P]), pad_i[:, P:P + npad + P]).then_inc(edges_copied, 16)
            with sp.Fori(1, LG // 2) as m:
                load_ln(2 * m, 0, m)
                load_ln(2 * m + 1, 1, m)
            sp.dma_start(bias_tab[:, 0:F], b1).then_inc(biases_out, 16)
            sp.dma_start(bias_tab[:, F:F + D], b2).then_inc(biases_out, 16)
            sp.wait_ge(edges_copied, 96)
            sp.dma_start(dst_all[:, 0:PK], dst_pad[0:NEP].rearrange("(p k) -> p k", p=P)).then_inc(dst_in, 16)
            firsts = dst_pad[CE:NEP].rearrange("(c e) -> c e", e=CE)[:, 0:1].rearrange("c e -> e c")
            with nc.allow_non_contiguous_dma("one element per partition, and per chunk"):
                sp.dma_start(dst_all[:, PK:PK + 1], dst_pad[PK:PK + NEP].rearrange("(p k) -> p k", p=P)[:, 0:1]).then_inc(dst_in, 16)
                sp.dma_start(base_row[:, 1:CH], firsts).then_inc(base_in, 16)

            def load_tokens(i, b, m, r):
                wait(sp, tok_res, i - 1)
                sp.dma_start(x_t[0:r, b, :], x[tile_rows(i, r), :]).then_inc(tok_in[b], 16)
                sp.dma_start(h_t[0:r, b, 0:D], h_rows[0][tile_rows(i, r), :]).then_inc(tok_in[b], 16)
                sp.dma_start(h_t[0:r, b, D:2 * D], h_rows[1][tile_rows(i, r), :]).then_inc(tok_in[b], 16)

            def load_edges(hop, c, b):
                wait(sp, tile_summed, CT * (c + CH * hop - 1))
                sp.dma_start(src_t[b][:], chunk_view(src_pad, c)).then_inc(edges_in[b], 16)
                sp.dma_start(dst_t[b][:], chunk_view(dst_pad, c)).then_inc(edges_in[b], 16)
                sp.dma_start(w_t[b][:], chunk_view(w_pad, c)).then_inc(edges_in[b], 16)

            def load_both(c, b, i, m):
                load_edges(1, c, b)
                wait_apart(sp, consts_ready, window_out, 16 * (CH + c))
                load_tokens(i, b, m, TR)

            sp.wait_ge(slow_known, 1)
            slow = sp.value_load(slow_i[0:1, 0:1], min_val=0, max_val=1)
            with sp.If(slow):
                for hop in range(2):
                    with sp.Fori(0, ETILES) as k:
                        e0 = k * P
                        sp.dma_start(s_src[:], src_pad[bass.ds(e0, P)].rearrange("(p a) -> p a", a=1)).then_inc(slow_loaded[hop][0], 16)
                        sp.dma_start(s_dst[:], dst_pad[bass.ds(e0, P)].rearrange("(p a) -> p a", a=1)).then_inc(slow_loaded[hop][1], 16)
                        sp.dma_start(s_w[:], w_pad[bass.ds(e0, P)].rearrange("(p a) -> p a", a=1)).then_inc(slow_loaded[hop][2], 16)
                        sp.dma_start(s_dst_row, as_row(dst_pad[bass.ds(e0, P)]).partition_broadcast(P)).then_inc(slow_loaded[hop][3], 16)
                        wait_apart(sp, consts_ready, slow_stored[hop], 16 * k + 16)
                load_tokens(0, 0, 0, TR)
                load_tokens(1, 1, 0, TR)
                with sp.Fori(1, TT // 2) as m:
                    load_tokens(2 * m, 0, m, TR)
                    load_tokens(2 * m + 1, 1, m, TR)
            with sp.Else():
                load_edges(0, 0, 0)
                load_edges(0, 1, 1)
                with sp.Fori(1, CH // 2) as q:
                    load_edges(0, 2 * q, 0)
                    load_edges(0, 2 * q + 1, 1)
                with sp.Fori(0, LAG // 2) as q:
                    load_edges(1, 2 * q, 0)
                    load_edges(1, 2 * q + 1, 1)
                load_both(LAG, 0, 0, 0)
                load_both(LAG + 1, 1, 1, 0)
                with sp.Fori(LAG // 2 + 1, CH // 2) as q:
                    load_both(2 * q, 0, 2 * q - LAG, q - LAG // 2)
                    load_both(2 * q + 1, 1, 2 * q + 1 - LAG, q - LAG // 2)
                sp.wait_ge(window_out, 16 * 2 * CH)
                load_tokens(TT - 3, 0, TT // 2 - 1, TR)
                load_tokens(TT - 2, 1, TT // 2 - 1, TR)
            load_tokens(TT - 1, 0, TT // 2, TLAST)

            sp.dma_start(slot_in[X * CAP:NSLOT, :].rearrange("(a p) d -> p a d", p=P),
                         zeros[:, :].unsqueeze(1).to_broadcast([P, SPARE, D])).then_inc(spare_out, 16)
            sp.wait_ge(steps_ready, 1)
            sp.dma_start(step_tab, step_i[:, :]).then_inc(steps_out, 16)
            sp.wait_ge(steps_out, 16)
            sp.dma_start(step_row[:, :], as_row(step_tab.rearrange("p a -> (p a)"))).then_inc(steps_in, 16)
            with sp.Fori(0, X) as e:
                at = sp.value_load(zero_at[0:1, bass.ds(e, 1)], min_val=0, max_val=NSLOT - P)
                sp.dma_start(slot_in[bass.ds(at, P), :], zeros[:, :]).then_inc(zeros_out, 16)
            sp.wait_ge(zeros_out, 16 * X)
            sp.wait_ge(spare_out, 16)
            for b in range(2):
                sp.wait_ge(tok_scattered[b], 32 * (TT // 2 + 1 - b))
            sp.wait_ge(steps_in, 16)

            sp.wait_ge(biases_out, 32)

            def load_slots(s, r, g):
                at = sp.value_load(step_row[0:1, bass.ds(2 * s, 1)], min_val=0, max_val=NSLOT - P)
                e = sp.value_load(step_row[0:1, bass.ds(2 * s + 1, 1)], min_val=0, max_val=X - 1)
                wait(sp, xs_turned, s - 3)
                sp.dma_start(xs[r], slot_in[bass.ds(at, P), :]).then_inc(xs_in[r], 16)
                wait(sp, y_kept, s - 3)
                sp.dma_start(bias_t[r], bias_tab[bass.ds(e, 1), :].partition_broadcast(P)).then_inc(bias_in[r], 16)

            steps_of_four(sp, STEPS, load_slots)

            for b in range(2):
                sp.wait_ge(y_out[b], 16 * (STEPS // 2 + 1 - b))
                sp.wait_ge(tok_out[b], 32 * (TT // 2 + 1 - b))

            def load_final(m, g, h, n, r):
                for b in range(n):
                    i, u = 2 * m + b, 2 * h + b
                    wait(sp, fin_var, m - 1)
                    sp.dma_start(f_t[u][0:r, :], t_rows[tile_rows(i, r), :]).then_inc(fin_t_in[u], 16)
                    wait(sp, fin_ready, 2 * (m - 1))
                    sp.dma_start(f_res[u][0:r, :], res_rows[tile_rows(i, r), :]).then_inc(fin_res_in[u], 16)

            pairs_of_tiles(sp, load_final)
            for b in range(2):
                sp.wait_ge(out_stored[b], 16 * (TT // 2 + 1 - b))

        @block.gpsimd
        def _(pool):
            exact = True
            pool.iota(col_id[:], [[1, P]], base=0, channel_multiplier=0, allow_small_or_imprecise_dtypes=exact).then_inc(iotas, 1)
            pool.iota(diff_id[:], [[-1, P]], base=0, channel_multiplier=1, allow_small_or_imprecise_dtypes=exact).then_inc(iotas, 1)
            pool.iota(row_id[:], [[0, 1]], base=0, channel_multiplier=1, allow_small_or_imprecise_dtypes=exact).then_inc(iotas, 1)
            pool.iota(need[:], [[TR, 64]], base=-TR * (LAG - 1), channel_multiplier=0, allow_small_or_imprecise_dtypes=exact).then_inc(iotas, 1)
            pool.iota(slot_base[:], [[CAP, X]], base=0, channel_multiplier=0, allow_small_or_imprecise_dtypes=exact).then_inc(iotas, 1)

            def scatter(i, b, m, r):
                wait_apart(pool, consts_ready, tok_placed, i + 1)
                for k in range(2):
                    pool.indirect_dma_start(slot_in[:, :], bass.IndirectOffsetOnAxis(ap=pos_t[b][0:r, k:k + 1], axis=0),
                                            t_t[0:r, b, :], None).then_inc(tok_scattered[b], 16)

            def gather_chunk(hop, c, b, q, scatters=None):
                wait_apart(pool, consts_ready, edges_in[b], 48 * (q + CH // 2 * hop) + 48)
                for j in range(CT):
                    if j % SR == 0:
                        wait_apart(pool, consts_ready, tile_summed, CT * (c + CH * hop) + j - SR)
                    pool.indirect_dma_start(rows[:, j, :], None, hop_in[hop][:, :],
                                            bass.IndirectOffsetOnAxis(ap=src_t[b][:, j:j + 1], axis=0)).then_inc(rows_in[j], 16)
                    if j == SR - 1 and scatters:
                        scatters()

            pool.wait_ge(slow_known, 1)
            for b in range(2):
                pool.wait_ge(ln_stored[b], 16 * (LG // 2))
            pool.wait_ge(tail_stored, 16)
            slow = pool.value_load(slow_i[0:1, 0:1], min_val=0, max_val=1)
            with pool.If(slow):
                pool.wait_ge(slow_zeroed, 16 * 2 * (NR // P))
                for hop in range(2):
                    with pool.Fori(0, ETILES) as k:
                        wait_apart(pool, consts_ready, slow_loaded[hop][0], 16 * k + 16)
                        pool.indirect_dma_start(s_rows, None, hop_in[hop][:, :],
                                                bass.IndirectOffsetOnAxis(ap=s_src[:, 0:1], axis=0)).then_inc(slow_rows[hop][0], 16)
                        wait_apart(pool, consts_ready, slow_loaded[hop][1], 16 * k + 16)
                        pool.indirect_dma_start(s_old, None, h_rows[hop][0:N, :],
                                                bass.IndirectOffsetOnAxis(ap=s_dst[:, 0:1], axis=0)).then_inc(slow_rows[hop][1], 16)
                        wait_apart(pool, consts_ready, slow_new, k + 1 + ETILES * hop)
                        pool.indirect_dma_start(h_rows[hop][0:N, :], bass.IndirectOffsetOnAxis(ap=s_put[:, 0:1], axis=0),
                                                s_new, None, bounds_check=N - 1, oob_is_err=False).then_inc(slow_stored[hop], 16)
                        wait_apart(pool, consts_ready, slow_stored[hop], 16 * k + 16)
                        pool.engine_nop()
                scatter(0, 0, 0, TR)
                scatter(1, 1, 0, TR)
                with pool.Fori(1, TT // 2) as m:
                    scatter(2 * m, 0, m, TR)
                    scatter(2 * m + 1, 1, m, TR)
            with pool.Else():
                gather_chunk(0, 0, 0, 0)
                gather_chunk(0, 1, 1, 0)
                with pool.Fori(1, CH // 2) as q:
                    gather_chunk(0, 2 * q, 0, q)
                    gather_chunk(0, 2 * q + 1, 1, q)
                pool.wait_ge(window_out, 16 * CH)
                with pool.Fori(0, LAG // 2) as q:
                    gather_chunk(1, 2 * q, 0, q)
                    gather_chunk(1, 2 * q + 1, 1, q)
                q0 = LAG // 2
                gather_chunk(1, LAG, 0, q0)
                gather_chunk(1, LAG + 1, 1, q0, lambda: scatter(0, 0, 0, TR))
                with pool.Fori(q0 + 1, CH // 2) as q:
                    gather_chunk(1, 2 * q, 0, q, lambda: scatter(2 * q - LAG - 1, 1, q - q0 - 1, TR))
                    gather_chunk(1, 2 * q + 1, 1, q, lambda: scatter(2 * q - LAG, 0, q - q0, TR))
                scatter(TT - 4, 1, TT // 2 - 2, TR)
                scatter(TT - 3, 0, TT // 2 - 1, TR)
                scatter(TT - 2, 1, TT // 2 - 1, TR)
            scatter(TT - 1, 0, TT // 2, TLAST)

            for b in range(2):
                pool.wait_ge(y_out[b], 16 * (STEPS // 2 + 1 - b))

            def gather_final(m, g, h, n, r):
                for b in range(n):
                    u = 2 * h + b
                    wait_apart(pool, consts_ready, fin_var, m - 1)
                    wait_apart(pool, consts_ready, pos_staged, 2 * m + b + 1)
                    for k, y in ((0, y_a), (1, y_b)):
                        pool.indirect_dma_start(y[u][0:r, :], None, slot_out[:, :],
                                                bass.IndirectOffsetOnAxis(ap=pos_s[u][0:r, k:k + 1], axis=0)).then_inc(y_in[u], 16)

            pairs_of_tiles(pool, gather_final)

        @block.scalar
        def _(act):
            for dest, view in ((gnn_w_sb[:], gnn_w_v), (gate_w_sb[:], gate_w_v),
                               (bias_sb[:], as_row(gnn_bias).partition_broadcast(P)),
                               (gamma_sb[:], as_row(gamma).partition_broadcast(P)),
                               (beta_sb[:], as_row(beta).partition_broadcast(P)),
                               (gate_b_sb[:], as_row(gate_b).partition_broadcast(P))):
                act.dma_start(dest, view).then_inc(params_in, 16)

            def ln_step(g, b, m, source, target, r, n):
                act.wait_ge(ln_var, g + 1)
                act.activation(ln_small[b][0:r, 1, 0:n], ln_small[b][0:r, 0, 0:n], ACT.Sqrt).then_inc(ln_sd, 1)
                wait(act, ln_stored[b], 16 * m)
                act.wait_ge(ln_scaled, g + 1)
                for k in range(n):
                    last = act.activation(target[0:r, k, :], source[0:r, k, :], ACT.Identity,
                                          scale=ln_small[b][0:r, 4, k:k + 1], bias=ln_small[b][0:r, 5, k:k + 1])
                last.then_inc(ln_applied, 1)
                act.wait_ge(ln_applied, g + 1)

            def ln_group(g, b, m):
                ln_step(g, b, m, ln_in[b], ln_out[b], P, LR)
                act.dma_start(xn_main[:, bass.ds(g * LR, LR), :], ln_out[b]).then_inc(ln_stored[b], 16)

            ln_group(0, 0, 0)
            ln_group(1, 1, 0)
            with act.Fori(1, LG // 2) as m:
                ln_group(2 * m, 0, m)
                ln_group(2 * m + 1, 1, m)
            ln_step(LG, 0, 0, tail_in, tail_out, LTAIL, 1)
            act.dma_start(xn_rows[LMAIN:N, :], tail_out[0:LTAIL, 0, :]).then_inc(tail_stored, 16)
            act.wait_ge(base_spread, 1)
            act.copy(base[:, :], small[:, 0:64]).then_inc(base_kept, 1)

            act.wait_ge(slow_known, 1)
            for b in range(2):
                act.wait_ge(ln_stored[b], 16 * (LG // 2))
            act.wait_ge(tail_stored, 16)

            def load_expert(e):
                act.dma_start(w1_sb[:, bass.ds(e * DH, DH), :], w1[bass.ds(e, 1)].rearrange("e (k p) f -> p (e k) f", p=P)).then_inc(weights_in, 16)
                act.dma_start(w2_sb[:, bass.ds(e * FH, FH), :], w2[bass.ds(e, 1)].rearrange("e (k p) d -> p (e k) d", p=P)).then_inc(weights_in, 16)

            def tok_keep_turned(i, b, m, r):
                act.wait_ge(tok_turned, i + 1)
                wait(act, tok_projected, i)
                act.copy(hT_t[:, :, 0:r], turn[:, :].rearrange("p (k t) -> p k t", t=P)[:, :, 0:r]).then_inc(tok_turned_kept, 1)

            def tok_root(i, b, m, r):
                act.wait_ge(tok_var, i + 1)
                act.activation(tok_small[0:r, 1, 0:1], tok_small[0:r, 0, 0:1], ACT.Sqrt).then_inc(tok_sd, 1)

            def tok_store(i, b, m, r):
                act.wait_ge(tok_t, i + 1)
                act.dma_start(res_rows[tile_rows(i, r), :], res_t[0:r, b, :]).then_inc(tok_out[b], 16)
                act.dma_start(t_rows[tile_rows(i, r), :], t_t[0:r, b, :]).then_inc(tok_out[b], 16)
                act.wait_ge(t_turned, i + 1)
                wait(act, tok_gated, i)
                act.copy(tT_t[:, :, 0:r], turn2[:, 0:DH * P].rearrange("p (k t) -> p k t", t=P)[:, :, 0:r]).then_inc(t_turned_kept, 1)

            def tok_weigh(i, b, m, r):
                act.wait_ge(tok_chosen, i + 1)
                act.activation(gap_e[0:r, :], gap[0:r, :], ACT.Exp).then_inc(tok_exp, 1)

            def tokens(i, b, m, r):
                for step in (tok_keep_turned, tok_root, tok_store, tok_weigh):
                    step(i, b, m, r)

            def keep_window(hop, c, b):
                n = c + CH * hop
                act.wait_ge(window_summed, n + 1)
                wait(act, window_out, 16 * (n - 1))
                act.copy(kept[:, b, :], win[b][:, 0:D]).then_inc(window_kept, 1)
                at = act.value_load(base_row[0:1, bass.ds(c, 1)], min_val=0, max_val=N - 1)
                wait(act, window_out, 16 * n)
                act.wait_ge(window_kept, n + 1)
                act.dma_start(h_rows[hop][bass.ds(at, P), :], kept[:, b, :]).then_inc(window_out, 16)

            slow = act.value_load(slow_i[0:1, 0:1], min_val=0, max_val=1)
            with act.If(slow):
                with act.Fori(0, X) as e:
                    load_expert(e)
                with act.Fori(0, NR // P) as k:
                    for table in h_rows:
                        act.dma_start(table[bass.ds(k * P, P), :], zeros[:, :]).then_inc(slow_zeroed, 16)
                tokens(0, 0, 0, TR)
                tokens(1, 1, 0, TR)
                with act.Fori(1, TT // 2) as m:
                    tokens(2 * m, 0, m, TR)
                    tokens(2 * m + 1, 1, m, TR)
            with act.Else():
                keep_window(0, 0, 0)
                keep_window(0, 1, 1)
                with act.Fori(1, X + 1) as q:
                    keep_window(0, 2 * q, 0)
                    keep_window(0, 2 * q + 1, 1)
                    load_expert(q - 1)
                with act.Fori(X + 1, CH // 2) as q:
                    keep_window(0, 2 * q, 0)
                    keep_window(0, 2 * q + 1, 1)
                with act.Fori(0, LAG // 2) as q:
                    keep_window(1, 2 * q, 0)
                    keep_window(1, 2 * q + 1, 1)
                tokens(0, 0, 0, TR)
                keep_window(1, LAG, 0)
                tokens(1, 1, 0, TR)
                keep_window(1, LAG + 1, 1)
                with act.Fori(LAG // 2 + 1, CH // 2) as q:
                    tokens(2 * q - LAG, 0, q - LAG // 2, TR)
                    keep_window(1, 2 * q, 0)
                    tokens(2 * q + 1 - LAG, 1, q - LAG // 2, TR)
                    keep_window(1, 2 * q + 1, 1)
                tokens(TT - 3, 0, TT // 2 - 1, TR)
                tokens(TT - 2, 1, TT // 2 - 1, TR)
            tokens(TT - 1, 0, TT // 2, TLAST)

            def keep_xs(s, b):
                act.wait_ge(xs_turned, s + 1)
                wait(act, up_done, s - 1)
                act.copy(xsT[b], turn2[:, 0:DH * P].rearrange("p (k t) -> p k t", t=P)).then_inc(xs_kept, 1)

            def keep_h(s, b):
                act.wait_ge(h_turned, s + 1)
                wait(act, down_done, s - 1)
                act.activation(hT[b], turn[:, :].rearrange("p (k t) -> p k t", t=P), ACT.Relu).then_inc(h_kept, 1)

            def store_y(s, b):
                act.wait_ge(y_kept, s + 1)
                act.dma_start(slot_out[bass.ds(s * P, P), :], ys[b]).then_inc(y_out[b], 16)

            def expert_step(s, r, g):
                b = r % 2
                keep_h(s, b)
                if not (isinstance(s, int) and s >= STEPS - 2):
                    keep_xs(s + 2, b)
                store_y(s, b)

            keep_xs(0, 0)
            keep_xs(1, 1)
            steps_of_four(act, STEPS, expert_step)

            def final_pair(m, g, h, n, r):
                act.wait_ge(fin_var, m + 1)
                act.activation(tok_small[0:r, 1, 0:n], tok_small[0:r, 0, 0:n], ACT.Sqrt).then_inc(fin_sd, 1)
                for b in range(n):
                    act.wait_ge(fin_ready, 2 * m + b + 1)
                    act.dma_start(out[tile_rows(2 * m + b, r), :], f_out[b][0:r, :]).then_inc(out_stored[b], 16)

            pairs_of_tiles(act, final_pair)

        @block.vector
        def _(dve):
            dve.memset(pad_i[:, 0:P], 0).then_inc(fills, 1)
            dve.memset(pad_i[:, P:3 * P], N - 1).then_inc(fills, 1)
            dve.memset(base_row[:, 0:1], 0).then_inc(fills, 1)
            dve.memset(ones[:], 1.0)
            dve.memset(zeros[:], 0.0)
            dve.memset(kept[:], 0.0)
            dve.memset(routed[:], 0.0)
            dve.memset(pos_all[:], 0.0)
            dve.memset(exp_all[:], 0.0)
            dve.memset(base_rowf[:, CH:64], N - 1.0)
            dve.wait_ge(iotas, 5)
            dve.tensor_scalar(ident[:], diff_id[:], 0.0, None, ALU.is_equal)
            dve.tensor_scalar(tri_eye[:, X:2 * X], diff_id[0:X, 0:X], 0.0, None, ALU.is_equal)
            dve.tensor_scalar(tri_eye[:, 0:X], diff_id[0:X, 0:X], 0.0, None, ALU.is_le)
            dve.tensor_scalar(below[:], diff_id[:], 0.0, None, ALU.is_lt)
            dve.drain()
            dve.memset(gap_d[:], 0.0).then_inc(consts_ready, 1)

            def scale_of(small_, mv, r, c0, c1):
                v, sd, a, t, s, z = (small_[0:r, k, c0:c1] for k in range(6))
                dve.reciprocal(a, sd)
                dve.drain()
                dve.tensor_tensor(t, a, a, ALU.mult)
                dve.drain()
                dve.tensor_tensor(t, t, v, ALU.mult)
                dve.drain()
                dve.tensor_scalar(t, t, -0.5, 1.5, ALU.mult, ALU.add)
                dve.drain()
                dve.tensor_tensor(s, a, t, ALU.mult)
                dve.drain()
                return dve.scalar_tensor_tensor(out=z, in0=mv[0:r, c0:c1, 0], scalar=-1.0, in1=s, op0=ALU.mult, op1=ALU.mult)

            def ln_step(g, b, source, r, n):
                wait(dve, ln_applied, g - 1)
                for k in range(n):
                    dve.bn_stats(ln_stats[0:r, k, :], source[0:r, k, :])
                dve.drain()
                for k in range(n):
                    dve.bn_aggr(ln_mv[b][0:r, k, :], ln_stats[0:r, k, :])
                dve.drain()
                dve.tensor_scalar(ln_small[b][0:r, 0, 0:n], ln_mv[b][0:r, 0:n, 1], EPS, None, ALU.add).then_inc(ln_var, 1)
                dve.wait_ge(ln_sd, g + 1)
                scale_of(ln_small[b], ln_mv[b], r, 0, n).then_inc(ln_scaled, 1)

            dve.wait_ge(ln_loaded[0], 16)
            ln_step(0, 0, ln_in[0], P, LR)
            dve.wait_ge(ln_loaded[1], 16)
            ln_step(1, 1, ln_in[1], P, LR)
            with dve.Fori(1, LG // 2) as m:
                for b in range(2):
                    dve.wait_ge(ln_loaded[b], 16 * m + 16)
                    ln_step(2 * m + b, b, ln_in[b], P, LR)
            dve.wait_ge(tail_loaded, 16)
            ln_step(LG, 0, tail_in, LTAIL, 1)

            dve.wait_ge(base_in, 16)
            dve.tensor_copy(base_rowf[:, 0:CH], base_row[:, 0:CH]).then_inc(base_ready, 1)
            dve.wait_ge(dst_in, 32)
            dve.tensor_tensor(unsorted, dst_all[:, 1:PK + 1], dst_all[:, 0:PK], ALU.is_lt)
            dve.drain()
            dve.tensor_reduce(bad[:, 0:1], unsorted, AX_X, ALU.add)
            dve.wait_ge(base_kept, 1)
            dve.tensor_tensor(delta[:, 1:CH + 1], base[:, 1:CH + 1], base[:, 0:CH], ALU.subtract)
            dve.tensor_tensor(need[:, LAG:CH], base[:, LAG:CH], need[:, LAG:CH], ALU.is_lt)
            dve.drain()
            dve.tensor_scalar(delta[:, CH + 1:64], delta[:, 1:2], 0.0, None, ALU.mult)
            dve.tensor_reduce(bad[:, 1:2], need[:, LAG:CH], AX_X, ALU.add)
            dve.tensor_reduce(bad[:, 2:3], delta[:, 1:CH + 1], AX_X, ALU.max)
            dve.drain()
            dve.memset(delta[:, 0:1], FAR)
            dve.tensor_scalar(bad[:, 2:3], bad[:, 2:3], P - 1.0, None, ALU.is_gt)
            dve.drain()
            dve.tensor_reduce(bad_sum[:], bad[:], AX_X, ALU.add).then_inc(bad_ready, 1)
            dve.wait_ge(bad_summed, 1)
            dve.tensor_scalar(slow_i[:], small[:, 64:65], 0.0, None, ALU.is_gt).then_inc(slow_known, 1)

            def tok_residual(i, b, m, r):
                dve.wait_ge(tok_in[b], 48 * m + 48)
                wait(dve, tok_out[b], 32 * m)
                dve.tensor_tensor(mid_t[0:r, :], x_t[0:r, b, :], bias_sb[0:r, :], ALU.add)
                dve.drain()
                dve.wait_ge(tok_projected, i + 1)
                dve.tensor_tensor(mid_t[0:r, :], mid_t[0:r, :], proj[0][0:r, 0:D], ALU.add)
                dve.drain()
                dve.tensor_tensor(res_t[0:r, b, :], mid_t[0:r, :], beta_sb[0:r, :], ALU.add).then_inc(tok_res, 1)
                dve.bn_stats(tok_stats[0:r, 0, :], mid_t[0:r, :])
                dve.drain()
                dve.bn_aggr(tok_mv[0:r, 0, :], tok_stats[0:r, 0, :])
                dve.drain()
                dve.tensor_scalar(tok_small[0:r, 0, 0:1], tok_mv[0:r, 0:1, 1], EPS, None, ALU.add).then_inc(tok_var, 1)

            def tok_norm(i, b, m, r):
                dve.wait_ge(tok_sd, i + 1)
                scale_of(tok_small, tok_mv, r, 0, 1)
                dve.drain()
                wait(dve, tok_scattered[b], 32 * m)
                dve.tensor_scalar(t_t[0:r, b, :], mid_t[0:r, :], tok_mv[0:r, 0, 0:1], tok_small[0:r, 4, 0:1],
                                  ALU.subtract, ALU.mult).then_inc(tok_t, 1)

            def tok_choose(i, b, m, r):
                dve.wait_ge(tok_gated, i + 1)
                dve.tensor_tensor(logits[0:r, :], small2[0:r, 0:X], gate_b_sb[0:r, :], ALU.add)
                dve.drain()
                dve.max(top_v[0:r, :], logits[0:r, :])
                dve.drain()
                dve.max_index(top_i[0:r, :], top_v[0:r, :], logits[0:r, :])
                dve.tensor_tensor(gap[0:r, :], top_v[0:r, 1:2], top_v[0:r, 0:1], ALU.subtract)
                dve.drain()
                dve.tensor_copy(top_f[0:r, :], top_i[0:r, 0:2])
                dve.drain()
                for k in range(2):
                    dve.tensor_scalar(chosen[0:r, k, :], col_id[0:r, 0:X], top_f[0:r, k:k + 1], None, ALU.is_equal)
                dve.drain()
                dve.tensor_tensor(both[0:r, :], chosen[0:r, 0, :], chosen[0:r, 1, :], ALU.add).then_inc(tok_chosen, 1)

            def tok_place(i, b, m, r):
                dve.wait_ge(tok_exp, i + 1)
                dve.tensor_scalar(gap_d[0:r, :], gap_e[0:r, :], 1.0, None, ALU.add)
                dve.drain()
                dve.reciprocal(gap_r[0:r, :], gap_d[0:r, :])
                dve.drain()
                dve.tensor_tensor(wts_all[0:r, bass.ds(2 * i + 1, 1)], gap_e[0:r, :], gap_r[0:r, :], ALU.mult)
                dve.tensor_copy(wts_all[0:r, bass.ds(2 * i, 1)], gap_r[0:r, :])
                dve.wait_ge(tok_ranked, i + 1)
                dve.tensor_tensor(place[0:r, :], small2[0:r, X:2 * X], slot_base[0:r, :], ALU.add)
                dve.tensor_tensor(routed[0:r, :], routed[0:r, :], both[0:r, :], ALU.add)
                dve.drain()
                for k in range(2):
                    dve.tensor_tensor(placed[0:r, k, :], chosen[0:r, k, :], place[0:r, :], ALU.mult)
                dve.drain()
                dve.tensor_reduce(pos_f[0:r, :], placed[0:r, :, :], AX_X, ALU.add)
                dve.drain()
                dve.tensor_copy(pos_all[0:r, bass.ds(2 * i, 2)], pos_f[0:r, :])
                dve.tensor_copy(exp_all[0:r, bass.ds(2 * i, 2)], top_f[0:r, :])
                dve.tensor_copy(pos_t[b][0:r, :], pos_f[0:r, :]).then_inc(tok_placed, 1)

            def tokens(i, b, m, r):
                for step in (tok_residual, tok_norm, tok_choose, tok_place):
                    step(i, b, m, r)

            def select_chunk(hop, c, b, q, steps=None):
                n = c + CH * hop
                dve.wait_ge(edges_in[b], 48 * (q + CH // 2 * hop) + 48)
                dve.tensor_scalar(dst_rel[b][:], dst_t[b][:], base[:, bass.ds(c, 1)], None, ALU.subtract)
                wait(dve, window_summed, n - 1)
                dve.tensor_scalar(shift[:, b, :], diff_id[:], delta[:, bass.ds(c, 1)], None, ALU.is_equal).then_inc(shift_built, 1)
                dve.drain()
                for j in range(CT):
                    wait(dve, tile_summed, CT * n + j - SR + 1)
                    dve.tensor_scalar(sel[:, j % SR, :], col_id[:], dst_rel[b][:, j:j + 1], w_t[b][:, j:j + 1],
                                      ALU.is_equal, ALU.mult).then_inc(sel_built, 1)
                    if steps and j in steps:
                        steps[j]()

            def with_tokens(i, b, m):
                return {j: (lambda f=f: f(i, b, m, TR)) for j, f in ((14, tok_residual), (16, tok_norm), (21, tok_choose), (25, tok_place))}

            dve.wait_ge(slow_known, 1)
            slow = dve.value_load(slow_i[0:1, 0:1], min_val=0, max_val=1)
            with dve.If(slow):
                for hop in range(2):
                    with dve.Fori(0, ETILES) as k:
                        for loaded in slow_loaded[hop][1:]:
                            dve.wait_ge(loaded, 16 * k + 16)
                        dve.tensor_copy(s_dstf[:], s_dst[:])
                        dve.tensor_copy(s_dst_rowf, s_dst_row)
                        dve.drain()
                        dve.tensor_scalar(s_same_w, s_dst_rowf, s_dstf[:], s_w[:], ALU.is_equal, ALU.mult)
                        dve.scalar_tensor_tensor(out=s_same_below, in0=s_dst_rowf, scalar=s_dstf[:, 0:1], in1=below[:],
                                                 op0=ALU.is_equal, op1=ALU.mult)
                        dve.drain()
                        dve.engine_nop().then_inc(slow_sel, 1)
                        dve.wait_ge(slow_rows[hop][1], 16 * k + 16)
                        dve.wait_ge(slow_summed, k + 1 + ETILES * hop)
                        dve.tensor_tensor(s_new, s_old, win[0][:, 0:D], ALU.add)
                        dve.tensor_scalar(s_repf[:], small[:, 0:1], 0.0, OUT, ALU.is_gt, ALU.mult)
                        dve.drain()
                        dve.tensor_tensor(s_rep[:], s_repf[:], s_dstf[:], ALU.add)
                        dve.drain()
                        dve.tensor_copy(s_put[:], s_rep[:]).then_inc(slow_new, 1)
                tokens(0, 0, 0, TR)
                tokens(1, 1, 0, TR)
                with dve.Fori(1, TT // 2) as m:
                    tokens(2 * m, 0, m, TR)
                    tokens(2 * m + 1, 1, m, TR)
            with dve.Else():
                select_chunk(0, 0, 0, 0)
                select_chunk(0, 1, 1, 0)
                with dve.Fori(1, CH // 2) as q:
                    select_chunk(0, 2 * q, 0, q)
                    select_chunk(0, 2 * q + 1, 1, q)
                with dve.Fori(0, LAG // 2) as q:
                    select_chunk(1, 2 * q, 0, q)
                    select_chunk(1, 2 * q + 1, 1, q)
                q0 = LAG // 2
                select_chunk(1, LAG, 0, q0, with_tokens(0, 0, 0))
                select_chunk(1, LAG + 1, 1, q0, with_tokens(1, 1, 0))
                with dve.Fori(q0 + 1, CH // 2) as q:
                    select_chunk(1, 2 * q, 0, q, with_tokens(2 * q - LAG, 0, q - q0))
                    select_chunk(1, 2 * q + 1, 1, q, with_tokens(2 * q + 1 - LAG, 1, q - q0))
                tokens(TT - 3, 0, TT // 2 - 1, TR)
                tokens(TT - 2, 1, TT // 2 - 1, TR)
            tokens(TT - 1, 0, TT // 2, TLAST)

            dve.drain()
            dve.memset(gap_d[:], 0.0).then_inc(counted, 1)
            dve.wait_ge(counted, 2)
            def tiles_of(target, counts):
                dve.tensor_scalar(target, counts, 1.0 / P, (P - 1.0) / P - 0.498, ALU.mult, ALU.add)
                dve.drain()
                dve.tensor_scalar(target, target, ROUND, None, ALU.add)
                dve.drain()
                return dve.tensor_scalar(target, target, -ROUND, None, ALU.add)

            tiles_of(tiles_T[:, :], small[0:X, 0:P]).then_inc(tiles_ready, 1)
            dve.tensor_tensor(zero_f[:], small[:, P:P + X], slot_base[:], ALU.add)
            dve.drain()
            dve.tensor_copy(zero_at[:], zero_f[:])
            dve.wait_ge(cumulated, 1)
            dve.tensor_copy(tiles_C[:], small2[:, 0:2 * X])
            dve.drain()
            dve.tensor_scalar(step_cmp[:], tiles_C[:, 0:X], row_id[:], None, ALU.is_le)
            dve.drain()
            dve.tensor_tensor(step_cum[:], step_cmp[:], tiles_C[:, X:2 * X], ALU.mult)
            dve.tensor_reduce(step_f[:, 0:1], step_cmp[:], AX_X, ALU.add)
            dve.drain()
            dve.tensor_reduce(step_f[:, 1:2], step_cum[:], AX_X, ALU.add)
            dve.drain()
            dve.tensor_tensor(step_f[:, 2:3], row_id[:], step_f[:, 1:2], ALU.subtract)
            dve.tensor_scalar(step_f[:, 3:4], step_f[:, 0:1], float(CAP), None, ALU.mult)
            dve.drain()
            dve.scalar_tensor_tensor(out=step_f[:, 3:4], in0=step_f[:, 2:3], scalar=float(P), in1=step_f[:, 3:4], op0=ALU.mult, op1=ALU.add)
            dve.tensor_scalar(step_f[:, 0:1], step_f[:, 0:1], X - 1.0, None, ALU.min)
            dve.drain()
            dve.tensor_copy(step_i[:, 0:1], step_f[:, 3:4])
            dve.tensor_copy(step_i[:, 1:2], step_f[:, 0:1])
            dve.drain()
            dve.memset(gap_d[:], 0.0).then_inc(steps_ready, 1)

            dve.tensor_tensor(slot_fix[:], tiles_C[:, 0:X], tiles_C[:, X:2 * X], ALU.subtract)
            dve.drain()
            dve.tensor_scalar(slot_fix[:], slot_fix[:], float(P), None, ALU.mult)
            dve.drain()
            dve.tensor_tensor(slot_fix[:], slot_fix[:], slot_base[:], ALU.subtract)
            for e in range(X):
                dve.drain()
                dve.tensor_scalar(pos_fix[:], exp_all[:], float(e), slot_fix[:, e:e + 1], ALU.is_equal, ALU.mult)
                dve.drain()
                dve.tensor_tensor(pos_all[:], pos_all[:], pos_fix[:], ALU.add)

            def keep_up(s, r, g):
                b = r % 2
                dve.wait_ge(bias_in[r], 16 * g + 16)
                wait(dve, h_turned, s - 1)
                dve.wait_ge(up_done, s + 1)
                dve.tensor_tensor(hb[b], win[b][:, :], bias_t[r][:, 0:F], ALU.add).then_inc(up_kept, 1)

            def keep_down(s, r, g):
                b = r % 2
                wait(dve, y_out[b], 16 * (2 * g + r // 2))
                dve.wait_ge(down_done, s + 1)
                dve.tensor_tensor(ys[b], proj[b][:, 0:D], bias_t[r][:, F:F + D], ALU.add).then_inc(y_kept, 1)

            def expert_step(s, r, g):
                if not (isinstance(s, int) and s == STEPS - 1):
                    keep_up(s + 1, (r + 1) % 4, g + (r + 1) // 4)
                keep_down(s, r, g)

            keep_up(0, 0, 0)
            steps_of_four(dve, STEPS, expert_step)

            def stage_places(i, u):
                dve.tensor_copy(pos_s[u][:], pos_all[:, bass.ds(2 * i, 2)]).then_inc(pos_staged, 1)

            def final_pair(m, g, h, n, r):
                for b in range(n):
                    u = 2 * h + b
                    dve.wait_ge(fin_t_in[u], 16 * g + 16)
                    dve.wait_ge(y_in[u], 32 * g + 32)
                    dve.scalar_tensor_tensor(out=f_mix[b][0:r, :], in0=y_a[u][0:r, :], scalar=wts_all[0:r, bass.ds(4 * m + 2 * b, 1)],
                                             in1=f_t[u][0:r, :], op0=ALU.mult, op1=ALU.add)
                dve.drain()
                for b in range(n):
                    dve.scalar_tensor_tensor(out=f_sum[b][0:r, :], in0=y_b[2 * h + b][0:r, :], scalar=wts_all[0:r, bass.ds(4 * m + 2 * b + 1, 1)],
                                             in1=f_mix[b][0:r, :], op0=ALU.mult, op1=ALU.add)
                dve.drain()
                for b in range(n):
                    dve.bn_stats(tok_stats[0:r, b, :], f_sum[b][0:r, :])
                dve.drain()
                for b in range(n):
                    dve.bn_aggr(tok_mv[0:r, b, :], tok_stats[0:r, b, :])
                dve.drain()
                dve.tensor_scalar(tok_small[0:r, 0, 0:n], tok_mv[0:r, 0:n, 1], EPS, None, ALU.add).then_inc(fin_var, 1)
                if not (isinstance(m, int) and m >= TT // 2 - 1):
                    for b in range(1 if isinstance(m, int) and m == TT // 2 - 2 else 2):
                        stage_places(2 * m + 4 + b, 2 * h + b)
                for b in range(n):
                    dve.scalar_tensor_tensor(out=f_scaled[b][0:r, :], in0=f_sum[b][0:r, :], scalar=tok_mv[0:r, b, 0:1],
                                             in1=gamma_sb[0:r, :], op0=ALU.subtract, op1=ALU.mult)
                dve.wait_ge(fin_sd, m + 1)
                scale_of(tok_small, tok_mv, r, 0, n)
                dve.drain()
                for b in range(n):
                    u = 2 * h + b
                    dve.wait_ge(fin_res_in[u], 16 * g + 16)
                    wait(dve, out_stored[b], 16 * m)
                    dve.scalar_tensor_tensor(out=f_out[b][0:r, :], in0=f_scaled[b][0:r, :], scalar=tok_small[0:r, 4, b:b + 1],
                                             in1=f_res[u][0:r, :], op0=ALU.mult, op1=ALU.add).then_inc(fin_ready, 1)

            for i in range(4):
                stage_places(i, i)
            for b in range(2):
                dve.wait_ge(y_out[b], 16 * (STEPS // 2 + 1 - b))
            pairs_of_tiles(dve, final_pair)

        @block.tensor
        def _(pe):
            pe.wait_ge(consts_ready, 1)
            pe.wait_ge(base_ready, 1)
            pe.matmul(small[:, 0:64], ones[0:1, :], base_rowf[:, :], start=True, stop=True).then_inc(base_spread, 1)
            pe.wait_ge(bad_ready, 1)
            pe.matmul(small[:, 64:65], ones[:], bad_sum[:], start=True, stop=True).then_inc(bad_summed, 1)
            pe.wait_ge(params_in, 96)

            def tok_turn(i, b, m, r):
                pe.wait_ge(tok_in[b], 48 * m + 48)
                wait(pe, tok_turned_kept, i)
                for k in range(2 * DH):
                    last = pe.transpose(turn[:, k * P:k * P + r], h_t[0:r, b, k * P:(k + 1) * P], ident[0:r, 0:r])
                last.then_inc(tok_turned, 1)

            def tok_project(i, b, m, r):
                wait(pe, tok_res, i)
                pe.wait_ge(tok_turned_kept, i + 1)
                for k in range(2 * DH):
                    last = pe.matmul(proj[0][0:r, 0:D], hT_t[:, k, 0:r], gnn_w_sb[:, k, :], start=(k == 0), stop=(k == 2 * DH - 1))
                last.then_inc(tok_projected, 1)

            def tok_turn_t(i, b, m, r):
                wait(pe, t_turned_kept, i)
                pe.wait_ge(tok_t, i + 1)
                for k in range(DH):
                    last = pe.transpose(turn2[:, k * P:k * P + r], t_t[0:r, b, k * P:(k + 1) * P], ident[0:r, 0:r])
                last.then_inc(t_turned, 1)

            def tok_gate(i, b, m, r):
                wait(pe, tok_placed, i)
                pe.wait_ge(t_turned_kept, i + 1)
                for k in range(DH):
                    last = pe.matmul(small2[0:r, 0:X], tT_t[:, k, 0:r], gate_w_sb[:, k, :], start=(k == 0), stop=(k == DH - 1))
                last.then_inc(tok_gated, 1)

            def tok_rank(i, b, m, r):
                pe.wait_ge(tok_chosen, i + 1)
                pe.matmul(small2[0:r, X:2 * X], below[0:r, 0:r], both[0:r, :], start=True, stop=False)
                pe.matmul(small2[0:r, X:2 * X], ones[:, 0:r], routed[:, :], start=False, stop=True).then_inc(tok_ranked, 1)

            steps_at = {8: tok_turn, 11: tok_project, 17: tok_turn_t, 20: tok_gate, 24: tok_rank}

            def tokens(i, b, m, r):
                for step in (tok_turn, tok_project, tok_turn_t, tok_gate, tok_rank):
                    step(i, b, m, r)

            def sum_chunk(hop, c, b, token_tile=None):
                n = c + CH * hop
                wait(pe, window_kept, n - 1)
                for j in range(CT):
                    pe.wait_ge(sel_built, CT * n + j + 1)
                    pe.wait_ge(rows_in[j], 16 * n + 16)
                    pe.matmul(win[b][:, 0:D], sel[:, j % SR, :], rows[:, j, :], start=(j == 0), stop=False).then_inc(tile_summed, 1)
                    if token_tile and j in steps_at:
                        steps_at[j](*token_tile)
                pe.wait_ge(shift_built, n + 1)
                wait(pe, window_kept, n)
                pe.matmul(win[b][:, 0:D], shift[:, b, :], kept[:, 1 - b, :], start=False, stop=True).then_inc(window_summed, 1)

            pe.wait_ge(slow_known, 1)
            slow = pe.value_load(slow_i[0:1, 0:1], min_val=0, max_val=1)
            with pe.If(slow):
                for hop in range(2):
                    with pe.Fori(0, ETILES) as k:
                        pe.wait_ge(slow_sel, k + 1 + ETILES * hop)
                        pe.wait_ge(slow_rows[hop][0], 16 * k + 16)
                        pe.matmul(win[0][:, 0:D], s_same_w, s_rows, start=True, stop=True)
                        pe.matmul(small[:, 0:1], s_same_below, ones[:, 0:1], start=True, stop=True).then_inc(slow_summed, 1)
                tokens(0, 0, 0, TR)
                tokens(1, 1, 0, TR)
                with pe.Fori(1, TT // 2) as m:
                    tokens(2 * m, 0, m, TR)
                    tokens(2 * m + 1, 1, m, TR)
            with pe.Else():
                sum_chunk(0, 0, 0)
                sum_chunk(0, 1, 1)
                with pe.Fori(1, CH // 2) as q:
                    sum_chunk(0, 2 * q, 0)
                    sum_chunk(0, 2 * q + 1, 1)
                with pe.Fori(0, LAG // 2) as q:
                    sum_chunk(1, 2 * q, 0)
                    sum_chunk(1, 2 * q + 1, 1)
                sum_chunk(1, LAG, 0, (0, 0, 0, TR))
                sum_chunk(1, LAG + 1, 1, (1, 1, 0, TR))
                with pe.Fori(LAG // 2 + 1, CH // 2) as q:
                    sum_chunk(1, 2 * q, 0, (2 * q - LAG, 0, q - LAG // 2, TR))
                    sum_chunk(1, 2 * q + 1, 1, (2 * q + 1 - LAG, 1, q - LAG // 2, TR))
                tokens(TT - 3, 0, TT // 2 - 1, TR)
                tokens(TT - 2, 1, TT // 2 - 1, TR)
            tokens(TT - 1, 0, TT // 2, TLAST)

            pe.wait_ge(counted, 1)
            pe.matmul(small[0:X, 0:P], routed[:, :], ones[:], start=True, stop=True)
            pe.matmul(small[:, P:P + X], ones[:], routed[:, :], start=True, stop=True).then_inc(counted, 1)
            pe.wait_ge(tiles_ready, 1)
            pe.matmul(small2[:, 0:2 * X], tiles_T[:, :], tri_eye[:, :], start=True, stop=True).then_inc(cumulated, 1)

            def turn_xs(s, r, g):
                pe.wait_ge(xs_in[r], 16 * g + 16)
                wait(pe, xs_kept, s)
                for k in range(DH):
                    last = pe.transpose(turn2[:, k * P:(k + 1) * P], xs[r][:, k * P:(k + 1) * P], ident[:])
                last.then_inc(xs_turned, 1)

            def expert_of(s):
                return pe.value_load(step_row[0:1, bass.ds(2 * s + 1, 1)], min_val=0, max_val=X - 1)

            def up(s, b):
                e = expert_of(s)
                wait(pe, up_kept, s - 1)
                pe.wait_ge(xs_kept, s + 1)
                for k in range(DH):
                    last = pe.matmul(win[b][:, :], xsT[b][:, k, :], w1_sb[:, bass.ds(e * DH + k, 1), :], start=(k == 0), stop=(k == DH - 1))
                last.then_inc(up_done, 1)

            def turn_h(s, b):
                wait(pe, h_kept, s)
                pe.wait_ge(up_kept, s + 1)
                for k in range(FH):
                    last = pe.transpose(turn[:, k * P:(k + 1) * P], hb[b][:, k * P:(k + 1) * P], ident[:])
                last.then_inc(h_turned, 1)

            def down(s, b):
                e = expert_of(s)
                wait(pe, y_kept, s - 1)
                pe.wait_ge(h_kept, s + 1)
                for k in range(FH):
                    last = pe.matmul(proj[b][:, 0:D], hT[b][:, k, :], w2_sb[:, bass.ds(e * FH + k, 1), :], start=(k == 0), stop=(k == FH - 1))
                last.then_inc(down_done, 1)

            def expert_step(s, r, g):
                b = r % 2
                known = isinstance(s, int)
                turn_h(s, b)
                if not (known and s == STEPS - 1):
                    up(s + 1, 1 - b)
                down(s, b)
                if not (known and s >= STEPS - 2):
                    turn_xs(s + 2, (r + 2) % 4, g + (r + 2) // 4)

            pe.wait_ge(weights_in, 16 * 2 * X)
            pe.wait_ge(steps_in, 16)
            turn_xs(0, 0, 0)
            up(0, 0)
            turn_xs(1, 1, 0)
            steps_of_four(pe, STEPS, expert_step)


_INS = ["x", "src", "dst", "edge_weight", "L0_gnn_W", "L0_gnn_bias", "L0_ffn_gate_w", "L0_ffn_gate_b", "L0_ffn_w1",
        "L0_ffn_b1", "L0_ffn_w2", "L0_ffn_b2", "L0_ffn_gamma", "L0_ffn_beta"]


def kernel(**inputs):
    import numpy as np
    import concourse.bacc as bacc
    from concourse.bass_utils import run_bass_kernel_spmd

    nc = bacc.Bacc("TRN2", target_bir_lowering=False, num_devices=1)
    arrays, args = {}, []
    for name in _INS:
        a = np.ascontiguousarray(inputs[name])
        arrays[f"in_{name}"] = a
        args.append(nc.dram_tensor(f"in_{name}", a.shape, mybir.dt.from_np(a.dtype), kind="ExternalInput").ap())
    args.append(nc.dram_tensor("out", (N, D), F32, kind="ExternalOutput").ap())
    build(nc, *args)
    r = run_bass_kernel_spmd(nc, [arrays], core_ids=[0])
    return r.results[0]["out"]
```

```python
from contextlib import ExitStack

import concourse.bass as bass
from concourse import mybir

ALU = mybir.AluOpType
ACT = mybir.ActivationFunctionType
AX_X = mybir.AxisListType.X
F32 = mybir.dt.float32
I32 = mybir.dt.int32
U32 = mybir.dt.uint32

P = 128
N = 6250
D = 256
DH = D // P
NE = 206250
EPS = 1e-5

CT = 26
CH = 62
CE = CT * P
NEP = CH * CE
SR = CT // 2
GROUPS = {0: 4, 5: 8, 9: 12}
NR = N + P + 22
assert NEP >= NE and CH % 2 == 0

LR = 6
LG = 8
LMAIN = P * LR * LG
LTAIL = N - LMAIN
assert 0 < LTAIL <= P

TR = 104
TT = -(-N // TR)
TLAST = N - (TT - 1) * TR
LAG = 4
assert TT % 4 == 1 and CH - LAG == TT - 3

X = 16
F = 512
FH = F // P
TE = 26
ROUND_TOKENS = [TE * TR, N - TE * TR]
CAP = max(ROUND_TOKENS) + P
STEPS = [(2 * n + X * (P - 1)) // P for n in ROUND_TOKENS]
SPARE = max(s - (-(-2 * n // P)) for s, n in zip(STEPS, ROUND_TOKENS))
NSLOT = X * CAP + SPARE * P
EARLY = TE + LAG + 2
assert max(STEPS) <= P and TE % 2 == 0 and EARLY % 2 == 0 and TE + LAG >= 8
assert STEPS[0] % 4 == 2 and STEPS[0] <= 2 * (CH - EARLY) and STEPS[0] // 4 == (CH - EARLY) // 2 - 1

FOURS = (TT - TE - 1) // 4
LEFT = TT - TE - 1 - 4 * FOURS
assert FOURS % 2 == 0 and LEFT > 0 and TE // 2 < (STEPS[1] - 3) // 4

ROUND = 8388608.0
FAR = 1000.0
OUT = 65536.0
ETILES = NEP // P


class Round:
    pass


class Finish:
    pass


def wait(eng, sem, value):
    if isinstance(value, int) and value <= 0:
        return
    eng.wait_ge(sem, value)


def wait_apart(eng, always, sem, value):
    if not isinstance(value, int):
        value = eng.to_reg(value)
    eng.wait_ge(always, 1)
    wait(eng, sem, value)


def steps_of_four(eng, count, step):
    for r in range(4):
        step(r, r, 0)
    whole = (count - 3) // 4
    with eng.Fori(1, whole) as g:
        for r in range(4):
            step(4 * g + r, r, g)
    for s in range(4 * whole, count):
        step(s, s % 4, s // 4)


def late_steps(eng, count, step):
    for r in range(4):
        step(r, r, 0, True)
    whole = (count - 3) // 4
    with eng.Fori(1, TE // 2) as g:
        for r in range(4):
            step(4 * g + r, r, g, True)
    with eng.Fori(TE // 2, whole) as g:
        for r in range(4):
            step(4 * g + r, r, g, False)
    for s in range(4 * whole, count):
        step(s, s % 4, s // 4, False)


def late_groups(eng, group):
    for h in range(2):
        group(h, 0, h, 4, TR)
    with eng.Fori(1, FOURS // 2 - 1) as g:
        for h in range(2):
            group(2 * g + h, g, h, 4, TR)
    for h in range(2):
        group(FOURS - 2 + h, FOURS // 2 - 1, h, 4, TR)
    group(FOURS, FOURS // 2, 0, LEFT, TR)
    group(FOURS + 1, FOURS // 2, 1, 1, TLAST)


def build(nc, x, src, dst, edge_weight, gnn_w, gnn_bias, gate_w, gate_b, w1, b1, w2, b2, gamma, beta, out):
    ctx = ExitStack()
    with ctx:
        def sb(name, shape, dt=F32):
            return ctx.enter_context(nc.sbuf_tensor(name, shape, dt))

        def bank(name):
            return ctx.enter_context(nc.psum_tensor(name, [P, 512], F32))

        def sem(name):
            return ctx.enter_context(nc.semaphore(name))

        def sems(name, n):
            return [sem(f"{name}{i}") for i in range(n)]

        def dram(name, shape, dt=F32):
            return nc.dram_tensor(name, shape, dt).ap()

        xn_rows = dram("xn_rows", (N, D))
        h_rows = [dram("h1_rows", (NR, D)), dram("h2_rows", (NR, D))]
        t_rows = dram("t_rows", (N, D))
        res_rows = dram("res_rows", (N, D))
        src_pad = dram("src_pad", (NEP,), I32)
        dst_pad = dram("dst_pad", (NEP + NEP // P,), I32)
        w_pad = dram("w_pad", (NEP,))
        slot_in = [dram(f"slot_in{k}", (NSLOT, D)) for k in range(2)]
        slot_out = dram("slot_out", (sum(STEPS) * P, D))
        bias_tab = dram("bias_tab", (X, F + D))
        step_tab = [dram(f"step_tab{k}", (P, 2), I32) for k in range(2)]

        w1_sb = sb("w1_sb", [P, X * DH, F])
        w2_sb = sb("w2_sb", [P, X * FH, D])
        scratch1 = w1_sb[:, 0:13, :].rearrange("p a b -> p (a b)")
        ln_in = [scratch1[:, b * LR * D:(b + 1) * LR * D].rearrange("p (r d) -> p r d", d=D) for b in range(2)]
        ln_out = [scratch1[:, (2 + b) * LR * D:(3 + b) * LR * D].rearrange("p (r d) -> p r d", d=D) for b in range(2)]
        tail_in = scratch1[:, 4 * LR * D:(4 * LR + 1) * D].unsqueeze(1)
        tail_out = scratch1[:, (4 * LR + 1) * D:(4 * LR + 2) * D].unsqueeze(1)
        PK = NEP // P
        scratch2 = w2_sb[:, 0:16, :].rearrange("p a b -> p (a b)")
        dst_all = scratch2[:, 0:PK + 1].bitcast(I32)
        unsorted = scratch2[:, PK + 1:2 * PK + 1]
        pad_i = sb("pad_i", [1, 3 * P], I32)

        rows = sb("rows", [P, SR, D])
        sel = sb("sel", [P, SR, P])
        kept = sb("kept", [P, 2, D])
        shift = sb("shift", [P, 2, P])
        src_t = [sb(f"src_t{b}", [P, CT], I32) for b in range(2)]
        dst_t = [sb(f"dst_t{b}", [P, CT], I32) for b in range(2)]
        w_t = [sb(f"w_t{b}", [P, CT]) for b in range(2)]
        dst_rel = [sb(f"dst_rel{b}", [P, CT]) for b in range(2)]

        col_id = sb("col_id", [P, P])
        diff_id = sb("diff_id", [P, P])
        ident = sb("ident", [P, P])
        below = sb("below", [P, P])
        ones = sb("ones", [P, P])
        zeros = sb("zeros", [P, D])
        tri_eye = sb("tri_eye", [X, 2 * X])
        row_id = sb("row_id", [P, 1])
        base_row = sb("base_row", [1, 64], I32)
        base_rowf = sb("base_rowf", [1, 64])
        base = sb("base", [P, 64])
        delta = sb("delta", [P, 64])
        need = sb("need", [P, 64])
        bad = sb("bad", [P, 3])
        bad_sum = sb("bad_sum", [P, 1])
        slow_i = sb("slow_i", [P, 1], I32)

        gnn_w_sb = sb("gnn_w_sb", [P, 2 * DH, D])
        bias_sb = sb("bias_sb", [P, D])
        gamma_sb = sb("gamma_sb", [P, D])
        beta_sb = sb("beta_sb", [P, D])
        gate_w_sb = sb("gate_w_sb", [P, DH, X])
        gate_b_sb = sb("gate_b_sb", [P, X])
        slot_base = sb("slot_base", [P, X])

        ln_stats = sb("ln_stats", [P, LR, 6])
        ln_mv = [sb(f"ln_mv{b}", [P, LR, 2]) for b in range(2)]
        ln_small = [sb(f"ln_small{b}", [P, 6, LR]) for b in range(2)]

        x_t = sb("x_t", [P, 2, D])
        h_t = sb("h_t", [P, 2, 2 * D])
        hT_t = sb("hT_t", [P, 2 * DH, TR])
        mid_t = sb("mid_t", [P, D])
        res_t = sb("res_t", [P, 2, D])
        t_t = sb("t_t", [P, 2, D])
        tT_t = sb("tT_t", [P, DH, TR])
        tok_stats = sb("tok_stats", [P, 4, 6])
        tok_mv = sb("tok_mv", [P, 4, 2])
        tok_small = sb("tok_small", [P, 6, 4])
        logits = sb("logits", [P, X])
        top_v = sb("top_v", [P, 8])
        top_i = sb("top_i", [P, 8], U32)
        top_f = sb("top_f", [P, 2])
        gap = sb("gap", [P, 1])
        gap_e = sb("gap_e", [P, 1])
        gap_d = sb("gap_d", [P, 1])
        gap_r = sb("gap_r", [P, 1])
        chosen = sb("chosen", [P, 2, X])
        both = sb("both", [P, X])
        routed = sb("routed", [P, X])
        place = sb("place", [P, X])
        placed = sb("placed", [P, 2, X])
        pos_f = sb("pos_f", [P, 2])
        pos_t = [sb(f"pos_t{b}", [P, 2], I32) for b in range(2)]
        pos_all = sb("pos_all", [P, 2 * TT])
        exp_all = sb("exp_all", [P, 2 * TT])
        pos_fix = sb("pos_fix", [P, 2 * TT])
        slot_fix = sb("slot_fix", [P, X])
        wts_all = sb("wts_all", [P, 2 * TT])

        tiles_T = sb("tiles_T", [X, P])
        tiles_C = sb("tiles_C", [P, 2 * X])
        step_cmp = sb("step_cmp", [P, X])
        step_cum = sb("step_cum", [P, X])
        step_f = sb("step_f", [P, 4])
        step_i = [sb(f"step_i{k}", [P, 2], I32) for k in range(2)]
        step_row = [sb(f"step_row{k}", [1, 2 * P], I32) for k in range(2)]
        zero_f = sb("zero_f", [P, X])
        zero_at = [sb(f"zero_at{k}", [P, X], I32) for k in range(2)]

        early_room = sb("early_room", [P, 3584])
        rooms = [t.rearrange("p a b -> p (a b)") for t in (rows[:, :, :], sel[:, :, :])] + [early_room[:, :]]
        sizes = [SR * D, SR * P, 3584]

        def parts(room_list):
            left = {k: 0 for k in room_list}

            def part(n):
                k = next(k for k in left if left[k] + n <= sizes[k])
                left[k] += n
                return rooms[k][:, left[k] - n:left[k]]
            return part

        def in_tiles(a):
            return a.rearrange("p (k t) -> p k t", t=P)

        def round_buffers(part, depth, ring):
            f = Round()
            f.depth, f.ring = depth, ring
            f.bias = [part(F + D) for _ in range(ring)]
            f.hb = [part(F) for _ in range(depth)]
            f.hT = [in_tiles(part(F)) for _ in range(depth)]
            f.xs = [part(D) for _ in range(ring)]
            f.xsT = [in_tiles(part(D)) for _ in range(depth)]
            f.ys = [part(D) for _ in range(depth)]
            return f

        early = round_buffers(parts([2]), 1, 2)
        late = round_buffers(parts([0, 1, 2]), 2, 4)
        fin_early, fin_late = Finish(), Finish()
        fin_early.y_a = [h_t[:, b, 0:D] for b in range(2)]
        fin_early.y_b = [h_t[:, b, D:2 * D] for b in range(2)]
        fin_early.t = [x_t[:, b, :] for b in range(2)]
        fin_early.res = [res_t[:, b, :] for b in range(2)]
        part = parts([0, 1, 2])
        fin_late.y_a, fin_late.y_b, fin_late.t, fin_late.res = ([part(D) for _ in range(8)] for _ in range(4))
        for f, name in ((fin_early, "early"), (fin_late, "late")):
            f.ring = len(f.t)
            f.half = f.ring // 2
            f.pos = [sb(f"pos_{name}{b}", [P, 2], I32) for b in range(f.ring)]

        s_src = sb("s_src", [P, 1], I32)
        s_dst = sb("s_dst", [P, 1], I32)
        s_w = sb("s_w", [P, 1])
        s_dstf = sb("s_dstf", [P, 1])
        s_rep = sb("s_rep", [P, 1])
        s_repf = sb("s_repf", [P, 1])
        s_put = sb("s_put", [P, 1], I32)
        s_dst_row = sel[:, 0, :].bitcast(I32)
        s_dst_rowf = sel[:, 1, :]
        s_same_w = sel[:, 2, :]
        s_same_below = sel[:, 3, :]
        s_rows, s_old, s_new = rows[:, 0, :], rows[:, 1, :], rows[:, 2, :]

        win = [bank("win0"), bank("win1")]
        turn = bank("turn")
        turn2 = bank("turn2")
        proj = [bank("proj0"), bank("proj1")]
        small = bank("small")
        small2 = bank("small2")
        early.xs_out, early.h_out = small[:, 0:2 * P], small[:, :]
        early.up_out, early.down_out = [proj[1][:, :]], [proj[1][:, 0:D]]
        late.xs_out, late.h_out = turn2[:, 0:2 * P], turn[:, :]
        late.up_out, late.down_out = [w[:, :] for w in win], [p[:, 0:D] for p in proj]

        iotas = sem("iotas")
        fills = sem("fills")
        consts_ready = sem("consts_ready")
        params_in = sem("params_in")
        edges_copied = sem("edges_copied")
        pad_in = sem("pad_in")
        dst_in = sem("dst_in")
        base_in = sem("base_in")
        base_ready = sem("base_ready")
        base_spread = sem("base_spread")
        base_kept = sem("base_kept")
        bad_ready = sem("bad_ready")
        bad_summed = sem("bad_summed")
        slow_known = sem("slow_known")
        ln_loaded = sems("ln_loaded", 2)
        tail_loaded = sem("tail_loaded")
        ln_var = sem("ln_var")
        ln_sd = sem("ln_sd")
        ln_scaled = sem("ln_scaled")
        ln_applied = sem("ln_applied")
        ln_stored = sems("ln_stored", 2)
        tail_stored = sem("tail_stored")
        weights_in = sem("weights_in")

        edges_in = sems("edges_in", 2)
        rel_ready = sem("rel_ready")
        sel_built = sem("sel_built")
        shift_built = sem("shift_built")
        rows_in = sems("rows_in", SR)
        tile_summed = sem("tile_summed")
        window_summed = sem("window_summed")
        window_kept = sem("window_kept")
        window_out = sem("window_out")

        slow_zeroed = sem("slow_zeroed")
        slow_loaded = [sems(f"slow_loaded{h}_", 4) for h in range(2)]
        slow_sel = sem("slow_sel")
        slow_rows = [sems(f"slow_rows{h}_", 2) for h in range(2)]
        slow_summed = sem("slow_summed")
        slow_new = sem("slow_new")
        slow_stored = sems("slow_stored", 2)

        tok_in = sems("tok_in", 2)
        tok_turned = sem("tok_turned")
        tok_turned_kept = sem("tok_turned_kept")
        tok_projected = sem("tok_projected")
        tok_res = sem("tok_res")
        tok_var = sem("tok_var")
        tok_sd = sem("tok_sd")
        tok_t = sem("tok_t")
        tok_out = sems("tok_out", 2)
        t_turned = sem("t_turned")
        t_turned_kept = sem("t_turned_kept")
        tok_gated = sem("tok_gated")
        tok_chosen = sem("tok_chosen")
        tok_exp = sem("tok_exp")
        tok_ranked = sem("tok_ranked")
        tok_placed = sem("tok_placed")
        tok_scattered = sems("tok_scattered", 2)

        counted = sem("counted")
        tiles_ready = sem("tiles_ready")
        cumulated = sem("cumulated")
        steps_ready = sem("steps_ready")
        steps_out = sem("steps_out")
        steps_in = sem("steps_in")
        zeros_out = sem("zeros_out")
        spare_out = sem("spare_out")
        biases_out = sem("biases_out")
        for k, f, name in ((0, early, "early"), (1, late, "late")):
            f.k = k
            f.steps = STEPS[k]
            f.xs_in = sems(f"{name}_xs_in", f.ring)
            f.bias_in = sems(f"{name}_bias_in", f.ring)
            f.xs_turned = sem(f"{name}_xs_turned")
            f.xs_kept = sem(f"{name}_xs_kept")
            f.up_done = sem(f"{name}_up_done")
            f.up_kept = sem(f"{name}_up_kept")
            f.h_turned = sem(f"{name}_h_turned")
            f.h_kept = sem(f"{name}_h_kept")
            f.down_done = sem(f"{name}_down_done")
            f.y_kept = sem(f"{name}_y_kept")
            f.y_out = sems(f"{name}_y_out", f.depth)

        for f, name in ((fin_early, "early"), (fin_late, "late")):
            f.pos_staged = sem(f"{name}_pos_staged")
            f.y_in = sems(f"{name}_y_in", 2)
            f.t_in = sems(f"{name}_t_in", 2)
            f.res_in = sems(f"{name}_res_in", 2)
            f.var = sem(f"{name}_var")
            f.sd = sem(f"{name}_sd")
            f.ready = sem(f"{name}_ready")
            f.stored = sems(f"{name}_stored", 2)

        block = ctx.enter_context(nc.Block())

        x_main = x[0:LMAIN, :].rearrange("(p r) d -> p r d", p=P)
        xn_main = xn_rows[0:LMAIN, :].rearrange("(p r) d -> p r d", p=P)
        hop_in = [xn_rows, h_rows[0][0:N, :]]
        gate_w_v = gate_w.rearrange("(k p) e -> p k e", p=P)
        gnn_w_v = gnn_w.rearrange("h (k p) d -> p (h k) d", p=P)

        def chunk_view(a, c):
            return a[bass.ds(c * CE, CE)].rearrange("(p j) -> p j", p=P)

        def as_row(a):
            return a.rearrange("(a n) -> a n", a=1)

        def tile_rows(i, r):
            return bass.ds(i * TR, r)

        def uses(r, g, n):
            return (4 // n) * g + r // n

        def tile_of(m):
            if not isinstance(m, int) or m <= FOURS:
                return TE + 4 * m
            return TT - 1

        def wait_all_out(eng):
            for f in (early, late):
                for b in range(f.depth):
                    eng.wait_ge(f.y_out[b], 16 * (-(-(f.steps - b) // f.depth)))

        @block.sync
        def _(sp):
            def load_ln(g, b, m):
                wait(sp, ln_applied, g - 1)
                sp.dma_start(ln_in[b], x_main[:, bass.ds(g * LR, LR), :]).then_inc(ln_loaded[b], 16)

            load_ln(0, 0, 0)
            load_ln(1, 1, 0)
            sp.dma_start(tail_in[0:LTAIL, 0, :], x[LMAIN:N, :]).then_inc(tail_loaded, 16)

            sp.dma_start(as_row(dst_pad[0:NE]), as_row(dst)).then_inc(edges_copied, 16)
            sp.dma_start(as_row(src_pad[0:NE]), as_row(src)).then_inc(edges_copied, 16)
            sp.dma_start(as_row(w_pad[0:NE]), as_row(edge_weight)).then_inc(edges_copied, 16)
            npad = NEP - NE
            sp.wait_ge(fills, 3)
            sp.dma_start(as_row(src_pad[NE:NEP]), pad_i[:, 0:npad]).then_inc(edges_copied, 16)
            sp.dma_start(as_row(w_pad[NE:NEP]), pad_i[:, 0:npad].bitcast(F32)).then_inc(edges_copied, 16)
            sp.dma_start(as_row(dst_pad[NE:NEP + P]), pad_i[:, P:P + npad + P]).then_inc(edges_copied, 16)
            with sp.Fori(1, LG // 2) as m:
                load_ln(2 * m, 0, m)
                load_ln(2 * m + 1, 1, m)
            sp.dma_start(bias_tab[:, 0:F], b1).then_inc(biases_out, 16)
            sp.dma_start(bias_tab[:, F:F + D], b2).then_inc(biases_out, 16)
            sp.wait_ge(edges_copied, 96)
            sp.dma_start(dst_all[:, 0:PK], dst_pad[0:NEP].rearrange("(p k) -> p k", p=P)).then_inc(dst_in, 16)
            firsts = dst_pad[CE:NEP].rearrange("(c e) -> c e", e=CE)[:, 0:1].rearrange("c e -> e c")
            with nc.allow_non_contiguous_dma("one element per partition, and per chunk"):
                sp.dma_start(dst_all[:, PK:PK + 1], dst_pad[PK:PK + NEP].rearrange("(p k) -> p k", p=P)[:, 0:1]).then_inc(dst_in, 16)
                sp.dma_start(base_row[:, 1:CH], firsts).then_inc(base_in, 16)

            def load_tokens(i, b, m, r):
                wait(sp, tok_res, i - 1)
                sp.dma_start(x_t[0:r, b, :], x[tile_rows(i, r), :]).then_inc(tok_in[b], 16)
                sp.dma_start(h_t[0:r, b, 0:D], h_rows[0][tile_rows(i, r), :]).then_inc(tok_in[b], 16)
                sp.dma_start(h_t[0:r, b, D:2 * D], h_rows[1][tile_rows(i, r), :]).then_inc(tok_in[b], 16)

            def load_edges(hop, c, b):
                wait(sp, tile_summed, CT * (c + CH * hop - 1))
                sp.dma_start(src_t[b][:], chunk_view(src_pad, c)).then_inc(edges_in[b], 16)
                sp.dma_start(dst_t[b][:], chunk_view(dst_pad, c)).then_inc(edges_in[b], 16)
                sp.dma_start(w_t[b][:], chunk_view(w_pad, c)).then_inc(edges_in[b], 16)

            def publish_steps(f):
                k = f.k
                sp.wait_ge(steps_ready, k + 1)
                sp.dma_start(step_tab[k], step_i[k][:, :]).then_inc(steps_out, 16)
                sp.wait_ge(steps_out, 16 * (k + 1))
                sp.dma_start(step_row[k][:, :], as_row(step_tab[k].rearrange("p a -> (p a)"))).then_inc(steps_in, 16)
                with sp.Fori(0, X) as e:
                    at = sp.value_load(zero_at[k][0:1, bass.ds(e, 1)], min_val=0, max_val=NSLOT - P)
                    sp.dma_start(slot_in[k][bass.ds(at, P), :], zeros[:, :]).then_inc(zeros_out, 16)
                sp.wait_ge(zeros_out, 16 * X * (k + 1))
                sp.wait_ge(spare_out, 32)
                tiles = TT if k else TE
                for b in range(2):
                    sp.wait_ge(tok_scattered[b], 32 * (-(-(tiles - b) // 2)))
                sp.wait_ge(steps_in, 16 * (k + 1))
                sp.wait_ge(biases_out, 32)

            def load_slots(f, s, r, g):
                u = r % f.ring
                at = sp.value_load(step_row[f.k][0:1, bass.ds(2 * s, 1)], min_val=0, max_val=NSLOT - P)
                e = sp.value_load(step_row[f.k][0:1, bass.ds(2 * s + 1, 1)], min_val=0, max_val=X - 1)
                wait(sp, f.xs_turned, s - f.ring + 1)
                sp.dma_start(f.xs[u], slot_in[f.k][bass.ds(at, P), :]).then_inc(f.xs_in[u], 16)
                wait(sp, f.y_kept, s - f.ring + 1)
                sp.dma_start(f.bias[u], bias_tab[bass.ds(e, 1), :].partition_broadcast(P)).then_inc(f.bias_in[u], 16)

            def load_both(c, b, i, m, q=None):
                load_edges(1, c, b)
                if isinstance(c, int) and c == EARLY - 1:
                    publish_steps(early)
                if q is not None:
                    for r in (2 * b, 2 * b + 1):
                        load_slots(early, 4 * q + r, r, q)
                wait_apart(sp, consts_ready, window_out, 16 * (CH + c))
                load_tokens(i, b, m, TR)

            sp.wait_ge(consts_ready, 1)
            for table in slot_in:
                sp.dma_start(table[X * CAP:NSLOT, :].rearrange("(a p) d -> p a d", p=P),
                             zeros[:, :].unsqueeze(1).to_broadcast([P, SPARE, D])).then_inc(spare_out, 16)

            sp.wait_ge(slow_known, 1)
            slow = sp.value_load(slow_i[0:1, 0:1], min_val=0, max_val=1)
            with sp.If(slow):
                for hop in range(2):
                    with sp.Fori(0, ETILES) as k:
                        e0 = k * P
                        sp.dma_start(s_src[:], src_pad[bass.ds(e0, P)].rearrange("(p a) -> p a", a=1)).then_inc(slow_loaded[hop][0], 16)
                        sp.dma_start(s_dst[:], dst_pad[bass.ds(e0, P)].rearrange("(p a) -> p a", a=1)).then_inc(slow_loaded[hop][1], 16)
                        sp.dma_start(s_w[:], w_pad[bass.ds(e0, P)].rearrange("(p a) -> p a", a=1)).then_inc(slow_loaded[hop][2], 16)
                        sp.dma_start(s_dst_row, as_row(dst_pad[bass.ds(e0, P)]).partition_broadcast(P)).then_inc(slow_loaded[hop][3], 16)
                        wait_apart(sp, consts_ready, slow_stored[hop], 16 * k + 16)
                load_tokens(0, 0, 0, TR)
                load_tokens(1, 1, 0, TR)
                with sp.Fori(1, TE // 2) as m:
                    load_tokens(2 * m, 0, m, TR)
                    load_tokens(2 * m + 1, 1, m, TR)
                publish_steps(early)
                steps_of_four(sp, early.steps, lambda s, r, g: load_slots(early, s, r, g))
                with sp.Fori(TE // 2, TT // 2) as m:
                    load_tokens(2 * m, 0, m, TR)
                    load_tokens(2 * m + 1, 1, m, TR)
            with sp.Else():
                load_edges(0, 0, 0)
                load_edges(0, 1, 1)
                with sp.Fori(1, CH // 2) as q:
                    load_edges(0, 2 * q, 0)
                    load_edges(0, 2 * q + 1, 1)
                with sp.Fori(0, LAG // 2) as q:
                    load_edges(1, 2 * q, 0)
                    load_edges(1, 2 * q + 1, 1)
                load_both(LAG, 0, 0, 0)
                load_both(LAG + 1, 1, 1, 0)
                def both_pair(q, g0=None, g1=None):
                    load_both(2 * q, 0, 2 * q - LAG, q - LAG // 2, g0)
                    load_both(2 * q + 1, 1, 2 * q + 1 - LAG, q - LAG // 2, g1)

                first = EARLY // 2
                with sp.Fori(LAG // 2 + 1, first - 1) as q:
                    both_pair(q)
                both_pair(first - 1)
                both_pair(first, 0, 0)
                with sp.Fori(first + 1, CH // 2 - 1) as q:
                    both_pair(q, q - first, q - first)
                both_pair(CH // 2 - 1, CH // 2 - 1 - first)
                sp.wait_ge(window_out, 16 * 2 * CH)
                load_tokens(TT - 3, 0, TT // 2 - 1, TR)
                load_tokens(TT - 2, 1, TT // 2 - 1, TR)
            load_tokens(TT - 1, 0, TT // 2, TLAST)

            publish_steps(late)

            def load_final(f, i, m, u, g, r):
                wait(sp, f.var, m - 1)
                sp.dma_start(f.t[u][0:r, :], t_rows[tile_rows(i, r), :]).then_inc(f.t_in[u // f.half], 16)
                wait(sp, f.stored[u // f.half], 16 * f.half * g)
                sp.dma_start(f.res[u][0:r, :], res_rows[tile_rows(i, r), :]).then_inc(f.res_in[u // f.half], 16)

            def late_step(s, r, g, finishing):
                load_slots(late, s, r, g)
                if finishing and r % 2:
                    i = 2 * g + r // 2
                    load_final(fin_early, i, i, r // 2, g, TR)

            sp.wait_ge(tok_res, TT)
            for b in range(2):
                sp.wait_ge(tok_out[b], 32 * (TT // 2 + 1 - b))
            late_steps(sp, late.steps, late_step)

            def load_group(m, g, h, n, r):
                for b in range(n):
                    load_final(fin_late, tile_of(m) + b, m, 4 * h + b, g, r)

            wait_all_out(sp)
            late_groups(sp, load_group)
            for b in range(2):
                sp.wait_ge(fin_early.stored[b], 16 * (TE // 2))
            sp.wait_ge(fin_late.stored[0], 16 * (2 * FOURS + LEFT))
            sp.wait_ge(fin_late.stored[1], 16 * (2 * FOURS + 1))

        @block.gpsimd
        def _(pool):
            exact = True
            pool.iota(col_id[:], [[1, P]], base=0, channel_multiplier=0, allow_small_or_imprecise_dtypes=exact).then_inc(iotas, 1)
            pool.iota(diff_id[:], [[-1, P]], base=0, channel_multiplier=1, allow_small_or_imprecise_dtypes=exact).then_inc(iotas, 1)
            pool.iota(row_id[:], [[0, 1]], base=0, channel_multiplier=1, allow_small_or_imprecise_dtypes=exact).then_inc(iotas, 1)
            pool.iota(need[:], [[TR, 64]], base=-TR * (LAG - 1), channel_multiplier=0, allow_small_or_imprecise_dtypes=exact).then_inc(iotas, 1)
            pool.iota(slot_base[:], [[CAP, X]], base=0, channel_multiplier=0, allow_small_or_imprecise_dtypes=exact).then_inc(iotas, 1)

            def scatter(i, b, m, r, k=1):
                wait_apart(pool, consts_ready, tok_placed, i + 1)
                for c in range(2):
                    pool.indirect_dma_start(slot_in[k][:, :], bass.IndirectOffsetOnAxis(ap=pos_t[b][0:r, c:c + 1], axis=0),
                                            t_t[0:r, b, :], None).then_inc(tok_scattered[b], 16)

            def gather_chunk(hop, c, b, q, scatters=None):
                wait_apart(pool, consts_ready, edges_in[b], 48 * (q + CH // 2 * hop) + 48)
                for j in range(CT):
                    if j % SR in GROUPS:
                        last = j - j % SR + GROUPS[j % SR]
                        wait_apart(pool, consts_ready, tile_summed, CT * (c + CH * hop) + last - SR + 1)
                    pool.indirect_dma_start(rows[:, j % SR, :], None, hop_in[hop][:, :],
                                            bass.IndirectOffsetOnAxis(ap=src_t[b][:, j:j + 1], axis=0)).then_inc(rows_in[j % SR], 16)
                    if j == SR - 1 and scatters:
                        scatters()

            pool.wait_ge(slow_known, 1)
            for b in range(2):
                pool.wait_ge(ln_stored[b], 16 * (LG // 2))
            pool.wait_ge(tail_stored, 16)
            slow = pool.value_load(slow_i[0:1, 0:1], min_val=0, max_val=1)
            with pool.If(slow):
                pool.wait_ge(slow_zeroed, 16 * 2 * (NR // P))
                for hop in range(2):
                    with pool.Fori(0, ETILES) as k:
                        wait_apart(pool, consts_ready, slow_loaded[hop][0], 16 * k + 16)
                        pool.indirect_dma_start(s_rows, None, hop_in[hop][:, :],
                                                bass.IndirectOffsetOnAxis(ap=s_src[:, 0:1], axis=0)).then_inc(slow_rows[hop][0], 16)
                        wait_apart(pool, consts_ready, slow_loaded[hop][1], 16 * k + 16)
                        pool.indirect_dma_start(s_old, None, h_rows[hop][0:N, :],
                                                bass.IndirectOffsetOnAxis(ap=s_dst[:, 0:1], axis=0)).then_inc(slow_rows[hop][1], 16)
                        wait_apart(pool, consts_ready, slow_new, k + 1 + ETILES * hop)
                        pool.indirect_dma_start(h_rows[hop][0:N, :], bass.IndirectOffsetOnAxis(ap=s_put[:, 0:1], axis=0),
                                                s_new, None, bounds_check=N - 1, oob_is_err=False).then_inc(slow_stored[hop], 16)
                        wait_apart(pool, consts_ready, slow_stored[hop], 16 * k + 16)
                        pool.engine_nop()
                scatter(0, 0, 0, TR, 0)
                scatter(1, 1, 0, TR, 0)
                with pool.Fori(1, TE // 2) as m:
                    scatter(2 * m, 0, m, TR, 0)
                    scatter(2 * m + 1, 1, m, TR, 0)
                with pool.Fori(TE // 2, TT // 2) as m:
                    scatter(2 * m, 0, m, TR)
                    scatter(2 * m + 1, 1, m, TR)
            with pool.Else():
                gather_chunk(0, 0, 0, 0)
                gather_chunk(0, 1, 1, 0)
                with pool.Fori(1, CH // 2) as q:
                    gather_chunk(0, 2 * q, 0, q)
                    gather_chunk(0, 2 * q + 1, 1, q)
                pool.wait_ge(window_out, 16 * CH)
                with pool.Fori(0, LAG // 2) as q:
                    gather_chunk(1, 2 * q, 0, q)
                    gather_chunk(1, 2 * q + 1, 1, q)
                q0 = LAG // 2
                gather_chunk(1, LAG, 0, q0)
                gather_chunk(1, LAG + 1, 1, q0, lambda: scatter(0, 0, 0, TR, 0))

                def gather_pair(q, k0, k1):
                    gather_chunk(1, 2 * q, 0, q, lambda: scatter(2 * q - LAG - 1, 1, q - q0 - 1, TR, k0))
                    gather_chunk(1, 2 * q + 1, 1, q, lambda: scatter(2 * q - LAG, 0, q - q0, TR, k1))

                with pool.Fori(q0 + 1, EARLY // 2 - 1) as q:
                    gather_pair(q, 0, 0)
                gather_pair(EARLY // 2 - 1, 0, 1)
                with pool.Fori(EARLY // 2, CH // 2) as q:
                    gather_pair(q, 1, 1)
                scatter(TT - 4, 1, TT // 2 - 2, TR)
                scatter(TT - 3, 0, TT // 2 - 1, TR)
                scatter(TT - 2, 1, TT // 2 - 1, TR)
            scatter(TT - 1, 0, TT // 2, TLAST)

            def gather_final(f, table, n, m, u, r):
                wait_apart(pool, consts_ready, f.ready, m - 1)
                wait_apart(pool, consts_ready, f.pos_staged, n + 1)
                for k, y in ((0, f.y_a), (1, f.y_b)):
                    pool.indirect_dma_start(y[u][0:r, :], None, table,
                                            bass.IndirectOffsetOnAxis(ap=f.pos[u][0:r, k:k + 1], axis=0)).then_inc(f.y_in[u // f.half], 16)

            pool.wait_ge(early.y_out[0], 16 * early.steps)
            pool.wait_ge(tok_turned, TT)
            early_rows = slot_out[0:early.steps * P, :]
            gather_final(fin_early, early_rows, 0, 0, 0, TR)
            gather_final(fin_early, early_rows, 1, 1, 1, TR)
            with pool.Fori(1, TE // 2) as g:
                gather_final(fin_early, early_rows, 2 * g, 2 * g, 0, TR)
                gather_final(fin_early, early_rows, 2 * g + 1, 2 * g + 1, 1, TR)

            def gather_group(m, g, h, n, r):
                for b in range(n):
                    gather_final(fin_late, slot_out[:, :], tile_of(m) - TE + b, m, 4 * h + b, r)

            wait_all_out(pool)
            late_groups(pool, gather_group)

        @block.scalar
        def _(act):
            for dest, view in ((gnn_w_sb[:], gnn_w_v), (gate_w_sb[:], gate_w_v),
                               (bias_sb[:], as_row(gnn_bias).partition_broadcast(P)),
                               (gamma_sb[:], as_row(gamma).partition_broadcast(P)),
                               (beta_sb[:], as_row(beta).partition_broadcast(P)),
                               (gate_b_sb[:], as_row(gate_b).partition_broadcast(P))):
                act.dma_start(dest, view).then_inc(params_in, 16)

            def ln_step(g, b, m, source, target, r, n):
                act.wait_ge(ln_var, g + 1)
                act.activation(ln_small[b][0:r, 1, 0:n], ln_small[b][0:r, 0, 0:n], ACT.Sqrt).then_inc(ln_sd, 1)
                wait(act, ln_stored[b], 16 * m)
                act.wait_ge(ln_scaled, g + 1)
                for k in range(n):
                    last = act.activation(target[0:r, k, :], source[0:r, k, :], ACT.Identity,
                                          scale=ln_small[b][0:r, 4, k:k + 1], bias=ln_small[b][0:r, 5, k:k + 1])
                last.then_inc(ln_applied, 1)
                act.wait_ge(ln_applied, g + 1)

            def ln_group(g, b, m):
                ln_step(g, b, m, ln_in[b], ln_out[b], P, LR)
                act.dma_start(xn_main[:, bass.ds(g * LR, LR), :], ln_out[b]).then_inc(ln_stored[b], 16)

            ln_group(0, 0, 0)
            ln_group(1, 1, 0)
            with act.Fori(1, LG // 2) as m:
                ln_group(2 * m, 0, m)
                ln_group(2 * m + 1, 1, m)
            ln_step(LG, 0, 0, tail_in, tail_out, LTAIL, 1)
            act.dma_start(xn_rows[LMAIN:N, :], tail_out[0:LTAIL, 0, :]).then_inc(tail_stored, 16)
            act.wait_ge(base_spread, 1)
            act.copy(base[:, :], small[:, 0:64]).then_inc(base_kept, 1)

            act.wait_ge(slow_known, 1)
            for b in range(2):
                act.wait_ge(ln_stored[b], 16 * (LG // 2))
            act.wait_ge(tail_stored, 16)

            def load_expert(e):
                act.dma_start(w1_sb[:, bass.ds(e * DH, DH), :], w1[bass.ds(e, 1)].rearrange("e (k p) f -> p (e k) f", p=P)).then_inc(weights_in, 16)
                act.dma_start(w2_sb[:, bass.ds(e * FH, FH), :], w2[bass.ds(e, 1)].rearrange("e (k p) d -> p (e k) d", p=P)).then_inc(weights_in, 16)

            def tok_keep_turned(i, b, m, r):
                act.wait_ge(tok_turned, i + 1)
                wait(act, tok_projected, i)
                act.copy(hT_t[:, :, 0:r], turn[:, :].rearrange("p (k t) -> p k t", t=P)[:, :, 0:r]).then_inc(tok_turned_kept, 1)

            def tok_root(i, b, m, r):
                act.wait_ge(tok_var, i + 1)
                act.activation(tok_small[0:r, 1, 0:1], tok_small[0:r, 0, 0:1], ACT.Sqrt).then_inc(tok_sd, 1)

            def tok_store(i, b, m, r):
                act.wait_ge(tok_t, i + 1)
                act.dma_start(res_rows[tile_rows(i, r), :], res_t[0:r, b, :]).then_inc(tok_out[b], 16)
                act.dma_start(t_rows[tile_rows(i, r), :], t_t[0:r, b, :]).then_inc(tok_out[b], 16)
                act.wait_ge(t_turned, i + 1)
                wait(act, tok_gated, i)
                act.copy(tT_t[:, :, 0:r], turn2[:, 0:DH * P].rearrange("p (k t) -> p k t", t=P)[:, :, 0:r]).then_inc(t_turned_kept, 1)

            def tok_weigh(i, b, m, r):
                act.wait_ge(tok_chosen, i + 1)
                act.activation(gap_e[0:r, :], gap[0:r, :], ACT.Exp).then_inc(tok_exp, 1)

            def tokens(i, b, m, r):
                for step in (tok_keep_turned, tok_root, tok_store, tok_weigh):
                    step(i, b, m, r)

            def tokens_but_weigh(i, b, m, r):
                for step in (tok_keep_turned, tok_root, tok_store):
                    step(i, b, m, r)

            def keep_xs(f, s, r, g):
                act.wait_ge(f.xs_turned, s + 1)
                wait(act, f.up_done, s - f.depth + 1)
                act.copy(f.xsT[r % f.depth], f.xs_out.rearrange("p (k t) -> p k t", t=P)).then_inc(f.xs_kept, 1)

            def keep_h(f, s, r, g):
                act.wait_ge(f.h_turned, s + 1)
                wait(act, f.down_done, s - f.depth + 1)
                act.activation(f.hT[r % f.depth], f.h_out.rearrange("p (k t) -> p k t", t=P), ACT.Relu).then_inc(f.h_kept, 1)

            def store_y(f, s, r, g):
                b = r % f.depth
                act.wait_ge(f.y_kept, s + 1)
                act.dma_start(slot_out[bass.ds((s + f.k * STEPS[0]) * P, P), :], f.ys[b]).then_inc(f.y_out[b], 16)

            def early_step(s, r, g):
                for part_of_step in (keep_xs, keep_h, store_y):
                    part_of_step(early, s, r, g)

            def keep_window(hop, c, b):
                n = c + CH * hop
                act.wait_ge(window_summed, n + 1)
                wait(act, window_out, 16 * (n - 1))
                act.copy(kept[:, b, :], win[b][:, 0:D]).then_inc(window_kept, 1)
                at = act.value_load(base_row[0:1, bass.ds(c, 1)], min_val=0, max_val=N - 1)
                wait(act, window_out, 16 * n)
                act.wait_ge(window_kept, n + 1)
                act.dma_start(h_rows[hop][bass.ds(at, P), :], kept[:, b, :]).then_inc(window_out, 16)

            slow = act.value_load(slow_i[0:1, 0:1], min_val=0, max_val=1)
            with act.If(slow):
                with act.Fori(0, X) as e:
                    load_expert(e)
                with act.Fori(0, NR // P) as k:
                    for table in h_rows:
                        act.dma_start(table[bass.ds(k * P, P), :], zeros[:, :]).then_inc(slow_zeroed, 16)
                tokens(0, 0, 0, TR)
                tokens(1, 1, 0, TR)
                with act.Fori(1, TE // 2) as m:
                    tokens(2 * m, 0, m, TR)
                    tokens(2 * m + 1, 1, m, TR)
                steps_of_four(act, early.steps, early_step)
                with act.Fori(TE // 2, TT // 2) as m:
                    tokens(2 * m, 0, m, TR)
                    tokens(2 * m + 1, 1, m, TR)
            with act.Else():
                keep_window(0, 0, 0)
                keep_window(0, 1, 1)
                with act.Fori(1, X + 1) as q:
                    keep_window(0, 2 * q, 0)
                    keep_window(0, 2 * q + 1, 1)
                    load_expert(q - 1)
                with act.Fori(X + 1, CH // 2) as q:
                    keep_window(0, 2 * q, 0)
                    keep_window(0, 2 * q + 1, 1)
                with act.Fori(0, LAG // 2) as q:
                    keep_window(1, 2 * q, 0)
                    keep_window(1, 2 * q + 1, 1)
                tokens_but_weigh(0, 0, 0, TR)
                keep_window(1, LAG, 0)
                tok_weigh(0, 0, 0, TR)
                tokens_but_weigh(1, 1, 0, TR)
                keep_window(1, LAG + 1, 1)

                def full_chunk(q, b, g=None):
                    token_tile = (2 * q + b - LAG, b, q - LAG // 2, TR)
                    tok_weigh(2 * q + b - LAG - 1, 1 - b, None, TR)
                    if g is None:
                        tokens_but_weigh(*token_tile)
                    else:
                        s0, s1 = ((early, 4 * g + r, r, g) for r in (2 * b, 2 * b + 1))
                        keep_xs(*s0)
                        keep_h(*s0)
                        tok_keep_turned(*token_tile)
                        store_y(*s0)
                        keep_xs(*s1)
                        tok_root(*token_tile)
                        tok_store(*token_tile)
                        keep_h(*s1)
                        store_y(*s1)
                    keep_window(1, 2 * q + b, b)

                first = EARLY // 2
                with act.Fori(LAG // 2 + 1, first) as q:
                    full_chunk(q, 0)
                    full_chunk(q, 1)
                full_chunk(first, 0, 0)
                full_chunk(first, 1, 0)
                with act.Fori(first + 1, CH // 2 - 1) as q:
                    full_chunk(q, 0, q - first)
                    full_chunk(q, 1, q - first)
                full_chunk(CH // 2 - 1, 0, CH // 2 - 1 - first)
                full_chunk(CH // 2 - 1, 1)
                tok_weigh(TT - 4, 1, None, TR)
                tokens(TT - 3, 0, TT // 2 - 1, TR)
                tokens(TT - 2, 1, TT // 2 - 1, TR)
            tokens(TT - 1, 0, TT // 2, TLAST)

            def final_root(f, m, n, r):
                act.wait_ge(f.var, m + 1)
                act.activation(tok_small[0:r, 1, 0:n], tok_small[0:r, 0, 0:n], ACT.Sqrt).then_inc(f.sd, 1)

            def final_store(f, m, i, us, r):
                act.wait_ge(f.ready, m + 1)
                for b, u in enumerate(us):
                    act.dma_start(out[tile_rows(i + b, r), :], f.res[u][0:r, :]).then_inc(f.stored[u // f.half], 16)

            def late_step(s, r, g, finishing):
                i = 2 * g + r // 2
                keep_h(late, s, r, g)
                if finishing and r % 2 == 0 and not (isinstance(s, int) and s == 0):
                    final_store(fin_early, i - 1, i - 1, [1 - r // 2], TR)
                if finishing and r % 2:
                    final_root(fin_early, i, 1, TR)
                if not (isinstance(s, int) and s >= late.steps - 2):
                    keep_xs(late, s + 2, (r + 2) % 4, g + (r + 2) // 4)
                store_y(late, s, r, g)

            keep_xs(late, 0, 0, 0)
            keep_xs(late, 1, 1, 0)
            late_steps(act, late.steps, late_step)
            final_store(fin_early, TE - 1, TE - 1, [1], TR)

            def finish_group(m, g, h, n, r):
                final_root(fin_late, m, n, r)
                final_store(fin_late, m, tile_of(m), [4 * h + b for b in range(n)], r)

            late_groups(act, finish_group)

        @block.vector
        def _(dve):
            dve.memset(pad_i[:, 0:P], 0).then_inc(fills, 1)
            dve.memset(pad_i[:, P:3 * P], N - 1).then_inc(fills, 1)
            dve.memset(base_row[:, 0:1], 0).then_inc(fills, 1)
            dve.memset(ones[:], 1.0)
            dve.memset(zeros[:], 0.0)
            dve.memset(kept[:], 0.0)
            dve.memset(routed[:], 0.0)
            dve.memset(pos_all[:], 0.0)
            dve.memset(exp_all[:], 0.0)
            dve.memset(base_rowf[:, CH:64], N - 1.0)
            dve.wait_ge(iotas, 5)
            dve.tensor_scalar(ident[:], diff_id[:], 0.0, None, ALU.is_equal)
            dve.tensor_scalar(tri_eye[:, X:2 * X], diff_id[0:X, 0:X], 0.0, None, ALU.is_equal)
            dve.tensor_scalar(tri_eye[:, 0:X], diff_id[0:X, 0:X], 0.0, None, ALU.is_le)
            dve.tensor_scalar(below[:], diff_id[:], 0.0, None, ALU.is_lt)
            dve.drain()
            dve.memset(gap_d[:], 0.0).then_inc(consts_ready, 1)

            def scale_of(small_, mv, r, c0, c1):
                v, sd, a, t, s, z = (small_[0:r, k, c0:c1] for k in range(6))
                dve.reciprocal(a, sd)
                dve.drain()
                dve.tensor_tensor(t, a, a, ALU.mult)
                dve.drain()
                dve.tensor_tensor(t, t, v, ALU.mult)
                dve.drain()
                dve.tensor_scalar(t, t, -0.5, 1.5, ALU.mult, ALU.add)
                dve.drain()
                dve.tensor_tensor(s, a, t, ALU.mult)
                dve.drain()
                return dve.scalar_tensor_tensor(out=z, in0=mv[0:r, c0:c1, 0], scalar=-1.0, in1=s, op0=ALU.mult, op1=ALU.mult)

            def ln_step(g, b, source, r, n):
                wait(dve, ln_applied, g - 1)
                for k in range(n):
                    dve.bn_stats(ln_stats[0:r, k, :], source[0:r, k, :])
                dve.drain()
                for k in range(n):
                    dve.bn_aggr(ln_mv[b][0:r, k, :], ln_stats[0:r, k, :])
                dve.drain()
                dve.tensor_scalar(ln_small[b][0:r, 0, 0:n], ln_mv[b][0:r, 0:n, 1], EPS, None, ALU.add).then_inc(ln_var, 1)
                dve.wait_ge(ln_sd, g + 1)
                scale_of(ln_small[b], ln_mv[b], r, 0, n).then_inc(ln_scaled, 1)

            dve.wait_ge(ln_loaded[0], 16)
            ln_step(0, 0, ln_in[0], P, LR)
            dve.wait_ge(ln_loaded[1], 16)
            ln_step(1, 1, ln_in[1], P, LR)
            with dve.Fori(1, LG // 2) as m:
                for b in range(2):
                    dve.wait_ge(ln_loaded[b], 16 * m + 16)
                    ln_step(2 * m + b, b, ln_in[b], P, LR)
            dve.wait_ge(tail_loaded, 16)
            ln_step(LG, 0, tail_in, LTAIL, 1)

            dve.wait_ge(base_in, 16)
            dve.tensor_copy(base_rowf[:, 0:CH], base_row[:, 0:CH]).then_inc(base_ready, 1)
            dve.wait_ge(dst_in, 32)
            dve.tensor_tensor(unsorted, dst_all[:, 1:PK + 1], dst_all[:, 0:PK], ALU.is_lt)
            dve.drain()
            dve.tensor_reduce(bad[:, 0:1], unsorted, AX_X, ALU.add)
            dve.wait_ge(base_kept, 1)
            dve.tensor_tensor(delta[:, 1:CH + 1], base[:, 1:CH + 1], base[:, 0:CH], ALU.subtract)
            dve.tensor_tensor(need[:, LAG:CH], base[:, LAG:CH], need[:, LAG:CH], ALU.is_lt)
            dve.drain()
            dve.tensor_scalar(delta[:, CH + 1:64], delta[:, 1:2], 0.0, None, ALU.mult)
            dve.tensor_reduce(bad[:, 1:2], need[:, LAG:CH], AX_X, ALU.add)
            dve.tensor_reduce(bad[:, 2:3], delta[:, 1:CH + 1], AX_X, ALU.max)
            dve.drain()
            dve.memset(delta[:, 0:1], FAR)
            dve.tensor_scalar(bad[:, 2:3], bad[:, 2:3], P - 1.0, None, ALU.is_gt)
            dve.drain()
            dve.tensor_reduce(bad_sum[:], bad[:], AX_X, ALU.add).then_inc(bad_ready, 1)
            dve.wait_ge(bad_summed, 1)
            dve.tensor_scalar(slow_i[:], small[:, 64:65], 0.0, None, ALU.is_gt).then_inc(slow_known, 1)

            def tok_residual(i, b, m, r):
                dve.wait_ge(tok_in[b], 48 * m + 48)
                wait(dve, tok_out[b], 32 * m)
                dve.tensor_tensor(mid_t[0:r, :], x_t[0:r, b, :], bias_sb[0:r, :], ALU.add)
                dve.drain()
                dve.wait_ge(tok_projected, i + 1)
                dve.tensor_tensor(mid_t[0:r, :], mid_t[0:r, :], proj[0][0:r, 0:D], ALU.add)
                dve.drain()
                dve.tensor_tensor(res_t[0:r, b, :], mid_t[0:r, :], beta_sb[0:r, :], ALU.add).then_inc(tok_res, 1)
                dve.bn_stats(tok_stats[0:r, 0, :], mid_t[0:r, :])
                dve.drain()
                dve.bn_aggr(tok_mv[0:r, 0, :], tok_stats[0:r, 0, :])
                dve.drain()
                dve.tensor_scalar(tok_small[0:r, 0, 0:1], tok_mv[0:r, 0:1, 1], EPS, None, ALU.add).then_inc(tok_var, 1)

            def tok_norm(i, b, m, r):
                dve.wait_ge(tok_sd, i + 1)
                scale_of(tok_small, tok_mv, r, 0, 1)
                dve.drain()
                wait(dve, tok_scattered[b], 32 * m)
                dve.tensor_scalar(t_t[0:r, b, :], mid_t[0:r, :], tok_mv[0:r, 0, 0:1], tok_small[0:r, 4, 0:1],
                                  ALU.subtract, ALU.mult).then_inc(tok_t, 1)

            def tok_choose(i, b, m, r):
                dve.wait_ge(tok_gated, i + 1)
                dve.tensor_tensor(logits[0:r, :], small2[0:r, 0:X], gate_b_sb[0:r, :], ALU.add)
                dve.drain()
                dve.max(top_v[0:r, :], logits[0:r, :])
                dve.drain()
                dve.max_index(top_i[0:r, :], top_v[0:r, :], logits[0:r, :])
                dve.tensor_tensor(gap[0:r, :], top_v[0:r, 1:2], top_v[0:r, 0:1], ALU.subtract)
                dve.drain()
                dve.tensor_copy(top_f[0:r, :], top_i[0:r, 0:2])
                dve.drain()
                for k in range(2):
                    dve.tensor_scalar(chosen[0:r, k, :], col_id[0:r, 0:X], top_f[0:r, k:k + 1], None, ALU.is_equal)
                dve.drain()
                dve.tensor_tensor(both[0:r, :], chosen[0:r, 0, :], chosen[0:r, 1, :], ALU.add).then_inc(tok_chosen, 1)

            def tok_place(i, b, m, r):
                dve.wait_ge(tok_exp, i + 1)
                dve.tensor_scalar(gap_d[0:r, :], gap_e[0:r, :], 1.0, None, ALU.add)
                dve.drain()
                dve.reciprocal(gap_r[0:r, :], gap_d[0:r, :])
                dve.drain()
                dve.tensor_tensor(wts_all[0:r, bass.ds(2 * i + 1, 1)], gap_e[0:r, :], gap_r[0:r, :], ALU.mult)
                dve.tensor_copy(wts_all[0:r, bass.ds(2 * i, 1)], gap_r[0:r, :])
                dve.wait_ge(tok_ranked, i + 1)
                dve.tensor_tensor(place[0:r, :], small2[0:r, X:2 * X], slot_base[0:r, :], ALU.add)
                dve.tensor_tensor(routed[0:r, :], routed[0:r, :], both[0:r, :], ALU.add)
                dve.drain()
                for k in range(2):
                    dve.tensor_tensor(placed[0:r, k, :], chosen[0:r, k, :], place[0:r, :], ALU.mult)
                dve.drain()
                dve.tensor_reduce(pos_f[0:r, :], placed[0:r, :, :], AX_X, ALU.add)
                dve.drain()
                dve.tensor_copy(pos_all[0:r, bass.ds(2 * i, 2)], pos_f[0:r, :])
                dve.tensor_copy(exp_all[0:r, bass.ds(2 * i, 2)], top_f[0:r, :])
                dve.tensor_copy(pos_t[b][0:r, :], pos_f[0:r, :]).then_inc(tok_placed, 1)

            def tokens(i, b, m, r):
                for step in (tok_residual, tok_norm, tok_choose, tok_place):
                    step(i, b, m, r)

            def signal_counted(k):
                dve.drain()
                dve.memset(gap_d[:], 0.0).then_inc(counted, 1)

            def tiles_of(target, counts):
                dve.tensor_scalar(target, counts, 1.0 / P, (P - 1.0) / P - 0.498, ALU.mult, ALU.add)
                dve.drain()
                dve.tensor_scalar(target, target, ROUND, None, ALU.add)
                dve.drain()
                return dve.tensor_scalar(target, target, -ROUND, None, ALU.add)

            def find_tiles(k):
                dve.wait_ge(counted, 2 * k + 2)
                dve.tensor_tensor(zero_f[:], small[:, P:P + X], slot_base[:], ALU.add)
                tiles_of(tiles_T[:, :], small[0:X, 0:P]).then_inc(tiles_ready, 1)
                if k == 0:
                    dve.memset(routed[:], 0.0)
                dve.drain()
                dve.tensor_copy(zero_at[k][:], zero_f[:])

            def find_steps(k):
                dve.wait_ge(cumulated, k + 1)
                dve.tensor_copy(tiles_C[:], small[:, 2 * P:2 * P + 2 * X])
                dve.drain()
                dve.tensor_scalar(step_cmp[:], tiles_C[:, 0:X], row_id[:], None, ALU.is_le)
                dve.drain()
                dve.tensor_tensor(step_cum[:], step_cmp[:], tiles_C[:, X:2 * X], ALU.mult)
                dve.tensor_reduce(step_f[:, 0:1], step_cmp[:], AX_X, ALU.add)
                dve.drain()
                dve.tensor_reduce(step_f[:, 1:2], step_cum[:], AX_X, ALU.add)
                dve.drain()
                dve.tensor_tensor(step_f[:, 2:3], row_id[:], step_f[:, 1:2], ALU.subtract)
                dve.tensor_scalar(step_f[:, 3:4], step_f[:, 0:1], float(CAP), None, ALU.mult)
                dve.drain()
                dve.scalar_tensor_tensor(out=step_f[:, 3:4], in0=step_f[:, 2:3], scalar=float(P), in1=step_f[:, 3:4], op0=ALU.mult, op1=ALU.add)
                dve.tensor_scalar(step_f[:, 0:1], step_f[:, 0:1], X - 1.0, None, ALU.min)
                dve.drain()
                dve.tensor_copy(step_i[k][:, 0:1], step_f[:, 3:4])
                dve.tensor_copy(step_i[k][:, 1:2], step_f[:, 0:1])
                dve.drain()
                dve.memset(gap_d[:], 0.0).then_inc(steps_ready, 1)

            def fix_places(k):
                dve.tensor_tensor(slot_fix[:], tiles_C[:, 0:X], tiles_C[:, X:2 * X], ALU.subtract)
                dve.drain()
                dve.tensor_scalar(slot_fix[:], slot_fix[:], float(P), float(P * STEPS[0] * k), ALU.mult, ALU.add)
                dve.drain()
                dve.tensor_tensor(slot_fix[:], slot_fix[:], slot_base[:], ALU.subtract)
                cols = slice(2 * TE, 2 * TT) if k else slice(0, 2 * TE)
                for e in range(X):
                    dve.drain()
                    dve.tensor_scalar(pos_fix[:, cols], exp_all[:, cols], float(e), slot_fix[:, e:e + 1], ALU.is_equal, ALU.mult)
                    dve.drain()
                    dve.tensor_tensor(pos_all[:, cols], pos_all[:, cols], pos_fix[:, cols], ALU.add)

            table_parts = (signal_counted, find_tiles, find_steps, fix_places)

            def keep_up(f, s, r, g):
                b, u = r % f.depth, r % f.ring
                dve.wait_ge(f.bias_in[u], 16 * uses(r, g, f.ring) + 16)
                wait(dve, f.h_turned, s - f.depth + 1)
                dve.wait_ge(f.up_done, s + 1)
                dve.tensor_tensor(f.hb[b], f.up_out[b], f.bias[u][:, 0:F], ALU.add).then_inc(f.up_kept, 1)

            def keep_down(f, s, r, g):
                b, u = r % f.depth, r % f.ring
                wait(dve, f.y_out[b], 16 * uses(r, g, f.depth))
                dve.wait_ge(f.down_done, s + 1)
                dve.tensor_tensor(f.ys[b], f.down_out[b], f.bias[u][:, F:F + D], ALU.add).then_inc(f.y_kept, 1)

            def early_step(s, r, g):
                keep_up(early, s, r, g)
                keep_down(early, s, r, g)

            def select_chunk(hop, c, b, q, steps=None):
                n = c + CH * hop
                dve.wait_ge(edges_in[b], 48 * (q + CH // 2 * hop) + 48)
                dve.tensor_scalar(dst_rel[b][:], dst_t[b][:], base[:, bass.ds(c, 1)], None, ALU.subtract)
                wait(dve, window_summed, n - 1)
                dve.tensor_scalar(shift[:, b, :], diff_id[:], delta[:, bass.ds(c, 1)], None, ALU.is_equal).then_inc(shift_built, 1)
                dve.drain()
                for j in range(CT):
                    wait(dve, tile_summed, CT * n + j - SR + 1)
                    dve.tensor_scalar(sel[:, j % SR, :], col_id[:], dst_rel[b][:, j:j + 1], w_t[b][:, j:j + 1],
                                      ALU.is_equal, ALU.mult).then_inc(sel_built, 1)
                    if steps and j in steps:
                        steps[j]()

            def with_tokens(i, b, m):
                at = {j: (lambda f=f: f(i, b, m, TR)) for j, f in ((15, tok_residual), (17, tok_norm))}
                if not (isinstance(i, int) and i == 0):
                    at.update({j: (lambda f=f: f(i - 1, 1 - b, None, TR)) for j, f in ((1, tok_choose), (8, tok_place))})
                return at

            def with_steps(g, b):
                at = {}
                for n, r in enumerate((2 * b, 2 * b + 1)):
                    at[SR * n + 6 - n] = lambda r=r: keep_up(early, 4 * g + r, r, g)
                    at[SR * n + 12] = lambda r=r: keep_down(early, 4 * g + r, r, g)
                return at

            def with_table():
                return {j: (lambda f=f: f(0)) for j, f in zip((9, 13, 16, 19), table_parts)}

            dve.wait_ge(slow_known, 1)
            slow = dve.value_load(slow_i[0:1, 0:1], min_val=0, max_val=1)
            with dve.If(slow):
                for hop in range(2):
                    with dve.Fori(0, ETILES) as k:
                        for loaded in slow_loaded[hop][1:]:
                            dve.wait_ge(loaded, 16 * k + 16)
                        dve.tensor_copy(s_dstf[:], s_dst[:])
                        dve.tensor_copy(s_dst_rowf, s_dst_row)
                        dve.drain()
                        dve.tensor_scalar(s_same_w, s_dst_rowf, s_dstf[:], s_w[:], ALU.is_equal, ALU.mult)
                        dve.scalar_tensor_tensor(out=s_same_below, in0=s_dst_rowf, scalar=s_dstf[:, 0:1], in1=below[:],
                                                 op0=ALU.is_equal, op1=ALU.mult)
                        dve.drain()
                        dve.engine_nop().then_inc(slow_sel, 1)
                        dve.wait_ge(slow_rows[hop][1], 16 * k + 16)
                        dve.wait_ge(slow_summed, k + 1 + ETILES * hop)
                        dve.tensor_tensor(s_new, s_old, win[0][:, 0:D], ALU.add)
                        dve.tensor_scalar(s_repf[:], small[:, 0:1], 0.0, OUT, ALU.is_gt, ALU.mult)
                        dve.drain()
                        dve.tensor_tensor(s_rep[:], s_repf[:], s_dstf[:], ALU.add)
                        dve.drain()
                        dve.tensor_copy(s_put[:], s_rep[:]).then_inc(slow_new, 1)
                tokens(0, 0, 0, TR)
                tokens(1, 1, 0, TR)
                with dve.Fori(1, TE // 2) as m:
                    tokens(2 * m, 0, m, TR)
                    tokens(2 * m + 1, 1, m, TR)
                for part_of_table in table_parts:
                    part_of_table(0)
                steps_of_four(dve, early.steps, early_step)
                with dve.Fori(TE // 2, TT // 2) as m:
                    tokens(2 * m, 0, m, TR)
                    tokens(2 * m + 1, 1, m, TR)
            with dve.Else():
                select_chunk(0, 0, 0, 0)
                select_chunk(0, 1, 1, 0)
                with dve.Fori(1, CH // 2) as q:
                    select_chunk(0, 2 * q, 0, q)
                    select_chunk(0, 2 * q + 1, 1, q)
                with dve.Fori(0, LAG // 2) as q:
                    select_chunk(1, 2 * q, 0, q)
                    select_chunk(1, 2 * q + 1, 1, q)
                q0 = LAG // 2
                select_chunk(1, LAG, 0, q0, with_tokens(0, 0, 0))
                select_chunk(1, LAG + 1, 1, q0, with_tokens(1, 1, 0))

                def full_chunk(q, b, others):
                    select_chunk(1, 2 * q + b, b, q, {**with_tokens(2 * q + b - LAG, b, q - q0), **others})

                first = EARLY // 2
                with dve.Fori(q0 + 1, first - 1) as q:
                    full_chunk(q, 0, {})
                    full_chunk(q, 1, {})
                full_chunk(first - 1, 0, with_table())
                full_chunk(first - 1, 1, {})
                full_chunk(first, 0, with_steps(0, 0))
                full_chunk(first, 1, with_steps(0, 1))
                with dve.Fori(first + 1, CH // 2 - 1) as q:
                    full_chunk(q, 0, with_steps(q - first, 0))
                    full_chunk(q, 1, with_steps(q - first, 1))
                full_chunk(CH // 2 - 1, 0, with_steps(CH // 2 - 1 - first, 0))
                full_chunk(CH // 2 - 1, 1, {})
                tok_choose(TT - 4, 1, None, TR)
                tok_place(TT - 4, 1, None, TR)
                tokens(TT - 3, 0, TT // 2 - 1, TR)
                tokens(TT - 2, 1, TT // 2 - 1, TR)
            tokens(TT - 1, 0, TT // 2, TLAST)

            for part_of_table in table_parts:
                part_of_table(1)

            def stage_places(f, i, us):
                for b, u in enumerate(us):
                    dve.tensor_copy(f.pos[u][:], pos_all[:, bass.ds(2 * (i + b), 2)]).then_inc(f.pos_staged, 1)

            def final_mix(f, i, us, g, r):
                n, h = len(us), us[0] // f.half
                dve.wait_ge(f.t_in[h], 16 * (f.half * g + n))
                dve.wait_ge(f.y_in[h], 32 * (f.half * g + n))
                for b, u in enumerate(us):
                    dve.scalar_tensor_tensor(out=f.y_a[u][0:r, :], in0=f.y_a[u][0:r, :], scalar=wts_all[0:r, bass.ds(2 * (i + b), 1)],
                                             in1=f.t[u][0:r, :], op0=ALU.mult, op1=ALU.add)
                dve.drain()
                for b, u in enumerate(us):
                    dve.scalar_tensor_tensor(out=f.y_b[u][0:r, :], in0=f.y_b[u][0:r, :], scalar=wts_all[0:r, bass.ds(2 * (i + b) + 1, 1)],
                                             in1=f.y_a[u][0:r, :], op0=ALU.mult, op1=ALU.add)
                dve.drain()
                for b, u in enumerate(us):
                    dve.bn_stats(tok_stats[0:r, b, :], f.y_b[u][0:r, :])
                dve.drain()
                for b in range(n):
                    dve.bn_aggr(tok_mv[0:r, b, :], tok_stats[0:r, b, :])
                dve.drain()
                dve.tensor_scalar(tok_small[0:r, 0, 0:n], tok_mv[0:r, 0:n, 1], EPS, None, ALU.add).then_inc(f.var, 1)
                for b, u in enumerate(us):
                    dve.scalar_tensor_tensor(out=f.y_a[u][0:r, :], in0=f.y_b[u][0:r, :], scalar=tok_mv[0:r, b, 0:1],
                                             in1=gamma_sb[0:r, :], op0=ALU.subtract, op1=ALU.mult)

            def final_add(f, m, us, g, r):
                dve.wait_ge(f.sd, m + 1)
                scale_of(tok_small, tok_mv, r, 0, len(us))
                dve.drain()
                dve.wait_ge(f.res_in[us[0] // f.half], 16 * (f.half * g + len(us)))
                for b, u in enumerate(us):
                    last = dve.scalar_tensor_tensor(out=f.res[u][0:r, :], in0=f.y_a[u][0:r, :], scalar=tok_small[0:r, 4, b:b + 1],
                                                    in1=f.res[u][0:r, :], op0=ALU.mult, op1=ALU.add)
                last.then_inc(f.ready, 1)

            def late_step(s, r, g, finishing):
                if not (isinstance(s, int) and s == late.steps - 1):
                    keep_up(late, s + 1, (r + 1) % 4, g + (r + 1) // 4)
                keep_down(late, s, r, g)
                i, us = 2 * g + r // 2, [r // 2]
                if finishing and r % 2 == 0:
                    final_mix(fin_early, i, us, g, TR)
                    stage_places(fin_early, i + 2, us)
                elif finishing:
                    final_add(fin_early, i, us, g, TR)

            dve.drain()
            stage_places(fin_early, 0, [0, 1])
            stage_places(fin_late, TE, list(range(8)))
            keep_up(late, 0, 0, 0)
            late_steps(dve, late.steps, late_step)

            def finish_group(m, g, h, n, r):
                us = [4 * h + b for b in range(n)]
                final_mix(fin_late, tile_of(m), us, g, r)
                after = 4
                if isinstance(m, int) and m >= FOURS - 2:
                    after = (LEFT, 1, 0, 0)[m - FOURS + 2]
                if after:
                    stage_places(fin_late, tile_of(m + 2), us[:after])
                final_add(fin_late, m, us, g, r)

            wait_all_out(dve)
            late_groups(dve, finish_group)

        @block.tensor
        def _(pe):
            pe.wait_ge(consts_ready, 1)
            pe.wait_ge(base_ready, 1)
            pe.matmul(small[:, 0:64], ones[0:1, :], base_rowf[:, :], start=True, stop=True).then_inc(base_spread, 1)
            pe.wait_ge(bad_ready, 1)
            pe.matmul(small[:, 64:65], ones[:], bad_sum[:], start=True, stop=True).then_inc(bad_summed, 1)
            pe.wait_ge(params_in, 96)

            def tok_turn(i, b, m, r):
                pe.wait_ge(tok_in[b], 48 * m + 48)
                wait(pe, tok_turned_kept, i)
                for k in range(2 * DH):
                    last = pe.transpose(turn[:, k * P:k * P + r], h_t[0:r, b, k * P:(k + 1) * P], ident[0:r, 0:r])
                last.then_inc(tok_turned, 1)

            def tok_project(i, b, m, r):
                wait(pe, tok_res, i)
                pe.wait_ge(tok_turned_kept, i + 1)
                for k in range(2 * DH):
                    last = pe.matmul(proj[0][0:r, 0:D], hT_t[:, k, 0:r], gnn_w_sb[:, k, :], start=(k == 0), stop=(k == 2 * DH - 1))
                last.then_inc(tok_projected, 1)

            def tok_turn_t(i, b, m, r):
                wait(pe, t_turned_kept, i)
                pe.wait_ge(tok_t, i + 1)
                for k in range(DH):
                    last = pe.transpose(turn2[:, k * P:k * P + r], t_t[0:r, b, k * P:(k + 1) * P], ident[0:r, 0:r])
                last.then_inc(t_turned, 1)

            def tok_gate(i, b, m, r):
                wait(pe, tok_placed, i)
                pe.wait_ge(t_turned_kept, i + 1)
                for k in range(DH):
                    last = pe.matmul(small2[0:r, 0:X], tT_t[:, k, 0:r], gate_w_sb[:, k, :], start=(k == 0), stop=(k == DH - 1))
                last.then_inc(tok_gated, 1)

            def tok_rank(i, b, m, r):
                pe.wait_ge(tok_chosen, i + 1)
                pe.matmul(small2[0:r, X:2 * X], below[0:r, 0:r], both[0:r, :], start=True, stop=False)
                pe.matmul(small2[0:r, X:2 * X], ones[:, 0:r], routed[:, :], start=False, stop=True).then_inc(tok_ranked, 1)

            def tokens(i, b, m, r):
                for step in (tok_turn, tok_project, tok_turn_t, tok_gate, tok_rank):
                    step(i, b, m, r)

            def count_tokens(k):
                pe.wait_ge(counted, 2 * k + 1)
                pe.matmul(small[0:X, 0:P], routed[:, :], ones[:], start=True, stop=True)
                pe.matmul(small[:, P:P + X], ones[:], routed[:, :], start=True, stop=True).then_inc(counted, 1)

            def cumulate(k):
                pe.wait_ge(tiles_ready, k + 1)
                pe.matmul(small[:, 2 * P:2 * P + 2 * X], tiles_T[:, :], tri_eye[:, :], start=True, stop=True).then_inc(cumulated, 1)

            def turn_xs(f, s, r, g):
                u = r % f.ring
                pe.wait_ge(f.xs_in[u], 16 * uses(r, g, f.ring) + 16)
                wait(pe, f.xs_kept, s)
                for k in range(DH):
                    last = pe.transpose(f.xs_out[:, k * P:(k + 1) * P], f.xs[u][:, k * P:(k + 1) * P], ident[:])
                last.then_inc(f.xs_turned, 1)

            def expert_of(f, s):
                return pe.value_load(step_row[f.k][0:1, bass.ds(2 * s + 1, 1)], min_val=0, max_val=X - 1)

            def up(f, s, r, g):
                b = r % f.depth
                e = expert_of(f, s)
                wait(pe, f.up_kept if f is late else f.y_kept, s - f.depth + 1)
                pe.wait_ge(f.xs_kept, s + 1)
                for k in range(DH):
                    last = pe.matmul(f.up_out[b], f.xsT[b][:, k, :], w1_sb[:, bass.ds(e * DH + k, 1), :], start=(k == 0), stop=(k == DH - 1))
                last.then_inc(f.up_done, 1)

            def turn_h(f, s, r, g):
                wait(pe, f.h_kept, s)
                pe.wait_ge(f.up_kept, s + 1)
                for k in range(FH):
                    last = pe.transpose(f.h_out[:, k * P:(k + 1) * P], f.hb[r % f.depth][:, k * P:(k + 1) * P], ident[:])
                last.then_inc(f.h_turned, 1)

            def down(f, s, r, g):
                b = r % f.depth
                e = expert_of(f, s)
                wait(pe, f.y_kept, s - f.depth + 1)
                pe.wait_ge(f.h_kept, s + 1)
                for k in range(FH):
                    last = pe.matmul(f.down_out[b], f.hT[b][:, k, :], w2_sb[:, bass.ds(e * FH + k, 1), :], start=(k == 0), stop=(k == FH - 1))
                last.then_inc(f.down_done, 1)

            def early_step(s, r, g):
                for part_of_step in (turn_xs, up, turn_h, down):
                    part_of_step(early, s, r, g)

            def with_tokens(i, b, m, r):
                at = {j: (lambda f=f: f(i, b, m, r)) for j, f in ((8, tok_turn), (11, tok_project), (19, tok_turn_t), (21, tok_gate))}
                if not (isinstance(i, int) and i == 0):
                    at[4] = lambda: tok_rank(i - 1, 1 - b, None, r)
                return at

            def with_table():
                return {10: lambda: count_tokens(0), 14: lambda: cumulate(0)}

            def with_steps(g, b):
                return {j: (lambda f=f, r=2 * b + n: f(early, 4 * g + r, r, g))
                        for n, places in enumerate(((0, 3, 6, 9), (12, 16, 18, 22)))
                        for j, f in zip(places, (turn_xs, up, turn_h, down))}

            def sum_chunk(hop, c, b, others={}):
                n = c + CH * hop
                wait(pe, window_kept, n - 1)
                for j in range(CT):
                    pe.wait_ge(sel_built, CT * n + j + 1)
                    pe.wait_ge(rows_in[j % SR], 16 * (2 * n + j // SR) + 16)
                    pe.matmul(win[b][:, 0:D], sel[:, j % SR, :], rows[:, j % SR, :], start=(j == 0), stop=False).then_inc(tile_summed, 1)
                    if j in others:
                        others[j]()
                pe.wait_ge(shift_built, n + 1)
                wait(pe, window_kept, n)
                pe.matmul(win[b][:, 0:D], shift[:, b, :], kept[:, 1 - b, :], start=False, stop=True).then_inc(window_summed, 1)

            pe.wait_ge(slow_known, 1)
            slow = pe.value_load(slow_i[0:1, 0:1], min_val=0, max_val=1)
            with pe.If(slow):
                for hop in range(2):
                    with pe.Fori(0, ETILES) as k:
                        pe.wait_ge(slow_sel, k + 1 + ETILES * hop)
                        pe.wait_ge(slow_rows[hop][0], 16 * k + 16)
                        pe.matmul(win[0][:, 0:D], s_same_w, s_rows, start=True, stop=True)
                        pe.matmul(small[:, 0:1], s_same_below, ones[:, 0:1], start=True, stop=True).then_inc(slow_summed, 1)
                tokens(0, 0, 0, TR)
                tokens(1, 1, 0, TR)
                with pe.Fori(1, TE // 2) as m:
                    tokens(2 * m, 0, m, TR)
                    tokens(2 * m + 1, 1, m, TR)
                count_tokens(0)
                cumulate(0)
                pe.wait_ge(weights_in, 16 * 2 * X)
                pe.wait_ge(steps_in, 16)
                steps_of_four(pe, early.steps, early_step)
                with pe.Fori(TE // 2, TT // 2) as m:
                    tokens(2 * m, 0, m, TR)
                    tokens(2 * m + 1, 1, m, TR)
            with pe.Else():
                sum_chunk(0, 0, 0)
                sum_chunk(0, 1, 1)
                with pe.Fori(1, CH // 2) as q:
                    sum_chunk(0, 2 * q, 0)
                    sum_chunk(0, 2 * q + 1, 1)
                with pe.Fori(0, LAG // 2) as q:
                    sum_chunk(1, 2 * q, 0)
                    sum_chunk(1, 2 * q + 1, 1)
                sum_chunk(1, LAG, 0, with_tokens(0, 0, 0, TR))
                sum_chunk(1, LAG + 1, 1, with_tokens(1, 1, 0, TR))

                def full_chunk(q, b, others):
                    sum_chunk(1, 2 * q + b, b, {**with_tokens(2 * q + b - LAG, b, q - LAG // 2, TR), **others})

                first = EARLY // 2
                with pe.Fori(LAG // 2 + 1, first - 1) as q:
                    full_chunk(q, 0, {})
                    full_chunk(q, 1, {})
                full_chunk(first - 1, 0, with_table())
                full_chunk(first - 1, 1, {})
                pe.wait_ge(weights_in, 16 * 2 * X)
                pe.wait_ge(steps_in, 16)
                full_chunk(first, 0, with_steps(0, 0))
                full_chunk(first, 1, with_steps(0, 1))
                with pe.Fori(first + 1, CH // 2 - 1) as q:
                    full_chunk(q, 0, with_steps(q - first, 0))
                    full_chunk(q, 1, with_steps(q - first, 1))
                full_chunk(CH // 2 - 1, 0, with_steps(CH // 2 - 1 - first, 0))
                full_chunk(CH // 2 - 1, 1, {})
                tok_rank(TT - 4, 1, None, TR)
                tokens(TT - 3, 0, TT // 2 - 1, TR)
                tokens(TT - 2, 1, TT // 2 - 1, TR)
            tokens(TT - 1, 0, TT // 2, TLAST)

            count_tokens(1)
            cumulate(1)

            def late_step(s, r, g):
                known = isinstance(s, int)
                turn_h(late, s, r, g)
                if not (known and s == late.steps - 1):
                    up(late, s + 1, (r + 1) % 4, g + (r + 1) // 4)
                down(late, s, r, g)
                if not (known and s >= late.steps - 2):
                    turn_xs(late, s + 2, (r + 2) % 4, g + (r + 2) // 4)

            pe.wait_ge(steps_in, 32)
            turn_xs(late, 0, 0, 0)
            up(late, 0, 0, 0)
            turn_xs(late, 1, 1, 0)
            steps_of_four(pe, late.steps, late_step)


_INS = ["x", "src", "dst", "edge_weight", "L0_gnn_W", "L0_gnn_bias", "L0_ffn_gate_w", "L0_ffn_gate_b", "L0_ffn_w1",
        "L0_ffn_b1", "L0_ffn_w2", "L0_ffn_b2", "L0_ffn_gamma", "L0_ffn_beta"]


def kernel(**inputs):
    import numpy as np
    import concourse.bacc as bacc
    from concourse.bass_utils import run_bass_kernel_spmd

    nc = bacc.Bacc("TRN2", target_bir_lowering=False, num_devices=1)
    arrays, args = {}, []
    for name in _INS:
        a = np.ascontiguousarray(inputs[name])
        arrays[f"in_{name}"] = a
        args.append(nc.dram_tensor(f"in_{name}", a.shape, mybir.dt.from_np(a.dtype), kind="ExternalInput").ap())
    args.append(nc.dram_tensor("out", (N, D), F32, kind="ExternalOutput").ap())
    build(nc, *args)
    r = run_bass_kernel_spmd(nc, [arrays], core_ids=[0])
    return r.results[0]["out"]
```

```python
from contextlib import ExitStack

import concourse.bass as bass
from concourse import mybir

ALU = mybir.AluOpType
ACT = mybir.ActivationFunctionType
AX_X = mybir.AxisListType.X
F32 = mybir.dt.float32
I32 = mybir.dt.int32
U32 = mybir.dt.uint32

P = 128
N = 6250
D = 256
DH = D // P
NE = 206250
EPS = 1e-5

CT = 26
CH = 62
CE = CT * P
NEP = CH * CE
SR = CT // 2
GROUPS = {0: 4, 5: 8, 9: 12}
NR = N + P + 22
assert NEP >= NE and CH % 2 == 0

LR = 6
LG = 8
LMAIN = P * LR * LG
LTAIL = N - LMAIN
assert 0 < LTAIL <= P and LG % 4 == 0

TR = 104
TT = -(-N // TR)
TLAST = N - (TT - 1) * TR
LAG = 4
assert TT % 4 == 1 and CH - LAG == TT - 3

X = 16
F = 512
FH = F // P
TE = 26
ROUND_TOKENS = [TE * TR, N - TE * TR]
CAP = max(ROUND_TOKENS) + P
STEPS = [(2 * n + X * (P - 1)) // P for n in ROUND_TOKENS]
SPARE = max(s - (-(-2 * n // P)) for s, n in zip(STEPS, ROUND_TOKENS))
NSLOT = X * CAP + SPARE * P
EARLY = TE + LAG + 2
assert max(STEPS) <= P and TE % 2 == 0 and EARLY % 2 == 0 and TE + LAG >= 8
assert STEPS[0] % 4 == 2 and STEPS[0] <= 2 * (CH - EARLY) and STEPS[0] // 4 == (CH - EARLY) // 2 - 1

FOURS = (TT - TE - 1) // 4
LEFT = TT - TE - 1 - 4 * FOURS
assert FOURS % 2 == 0 and LEFT > 0 and TE // 2 < (STEPS[1] - 3) // 4

ROUND = 8388608.0
FAR = 1000.0
OUT = 65536.0
ETILES = NEP // P


class Round:
    pass


class Finish:
    pass


def wait(eng, sem, value):
    if isinstance(value, int) and value <= 0:
        return
    eng.wait_ge(sem, value)


def wait_apart(eng, always, sem, value):
    if not isinstance(value, int):
        value = eng.to_reg(value)
    eng.wait_ge(always, 1)
    wait(eng, sem, value)


def ln_groups(eng, group, check):
    for r in range(4):
        group(r, r, 0)
    check()
    with eng.Fori(1, LG // 4) as g:
        for r in range(4):
            group(4 * g + r, r, g)


def steps_of_four(eng, count, step):
    for r in range(4):
        step(r, r, 0)
    whole = (count - 3) // 4
    with eng.Fori(1, whole) as g:
        for r in range(4):
            step(4 * g + r, r, g)
    for s in range(4 * whole, count):
        step(s, s % 4, s // 4)


def late_steps(eng, count, step):
    for r in range(4):
        step(r, r, 0, True)
    whole = (count - 3) // 4
    with eng.Fori(1, TE // 2) as g:
        for r in range(4):
            step(4 * g + r, r, g, True)
    with eng.Fori(TE // 2, whole) as g:
        for r in range(4):
            step(4 * g + r, r, g, False)
    for s in range(4 * whole, count):
        step(s, s % 4, s // 4, False)


def late_groups(eng, group):
    for h in range(2):
        group(h, 0, h, 4, TR)
    with eng.Fori(1, FOURS // 2 - 1) as g:
        for h in range(2):
            group(2 * g + h, g, h, 4, TR)
    for h in range(2):
        group(FOURS - 2 + h, FOURS // 2 - 1, h, 4, TR)
    group(FOURS, FOURS // 2, 0, LEFT, TR)
    group(FOURS + 1, FOURS // 2, 1, 1, TLAST)


def build(nc, x, src, dst, edge_weight, gnn_w, gnn_bias, gate_w, gate_b, w1, b1, w2, b2, gamma, beta, out):
    ctx = ExitStack()
    with ctx:
        def sb(name, shape, dt=F32):
            return ctx.enter_context(nc.sbuf_tensor(name, shape, dt))

        def bank(name):
            return ctx.enter_context(nc.psum_tensor(name, [P, 512], F32))

        def sem(name):
            return ctx.enter_context(nc.semaphore(name))

        def sems(name, n):
            return [sem(f"{name}{i}") for i in range(n)]

        def dram(name, shape, dt=F32):
            return nc.dram_tensor(name, shape, dt).ap()

        xn_rows = dram("xn_rows", (N, D))
        h_rows = [dram("h1_rows", (NR, D)), dram("h2_rows", (NR, D))]
        res_rows = dram("res_rows", (N, D))
        src_pad = dram("src_pad", (NEP,), I32)
        dst_pad = dram("dst_pad", (NEP + NEP // P,), I32)
        w_pad = dram("w_pad", (NEP,))
        slot_in = [dram(f"slot_in{k}", (NSLOT, D)) for k in range(2)]
        slot_out = dram("slot_out", (sum(STEPS) * P, D))
        bias_tab = dram("bias_tab", (X, F + D))
        step_tab = [dram(f"step_tab{k}", (P, 2), I32) for k in range(2)]

        w1_sb = sb("w1_sb", [P, X * DH, F])
        w2_sb = sb("w2_sb", [P, X * FH, D])
        scratch1 = w1_sb[:, :, :].rearrange("p a b -> p (a b)")
        ln_in = [scratch1[:, b * LR * D:(b + 1) * LR * D].rearrange("p (r d) -> p r d", d=D) for b in range(4)]
        ln_out = [scratch1[:, (4 + b) * LR * D:(5 + b) * LR * D].rearrange("p (r d) -> p r d", d=D) for b in range(2)]
        tail_in = scratch1[:, 6 * LR * D:(6 * LR + 1) * D].unsqueeze(1)
        tail_out = scratch1[:, (6 * LR + 1) * D:(6 * LR + 2) * D].unsqueeze(1)
        PK = NEP // P
        scratch2 = w2_sb[:, 0:16, :].rearrange("p a b -> p (a b)")
        dst_all = scratch2[:, 0:PK + 1].bitcast(I32)
        unsorted = scratch2[:, PK + 1:2 * PK + 1]
        pad_i = sb("pad_i", [1, 3 * P], I32)

        rows = sb("rows", [P, SR, D])
        sel = sb("sel", [P, SR, P])
        kept = sb("kept", [P, 2, D])
        shift = sb("shift", [P, 2, P])
        src_t = [sb(f"src_t{b}", [P, CT], I32) for b in range(2)]
        dst_t = [sb(f"dst_t{b}", [P, CT], I32) for b in range(2)]
        w_t = [sb(f"w_t{b}", [P, CT]) for b in range(2)]
        dst_rel = [sb(f"dst_rel{b}", [P, CT]) for b in range(2)]

        col_id = sb("col_id", [P, P])
        diff_id = sb("diff_id", [P, P])
        ident = sb("ident", [P, P])
        below = sb("below", [P, P])
        ones = sb("ones", [P, P])
        zeros = sb("zeros", [P, D])
        tri_eye = sb("tri_eye", [X, 2 * X])
        row_id = sb("row_id", [P, 1])
        base_row = sb("base_row", [1, 64], I32)
        base_rowf = sb("base_rowf", [1, 64])
        base = sb("base", [P, 64])
        delta = sb("delta", [P, 64])
        need = sb("need", [P, 64])
        bad = sb("bad", [P, 3])
        bad_sum = sb("bad_sum", [P, 1])
        slow_i = sb("slow_i", [P, 1], I32)

        gnn_w_sb = sb("gnn_w_sb", [P, 2 * DH, D])
        bias_sb = sb("bias_sb", [P, D])
        gamma_sb = sb("gamma_sb", [P, D])
        beta_sb = sb("beta_sb", [P, D])
        gate_w_sb = sb("gate_w_sb", [P, DH, X])
        gate_b_sb = sb("gate_b_sb", [P, X])
        slot_base = sb("slot_base", [P, X])

        ln_stats = sb("ln_stats", [P, LR, 6])
        ln_mv = [sb(f"ln_mv{b}", [P, LR, 2]) for b in range(4)]
        ln_small = [sb(f"ln_small{b}", [P, 6, LR]) for b in range(4)]

        x_t = sb("x_t", [P, 2, D])
        h_t = sb("h_t", [P, 2, 2 * D])
        hT_t = sb("hT_t", [P, 2 * DH, TR])
        mid_t = sb("mid_t", [P, D])
        res_t = sb("res_t", [P, 2, D])
        t_t = sb("t_t", [P, 2, D])
        tT_t = sb("tT_t", [P, DH, TR])
        tok_stats = sb("tok_stats", [P, 4, 6])
        tok_mv = sb("tok_mv", [P, 4, 2])
        tok_small = sb("tok_small", [P, 6, 4])
        logits = sb("logits", [P, X])
        top_v = sb("top_v", [P, 8])
        top_i = sb("top_i", [P, 8], U32)
        top_f = sb("top_f", [P, 2])
        gaps = sb("gaps", [P, TT])
        gaps_exp = sb("gaps_exp", [P, TT])
        gaps_sum = sb("gaps_sum", [P, TT])
        weights_1 = sb("weights_1", [P, TT])
        weights_2 = sb("weights_2", [P, TT])
        done = sb("done", [P, 1])
        chosen = sb("chosen", [P, 2, X])
        both = sb("both", [P, X])
        routed = sb("routed", [P, X])
        place = sb("place", [P, X])
        placed = sb("placed", [P, 2, X])
        pos_f = sb("pos_f", [P, 2])
        pos_t = [sb(f"pos_t{b}", [P, 2], I32) for b in range(2)]
        pos_all = sb("pos_all", [P, 2 * TT])
        exp_all = sb("exp_all", [P, 2 * TT])
        pos_fix = sb("pos_fix", [P, 2 * TT])
        slot_fix = sb("slot_fix", [P, X])

        tiles_T = sb("tiles_T", [X, P])
        tiles_C = sb("tiles_C", [P, 2 * X])
        step_cmp = sb("step_cmp", [P, X])
        step_cum = sb("step_cum", [P, X])
        step_f = sb("step_f", [P, 4])
        step_i = [sb(f"step_i{k}", [P, 2], I32) for k in range(2)]
        step_row = [sb(f"step_row{k}", [1, 2 * P], I32) for k in range(2)]
        zero_f = sb("zero_f", [P, X])
        zero_at = [sb(f"zero_at{k}", [P, X], I32) for k in range(2)]

        early_room = sb("early_room", [P, 3584])
        rooms = [t.rearrange("p a b -> p (a b)") for t in (rows[:, :, :], sel[:, :, :])] + [early_room[:, :]]
        sizes = [SR * D, SR * P, 3584]

        def parts(room_list):
            left = {k: 0 for k in room_list}

            def part(n):
                k = next(k for k in left if left[k] + n <= sizes[k])
                left[k] += n
                return rooms[k][:, left[k] - n:left[k]]
            return part

        def in_tiles(a):
            return a.rearrange("p (k t) -> p k t", t=P)

        def round_buffers(part, depth, ring):
            f = Round()
            f.depth, f.ring = depth, ring
            f.bias = [part(F + D) for _ in range(ring)]
            f.hb = [part(F) for _ in range(depth)]
            f.hT = [in_tiles(part(F)) for _ in range(depth)]
            f.xs = [part(D) for _ in range(ring)]
            f.xsT = [in_tiles(part(D)) for _ in range(depth)]
            f.ys = [part(D) for _ in range(depth)]
            return f

        early = round_buffers(parts([2]), 1, 2)
        late = round_buffers(parts([0, 1, 2]), 2, 4)
        fin_early, fin_late = Finish(), Finish()
        fin_early.y_a = [h_t[:, b, 0:D] for b in range(2)]
        fin_early.y_b = [h_t[:, b, D:2 * D] for b in range(2)]
        fin_early.sum = [x_t[:, b, :] for b in range(2)]
        fin_early.res = [res_t[:, b, :] for b in range(2)]
        part = parts([0, 1, 2])
        fin_late.y_a, fin_late.y_b, fin_late.sum, fin_late.res = ([part(D) for _ in range(8)] for _ in range(4))
        for f, name in ((fin_early, "early"), (fin_late, "late")):
            f.ring = len(f.res)
            f.half = f.ring // 2
            f.pos = [sb(f"pos_{name}{b}", [P, 2], I32) for b in range(f.ring)]

        s_src = sb("s_src", [P, 1], I32)
        s_dst = sb("s_dst", [P, 1], I32)
        s_w = sb("s_w", [P, 1])
        s_dstf = sb("s_dstf", [P, 1])
        s_rep = sb("s_rep", [P, 1])
        s_repf = sb("s_repf", [P, 1])
        s_put = sb("s_put", [P, 1], I32)
        s_dst_row = sel[:, 0, :].bitcast(I32)
        s_dst_rowf = sel[:, 1, :]
        s_same_w = sel[:, 2, :]
        s_same_below = sel[:, 3, :]
        s_rows, s_old, s_new = rows[:, 0, :], rows[:, 1, :], rows[:, 2, :]

        win = [bank("win0"), bank("win1")]
        turn = bank("turn")
        turn2 = bank("turn2")
        proj = [bank("proj0"), bank("proj1")]
        small = bank("small")
        small2 = bank("small2")
        early.xs_out, early.h_out = small[:, 0:2 * P], small[:, :]
        early.up_out, early.down_out = [proj[1][:, :]], [proj[1][:, 0:D]]
        late.xs_out, late.h_out = turn2[:, 0:2 * P], turn[:, :]
        late.up_out, late.down_out = [w[:, :] for w in win], [p[:, 0:D] for p in proj]

        iotas = sem("iotas")
        fills = sem("fills")
        consts_ready = sem("consts_ready")
        params_in = sem("params_in")
        edges_copied = sem("edges_copied")
        pad_in = sem("pad_in")
        dst_in = sem("dst_in")
        base_in = sem("base_in")
        base_ready = sem("base_ready")
        base_spread = sem("base_spread")
        base_kept = sem("base_kept")
        bad_ready = sem("bad_ready")
        bad_summed = sem("bad_summed")
        slow_known = sem("slow_known")
        ln_loaded = sems("ln_loaded", 4)
        tail_loaded = sem("tail_loaded")
        ln_var = sem("ln_var")
        ln_sd = sem("ln_sd")
        ln_scaled = sem("ln_scaled")
        ln_applied = sem("ln_applied")
        ln_stored = sems("ln_stored", 2)
        tail_stored = sem("tail_stored")
        weights_in = sem("weights_in")

        edges_in = sems("edges_in", 2)
        rel_ready = sem("rel_ready")
        sel_built = sem("sel_built")
        shift_built = sem("shift_built")
        rows_in = sems("rows_in", SR)
        tile_summed = sem("tile_summed")
        window_summed = sem("window_summed")
        window_kept = sem("window_kept")
        window_out = sem("window_out")

        slow_zeroed = sem("slow_zeroed")
        slow_loaded = [sems(f"slow_loaded{h}_", 4) for h in range(2)]
        slow_sel = sem("slow_sel")
        slow_rows = [sems(f"slow_rows{h}_", 2) for h in range(2)]
        slow_summed = sem("slow_summed")
        slow_new = sem("slow_new")
        slow_stored = sems("slow_stored", 2)

        tok_in = sems("tok_in", 2)
        tok_turned = sem("tok_turned")
        tok_turned_kept = sem("tok_turned_kept")
        tok_projected = sem("tok_projected")
        tok_res = sem("tok_res")
        tok_var = sem("tok_var")
        tok_sd = sem("tok_sd")
        tok_t = sem("tok_t")
        tok_out = sems("tok_out", 2)
        t_turned = sem("t_turned")
        t_turned_kept = sem("t_turned_kept")
        tok_gated = sem("tok_gated")
        tok_chosen = sem("tok_chosen")
        gaps_raised = sem("gaps_raised")
        weights_ready = sem("weights_ready")
        tok_ranked = sem("tok_ranked")
        tok_placed = sem("tok_placed")
        tok_scattered = sems("tok_scattered", 2)

        counted = sem("counted")
        tiles_ready = sem("tiles_ready")
        cumulated = sem("cumulated")
        steps_ready = sem("steps_ready")
        steps_out = sem("steps_out")
        steps_in = sem("steps_in")
        zeros_out = sem("zeros_out")
        spare_out = sem("spare_out")
        biases_out = sem("biases_out")
        for k, f, name in ((0, early, "early"), (1, late, "late")):
            f.k = k
            f.steps = STEPS[k]
            f.xs_in = sems(f"{name}_xs_in", f.ring)
            f.bias_in = sems(f"{name}_bias_in", f.ring)
            f.xs_turned = sem(f"{name}_xs_turned")
            f.xs_kept = sem(f"{name}_xs_kept")
            f.up_done = sem(f"{name}_up_done")
            f.up_kept = sem(f"{name}_up_kept")
            f.h_turned = sem(f"{name}_h_turned")
            f.h_kept = sem(f"{name}_h_kept")
            f.down_done = sem(f"{name}_down_done")
            f.y_kept = sem(f"{name}_y_kept")
            f.y_out = sems(f"{name}_y_out", f.depth)

        for f, name in ((fin_early, "early"), (fin_late, "late")):
            f.pos_staged = sem(f"{name}_pos_staged")
            f.y_in = sems(f"{name}_y_in", 2)
            f.weighed = sem(f"{name}_weighed")
            f.mixed = sem(f"{name}_mixed")
            f.res_in = sems(f"{name}_res_in", 2)
            f.var = sem(f"{name}_var")
            f.sd = sem(f"{name}_sd")
            f.ready = sem(f"{name}_ready")
            f.stored = sems(f"{name}_stored", 2)

        block = ctx.enter_context(nc.Block())

        x_main = x[0:LMAIN, :].rearrange("(p r) d -> p r d", p=P)
        xn_main = xn_rows[0:LMAIN, :].rearrange("(p r) d -> p r d", p=P)
        hop_in = [xn_rows, h_rows[0][0:N, :]]
        gate_w_v = gate_w.rearrange("(k p) e -> p k e", p=P)
        gnn_w_v = gnn_w.rearrange("h (k p) d -> p (h k) d", p=P)

        def chunk_view(a, c):
            return a[bass.ds(c * CE, CE)].rearrange("(p j) -> p j", p=P)

        def as_row(a):
            return a.rearrange("(a n) -> a n", a=1)

        def tile_rows(i, r):
            return bass.ds(i * TR, r)

        def uses(r, g, n):
            return (4 // n) * g + r // n

        left_tiles = [(TT - 4, 1, TT // 2 - 2, TR), (TT - 3, 0, TT // 2 - 1, TR), (TT - 2, 1, TT // 2 - 1, TR), (TT - 1, 0, TT // 2, TLAST)]

        def tile_of(m):
            if not isinstance(m, int) or m <= FOURS:
                return TE + 4 * m
            return TT - 1

        def fill_zeros(eng, k, first, end):
            with eng.Fori(first // 4, end // 4) as q:
                places = [eng.value_load(zero_at[k][0:1, bass.ds(4 * q + n, 1)], min_val=0, max_val=NSLOT - P) for n in range(4)]
                for at in places:
                    eng.dma_start(slot_in[k][bass.ds(at, P), :], zeros[:, :]).then_inc(zeros_out, 16)

        def wait_all_out(eng):
            for f in (early, late):
                for b in range(f.depth):
                    eng.wait_ge(f.y_out[b], 16 * (-(-(f.steps - b) // f.depth)))

        @block.sync
        def _(sp):
            sp.dma_start(as_row(dst_pad[0:NE]), as_row(dst)).then_inc(edges_copied, 16)

            def load_ln(s, r, g):
                wait(sp, ln_applied, s - 3)
                sp.dma_start(ln_in[r], x_main[:, bass.ds(s * LR, LR), :]).then_inc(ln_loaded[r], 16)

            def load_dst():
                sp.dma_start(tail_in[0:LTAIL, 0, :], x[LMAIN:N, :]).then_inc(tail_loaded, 16)
                npad = NEP - NE
                sp.wait_ge(fills, 3)
                sp.dma_start(as_row(dst_pad[NE:NEP + P]), pad_i[:, P:P + npad + P]).then_inc(edges_copied, 16)
                sp.wait_ge(edges_copied, 32)
                sp.dma_start(dst_all[:, 0:PK], dst_pad[0:NEP].rearrange("(p k) -> p k", p=P)).then_inc(dst_in, 16)
                firsts = dst_pad[CE:NEP].rearrange("(c e) -> c e", e=CE)[:, 0:1].rearrange("c e -> e c")
                with nc.allow_non_contiguous_dma("one element per partition, and per chunk"):
                    sp.dma_start(dst_all[:, PK:PK + 1], dst_pad[PK:PK + NEP].rearrange("(p k) -> p k", p=P)[:, 0:1]).then_inc(dst_in, 16)
                    sp.dma_start(base_row[:, 1:CH], firsts).then_inc(base_in, 16)
                sp.dma_start(as_row(src_pad[0:NE]), as_row(src)).then_inc(edges_copied, 16)
                sp.dma_start(as_row(w_pad[0:NE]), as_row(edge_weight)).then_inc(edges_copied, 16)
                sp.dma_start(as_row(src_pad[NE:NEP]), pad_i[:, 0:npad]).then_inc(edges_copied, 16)
                sp.dma_start(as_row(w_pad[NE:NEP]), pad_i[:, 0:npad].bitcast(F32)).then_inc(edges_copied, 16)

            ln_groups(sp, load_ln, load_dst)
            sp.dma_start(bias_tab[:, 0:F], b1).then_inc(biases_out, 16)
            sp.dma_start(bias_tab[:, F:F + D], b2).then_inc(biases_out, 16)
            sp.wait_ge(edges_copied, 96)

            def load_tokens(i, b, m, r):
                wait(sp, tok_res, i - 1)
                sp.dma_start(x_t[0:r, b, :], x[tile_rows(i, r), :]).then_inc(tok_in[b], 16)
                sp.dma_start(h_t[0:r, b, 0:D], h_rows[0][tile_rows(i, r), :]).then_inc(tok_in[b], 16)
                sp.dma_start(h_t[0:r, b, D:2 * D], h_rows[1][tile_rows(i, r), :]).then_inc(tok_in[b], 16)

            def load_edges(hop, c, b):
                wait(sp, tile_summed, CT * (c + CH * hop - 1))
                sp.dma_start(src_t[b][:], chunk_view(src_pad, c)).then_inc(edges_in[b], 16)
                sp.dma_start(dst_t[b][:], chunk_view(dst_pad, c)).then_inc(edges_in[b], 16)
                sp.dma_start(w_t[b][:], chunk_view(w_pad, c)).then_inc(edges_in[b], 16)

            def publish_steps(f):
                k = f.k
                sp.wait_ge(steps_ready, k + 1)
                sp.dma_start(step_tab[k], step_i[k][:, :]).then_inc(steps_out, 16)
                sp.wait_ge(steps_out, 16 * (k + 1))
                sp.dma_start(step_row[k][:, :], as_row(step_tab[k].rearrange("p a -> (p a)"))).then_inc(steps_in, 16)
                fill_zeros(sp, k, 0, X // 2 if k else X)
                sp.wait_ge(zeros_out, 16 * X * (k + 1))
                sp.wait_ge(spare_out, 32)
                tiles = TT if k else TE
                for b in range(2):
                    sp.wait_ge(tok_scattered[b], 32 * (-(-(tiles - b) // 2)))
                sp.wait_ge(steps_in, 16 * (k + 1))
                sp.wait_ge(biases_out, 32)

            def load_slots(f, s, r, g):
                u = r % f.ring
                at = sp.value_load(step_row[f.k][0:1, bass.ds(2 * s, 1)], min_val=0, max_val=NSLOT - P)
                e = sp.value_load(step_row[f.k][0:1, bass.ds(2 * s + 1, 1)], min_val=0, max_val=X - 1)
                wait(sp, f.y_kept, s - f.ring + 1)
                sp.dma_start(f.xs[u], slot_in[f.k][bass.ds(at, P), :]).then_inc(f.xs_in[u], 16)
                sp.dma_start(f.bias[u], bias_tab[bass.ds(e, 1), :].partition_broadcast(P)).then_inc(f.bias_in[u], 16)

            def load_both(c, b, i, m, q=None):
                load_edges(1, c, b)
                if isinstance(c, int) and c == EARLY - 1:
                    publish_steps(early)
                if q is not None:
                    for r in (2 * b, 2 * b + 1):
                        load_slots(early, 4 * q + r, r, q)
                wait_apart(sp, consts_ready, window_out, 16 * (CH + c))
                load_tokens(i, b, m, TR)

            def fill_spare(k):
                sp.dma_start(slot_in[k][X * CAP:NSLOT, :].rearrange("(a p) d -> p a d", p=P),
                             zeros[:, :].unsqueeze(1).to_broadcast([P, SPARE, D])).then_inc(spare_out, 16)

            sp.wait_ge(slow_known, 1)
            slow = sp.value_load(slow_i[0:1, 0:1], min_val=0, max_val=1)
            sp.wait_ge(consts_ready, 1)
            with sp.If(slow):
                fill_spare(0)
                fill_spare(1)
                for hop in range(2):
                    with sp.Fori(0, ETILES) as k:
                        e0 = k * P
                        sp.dma_start(s_src[:], src_pad[bass.ds(e0, P)].rearrange("(p a) -> p a", a=1)).then_inc(slow_loaded[hop][0], 16)
                        sp.dma_start(s_dst[:], dst_pad[bass.ds(e0, P)].rearrange("(p a) -> p a", a=1)).then_inc(slow_loaded[hop][1], 16)
                        sp.dma_start(s_w[:], w_pad[bass.ds(e0, P)].rearrange("(p a) -> p a", a=1)).then_inc(slow_loaded[hop][2], 16)
                        sp.dma_start(s_dst_row, as_row(dst_pad[bass.ds(e0, P)]).partition_broadcast(P)).then_inc(slow_loaded[hop][3], 16)
                        wait_apart(sp, consts_ready, slow_stored[hop], 16 * k + 16)
                load_tokens(0, 0, 0, TR)
                load_tokens(1, 1, 0, TR)
                with sp.Fori(1, TE // 2) as m:
                    load_tokens(2 * m, 0, m, TR)
                    load_tokens(2 * m + 1, 1, m, TR)
                publish_steps(early)
                steps_of_four(sp, early.steps, lambda s, r, g: load_slots(early, s, r, g))
                with sp.Fori(TE // 2, TT // 2) as m:
                    load_tokens(2 * m, 0, m, TR)
                    load_tokens(2 * m + 1, 1, m, TR)
            with sp.Else():
                load_edges(0, 0, 0)
                load_edges(0, 1, 1)
                with sp.Fori(1, CH // 2) as q:
                    load_edges(0, 2 * q, 0)
                    load_edges(0, 2 * q + 1, 1)
                fill_spare(0)
                with sp.Fori(0, LAG // 2) as q:
                    load_edges(1, 2 * q, 0)
                    load_edges(1, 2 * q + 1, 1)
                fill_spare(1)
                load_both(LAG, 0, 0, 0)
                load_both(LAG + 1, 1, 1, 0)
                def both_pair(q, g0=None, g1=None):
                    load_both(2 * q, 0, 2 * q - LAG, q - LAG // 2, g0)
                    load_both(2 * q + 1, 1, 2 * q + 1 - LAG, q - LAG // 2, g1)

                first = EARLY // 2
                with sp.Fori(LAG // 2 + 1, first - 1) as q:
                    both_pair(q)
                both_pair(first - 1)
                both_pair(first, 0, 0)
                with sp.Fori(first + 1, CH // 2 - 1) as q:
                    both_pair(q, q - first, q - first)
                both_pair(CH // 2 - 1, CH // 2 - 1 - first)
                sp.wait_ge(window_out, 16 * 2 * CH)
                load_tokens(TT - 3, 0, TT // 2 - 1, TR)
                load_tokens(TT - 2, 1, TT // 2 - 1, TR)
            load_tokens(TT - 1, 0, TT // 2, TLAST)

            publish_steps(late)

            def load_final(f, i, u, g, r):
                wait(sp, f.stored[u // f.half], 16 * f.half * g)
                sp.dma_start(f.res[u][0:r, :], res_rows[tile_rows(i, r), :]).then_inc(f.res_in[u // f.half], 16)

            def late_step(s, r, g, finishing):
                load_slots(late, s, r, g)
                if finishing and r % 2:
                    i = 2 * g + r // 2
                    load_final(fin_early, i, r // 2, g, TR)

            for b in range(2):
                sp.wait_ge(tok_out[b], 16 * (TT // 2 + 1 - b))
            late_steps(sp, late.steps, late_step)

            def load_group(m, g, h, n, r):
                for b in range(n):
                    load_final(fin_late, tile_of(m) + b, 4 * h + b, g, r)

            wait_all_out(sp)
            late_groups(sp, load_group)
            for b in range(2):
                sp.wait_ge(fin_early.stored[b], 16 * (TE // 2))
            sp.wait_ge(fin_late.stored[0], 16 * (2 * FOURS + LEFT))
            sp.wait_ge(fin_late.stored[1], 16 * (2 * FOURS + 1))

        @block.gpsimd
        def _(pool):
            exact = True
            pool.iota(col_id[:], [[1, P]], base=0, channel_multiplier=0, allow_small_or_imprecise_dtypes=exact).then_inc(iotas, 1)
            pool.iota(diff_id[:], [[-1, P]], base=0, channel_multiplier=1, allow_small_or_imprecise_dtypes=exact).then_inc(iotas, 1)
            pool.iota(row_id[:], [[0, 1]], base=0, channel_multiplier=1, allow_small_or_imprecise_dtypes=exact).then_inc(iotas, 1)
            pool.iota(need[:], [[TR, 64]], base=-TR * (LAG - 1), channel_multiplier=0, allow_small_or_imprecise_dtypes=exact).then_inc(iotas, 1)
            pool.iota(slot_base[:], [[CAP, X]], base=0, channel_multiplier=0, allow_small_or_imprecise_dtypes=exact).then_inc(iotas, 1)

            def scatter(i, b, m, r, k=1):
                wait_apart(pool, consts_ready, tok_placed, i + 1)
                for c in range(2):
                    pool.indirect_dma_start(slot_in[k][:, :], bass.IndirectOffsetOnAxis(ap=pos_t[b][0:r, c:c + 1], axis=0),
                                            t_t[0:r, b, :], None).then_inc(tok_scattered[b], 16)

            def gather_chunk(hop, c, b, q, scatters=None):
                wait_apart(pool, consts_ready, edges_in[b], 48 * (q + CH // 2 * hop) + 48)
                for j in range(CT):
                    if j % SR in GROUPS:
                        last = j - j % SR + GROUPS[j % SR]
                        wait_apart(pool, consts_ready, tile_summed, CT * (c + CH * hop) + last - SR + 1)
                    pool.indirect_dma_start(rows[:, j % SR, :], None, hop_in[hop][:, :],
                                            bass.IndirectOffsetOnAxis(ap=src_t[b][:, j:j + 1], axis=0)).then_inc(rows_in[j % SR], 16)
                    if j == SR - 1 and scatters:
                        scatters()

            pool.wait_ge(slow_known, 1)
            for b in range(2):
                pool.wait_ge(ln_stored[b], 16 * (LG // 2))
            pool.wait_ge(tail_stored, 16)
            slow = pool.value_load(slow_i[0:1, 0:1], min_val=0, max_val=1)
            with pool.If(slow):
                pool.wait_ge(slow_zeroed, 16 * 2 * (NR // P))
                for hop in range(2):
                    with pool.Fori(0, ETILES) as k:
                        wait_apart(pool, consts_ready, slow_loaded[hop][0], 16 * k + 16)
                        pool.indirect_dma_start(s_rows, None, hop_in[hop][:, :],
                                                bass.IndirectOffsetOnAxis(ap=s_src[:, 0:1], axis=0)).then_inc(slow_rows[hop][0], 16)
                        wait_apart(pool, consts_ready, slow_loaded[hop][1], 16 * k + 16)
                        pool.indirect_dma_start(s_old, None, h_rows[hop][0:N, :],
                                                bass.IndirectOffsetOnAxis(ap=s_dst[:, 0:1], axis=0)).then_inc(slow_rows[hop][1], 16)
                        wait_apart(pool, consts_ready, slow_new, k + 1 + ETILES * hop)
                        pool.indirect_dma_start(h_rows[hop][0:N, :], bass.IndirectOffsetOnAxis(ap=s_put[:, 0:1], axis=0),
                                                s_new, None, bounds_check=N - 1, oob_is_err=False).then_inc(slow_stored[hop], 16)
                        wait_apart(pool, consts_ready, slow_stored[hop], 16 * k + 16)
                        pool.engine_nop()
                scatter(0, 0, 0, TR, 0)
                scatter(1, 1, 0, TR, 0)
                with pool.Fori(1, TE // 2) as m:
                    scatter(2 * m, 0, m, TR, 0)
                    scatter(2 * m + 1, 1, m, TR, 0)
                with pool.Fori(TE // 2, TT // 2) as m:
                    scatter(2 * m, 0, m, TR)
                    scatter(2 * m + 1, 1, m, TR)
            with pool.Else():
                gather_chunk(0, 0, 0, 0)
                gather_chunk(0, 1, 1, 0)
                with pool.Fori(1, CH // 2) as q:
                    gather_chunk(0, 2 * q, 0, q)
                    gather_chunk(0, 2 * q + 1, 1, q)
                pool.wait_ge(window_out, 16 * CH)
                with pool.Fori(0, LAG // 2) as q:
                    gather_chunk(1, 2 * q, 0, q)
                    gather_chunk(1, 2 * q + 1, 1, q)
                q0 = LAG // 2
                gather_chunk(1, LAG, 0, q0)
                gather_chunk(1, LAG + 1, 1, q0, lambda: scatter(0, 0, 0, TR, 0))

                def gather_pair(q, k0, k1):
                    gather_chunk(1, 2 * q, 0, q, lambda: scatter(2 * q - LAG - 1, 1, q - q0 - 1, TR, k0))
                    gather_chunk(1, 2 * q + 1, 1, q, lambda: scatter(2 * q - LAG, 0, q - q0, TR, k1))

                with pool.Fori(q0 + 1, EARLY // 2 - 1) as q:
                    gather_pair(q, 0, 0)
                gather_pair(EARLY // 2 - 1, 0, 1)
                with pool.Fori(EARLY // 2, CH // 2) as q:
                    gather_pair(q, 1, 1)
                scatter(TT - 4, 1, TT // 2 - 2, TR)
                scatter(TT - 3, 0, TT // 2 - 1, TR)
                scatter(TT - 2, 1, TT // 2 - 1, TR)
            scatter(TT - 1, 0, TT // 2, TLAST)

            def gather_final(f, table, n, m, u, r):
                wait_apart(pool, consts_ready, f.mixed, m - 1)
                wait_apart(pool, consts_ready, f.pos_staged, n + 1)
                for k, y in ((0, f.y_a), (1, f.y_b)):
                    pool.indirect_dma_start(y[u][0:r, :], None, table,
                                            bass.IndirectOffsetOnAxis(ap=f.pos[u][0:r, k:k + 1], axis=0)).then_inc(f.y_in[u // f.half], 16)

            pool.wait_ge(early.y_out[0], 16 * early.steps)
            pool.wait_ge(tok_turned, TT)
            early_rows = slot_out[0:early.steps * P, :]
            gather_final(fin_early, early_rows, 0, 0, 0, TR)
            gather_final(fin_early, early_rows, 1, 1, 1, TR)
            with pool.Fori(1, TE // 2) as g:
                gather_final(fin_early, early_rows, 2 * g, 2 * g, 0, TR)
                gather_final(fin_early, early_rows, 2 * g + 1, 2 * g + 1, 1, TR)

            def gather_group(m, g, h, n, r):
                for b in range(n):
                    gather_final(fin_late, slot_out[:, :], tile_of(m) - TE + b, m, 4 * h + b, r)

            wait_all_out(pool)
            late_groups(pool, gather_group)

        @block.scalar
        def _(act):
            for dest, view in ((gnn_w_sb[:], gnn_w_v), (gate_w_sb[:], gate_w_v),
                               (bias_sb[:], as_row(gnn_bias).partition_broadcast(P)),
                               (gamma_sb[:], as_row(gamma).partition_broadcast(P)),
                               (beta_sb[:], as_row(beta).partition_broadcast(P)),
                               (gate_b_sb[:], as_row(gate_b).partition_broadcast(P))):
                act.dma_start(dest, view).then_inc(params_in, 16)

            def ln_root(s, b, r, n):
                act.wait_ge(ln_var, s + 1)
                act.activation(ln_small[b][0:r, 1, 0:n], ln_small[b][0:r, 0, 0:n], ACT.Sqrt).then_inc(ln_sd, 1)

            def ln_apply(s, b, source, target, r, n):
                act.wait_ge(ln_scaled, s + 1)
                for k in range(n):
                    last = act.activation(target[0:r, k, :], source[0:r, k, :], ACT.Identity,
                                          scale=ln_small[b][0:r, 4, k:k + 1], bias=ln_small[b][0:r, 5, k:k + 1])
                last.then_inc(ln_applied, 1)
                act.wait_ge(ln_applied, s + 1)

            def ln_finish(s, r, g):
                b = r % 2
                wait(act, ln_stored[b], 16 * (2 * g + r // 2))
                ln_apply(s, r, ln_in[r], ln_out[b], P, LR)
                act.dma_start(xn_main[:, bass.ds(s * LR, LR), :], ln_out[b]).then_inc(ln_stored[b], 16)

            def ln_group(s, r, g):
                ln_root(s, r, P, LR)
                if not (isinstance(s, int) and s == 0):
                    ln_finish(s - 1, (r - 1) % 4, g + (r - 1) // 4)

            def keep_base():
                act.wait_ge(base_spread, 1)
                act.copy(base[:, :], small[:, 0:64]).then_inc(base_kept, 1)

            ln_groups(act, ln_group, keep_base)
            ln_root(LG, 0, LTAIL, 1)
            ln_finish(LG - 1, 3, LG // 4 - 1)
            ln_apply(LG, 0, tail_in, tail_out, LTAIL, 1)
            act.dma_start(xn_rows[LMAIN:N, :], tail_out[0:LTAIL, 0, :]).then_inc(tail_stored, 16)
            act.wait_ge(slow_known, 1)
            for b in range(2):
                act.wait_ge(ln_stored[b], 16 * (LG // 2))
            act.wait_ge(tail_stored, 16)

            def load_expert(e):
                act.dma_start(w1_sb[:, bass.ds(e * DH, DH), :], w1[bass.ds(e, 1)].rearrange("e (k p) f -> p (e k) f", p=P)).then_inc(weights_in, 16)
                act.dma_start(w2_sb[:, bass.ds(e * FH, FH), :], w2[bass.ds(e, 1)].rearrange("e (k p) d -> p (e k) d", p=P)).then_inc(weights_in, 16)

            def tok_keep_turned(i, b, m, r):
                act.wait_ge(tok_turned, i + 1)
                wait(act, tok_projected, i)
                act.copy(hT_t[:, :, 0:r], turn[:, :].rearrange("p (k t) -> p k t", t=P)[:, :, 0:r]).then_inc(tok_turned_kept, 1)

            def tok_root(i, b, m, r):
                act.wait_ge(tok_var, i + 1)
                act.activation(tok_small[0:r, 1, 0:1], tok_small[0:r, 0, 0:1], ACT.Sqrt).then_inc(tok_sd, 1)

            def tok_store(i, b, m, r):
                act.wait_ge(t_turned, i + 1)
                wait(act, tok_gated, i)
                act.copy(tT_t[:, :, 0:r], turn2[:, 0:DH * P].rearrange("p (k t) -> p k t", t=P)[:, :, 0:r]).then_inc(t_turned_kept, 1)
                act.wait_ge(tok_res, i + 1)
                act.dma_start(res_rows[tile_rows(i, r), :], res_t[0:r, b, :]).then_inc(tok_out[b], 16)

            def tokens(i, b, m, r):
                for step in (tok_keep_turned, tok_root, tok_store):
                    step(i, b, m, r)

            def keep_xs(f, s, r, g):
                act.wait_ge(f.xs_turned, s + 1)
                wait(act, f.up_done, s - f.depth + 1)
                act.copy(f.xsT[r % f.depth], f.xs_out.rearrange("p (k t) -> p k t", t=P)).then_inc(f.xs_kept, 1)

            def keep_h(f, s, r, g):
                act.wait_ge(f.h_turned, s + 1)
                wait(act, f.down_done, s - f.depth + 1)
                act.activation(f.hT[r % f.depth], f.h_out.rearrange("p (k t) -> p k t", t=P), ACT.Relu).then_inc(f.h_kept, 1)

            def store_y(f, s, r, g):
                b = r % f.depth
                act.wait_ge(f.y_kept, s + 1)
                act.dma_start(slot_out[bass.ds((s + f.k * STEPS[0]) * P, P), :], f.ys[b]).then_inc(f.y_out[b], 16)

            def early_step(s, r, g):
                for part_of_step in (keep_xs, keep_h, store_y):
                    part_of_step(early, s, r, g)

            def keep_window(hop, c, b):
                n = c + CH * hop
                act.wait_ge(window_summed, n + 1)
                wait(act, window_out, 16 * (n - 1))
                act.copy(kept[:, b, :], win[b][:, 0:D]).then_inc(window_kept, 1)
                at = act.value_load(base_row[0:1, bass.ds(c, 1)], min_val=0, max_val=N - 1)
                wait(act, window_out, 16 * n)
                act.wait_ge(window_kept, n + 1)
                act.dma_start(h_rows[hop][bass.ds(at, P), :], kept[:, b, :]).then_inc(window_out, 16)

            slow = act.value_load(slow_i[0:1, 0:1], min_val=0, max_val=1)
            with act.If(slow):
                with act.Fori(0, X) as e:
                    load_expert(e)
                with act.Fori(0, NR // P) as k:
                    for table in h_rows:
                        act.dma_start(table[bass.ds(k * P, P), :], zeros[:, :]).then_inc(slow_zeroed, 16)
                tokens(0, 0, 0, TR)
                tokens(1, 1, 0, TR)
                with act.Fori(1, TE // 2) as m:
                    tokens(2 * m, 0, m, TR)
                    tokens(2 * m + 1, 1, m, TR)
                steps_of_four(act, early.steps, early_step)
                with act.Fori(TE // 2, TT // 2) as m:
                    tokens(2 * m, 0, m, TR)
                    tokens(2 * m + 1, 1, m, TR)
                tokens(TT - 1, 0, TT // 2, TLAST)
            with act.Else():
                keep_window(0, 0, 0)
                keep_window(0, 1, 1)
                with act.Fori(1, X + 1) as q:
                    keep_window(0, 2 * q, 0)
                    keep_window(0, 2 * q + 1, 1)
                    load_expert(q - 1)
                with act.Fori(X + 1, CH // 2) as q:
                    keep_window(0, 2 * q, 0)
                    keep_window(0, 2 * q + 1, 1)
                with act.Fori(0, LAG // 2) as q:
                    keep_window(1, 2 * q, 0)
                    keep_window(1, 2 * q + 1, 1)
                tokens(0, 0, 0, TR)
                keep_window(1, LAG, 0)
                tokens(1, 1, 0, TR)
                keep_window(1, LAG + 1, 1)

                def full_chunk(q, b, g=None):
                    token_tile = (2 * q + b - LAG, b, q - LAG // 2, TR)
                    if g is None:
                        tokens(*token_tile)
                    else:
                        s0, s1 = ((early, 4 * g + r, r, g) for r in (2 * b, 2 * b + 1))
                        keep_xs(*s0)
                        keep_h(*s0)
                        tok_keep_turned(*token_tile)
                        store_y(*s0)
                        keep_xs(*s1)
                        tok_root(*token_tile)
                        tok_store(*token_tile)
                        keep_h(*s1)
                        store_y(*s1)
                    keep_window(1, 2 * q + b, b)

                first = EARLY // 2
                with act.Fori(LAG // 2 + 1, first) as q:
                    full_chunk(q, 0)
                    full_chunk(q, 1)
                full_chunk(first, 0, 0)
                full_chunk(first, 1, 0)
                with act.Fori(first + 1, CH // 2 - 1) as q:
                    full_chunk(q, 0, q - first)
                    full_chunk(q, 1, q - first)
                full_chunk(CH // 2 - 1, 0, CH // 2 - 1 - first)
                full_chunk(CH // 2 - 1, 1)
                tok_keep_turned(*left_tiles[1])
                for n in (1, 2, 3):
                    tok_root(*left_tiles[n])
                    tok_store(*left_tiles[n])
                    if n < 3:
                        tok_keep_turned(*left_tiles[n + 1])

            def final_weigh(f, i, us, g, r):
                act.wait_ge(f.y_in[us[0] // f.half], 32 * (f.half * g + len(us)))
                for b, u in enumerate(us):
                    last = act.activation(f.y_a[u][0:r, :], f.y_a[u][0:r, :], ACT.Identity, scale=weights_1[0:r, bass.ds(i + b, 1)])
                last.then_inc(f.weighed, 1)

            def final_root(f, m, n, r):
                act.wait_ge(f.var, m + 1)
                act.activation(tok_small[0:r, 1, 0:n], tok_small[0:r, 0, 0:n], ACT.Sqrt).then_inc(f.sd, 1)

            def final_store(f, m, i, us, r):
                act.wait_ge(f.ready, m + 1)
                for b, u in enumerate(us):
                    act.dma_start(out[tile_rows(i + b, r), :], f.res[u][0:r, :]).then_inc(f.stored[u // f.half], 16)

            act.wait_ge(tok_chosen, TT)
            act.activation(gaps_exp[:], gaps[:], ACT.Exp).then_inc(gaps_raised, 1)

            act.wait_ge(steps_ready, 2)
            fill_zeros(act, 1, X // 2, X)

            def late_step(s, r, g, finishing):
                i = 2 * g + r // 2
                keep_h(late, s, r, g)
                if finishing and r % 2 == 0 and not (isinstance(s, int) and s == 0):
                    final_store(fin_early, i - 1, i - 1, [1 - r // 2], TR)
                if finishing and r % 2:
                    final_root(fin_early, i, 1, TR)
                if not (isinstance(s, int) and s >= late.steps - 2):
                    keep_xs(late, s + 2, (r + 2) % 4, g + (r + 2) // 4)
                if not (isinstance(s, int) and s == 0):
                    store_y(late, s - 1, (r - 1) % 4, g + (r - 1) // 4)
                if finishing and r % 2 == 0:
                    final_weigh(fin_early, i, [r // 2], g, TR)

            keep_xs(late, 0, 0, 0)
            keep_xs(late, 1, 1, 0)
            act.wait_ge(weights_ready, 1)
            late_steps(act, late.steps, late_step)
            store_y(late, late.steps - 1, (late.steps - 1) % 4, (late.steps - 1) // 4)
            final_store(fin_early, TE - 1, TE - 1, [1], TR)

            def finish_group(m, g, h, n, r):
                final_root(fin_late, m, n, r)
                if not (isinstance(m, int) and m == FOURS + 1):
                    n_next, r_next = 4, TR
                    if isinstance(m, int) and m >= FOURS - 1:
                        n_next, r_next = ((LEFT, TR), (1, TLAST))[m - FOURS + 1]
                    final_weigh(fin_late, tile_of(m + 1), [4 * (1 - h) + b for b in range(n_next)], g + h, r_next)
                final_store(fin_late, m, tile_of(m), [4 * h + b for b in range(n)], r)

            final_weigh(fin_late, TE, [0, 1, 2, 3], 0, TR)
            late_groups(act, finish_group)

        @block.vector
        def _(dve):
            dve.memset(pad_i[:, 0:P], 0).then_inc(fills, 1)
            dve.memset(pad_i[:, P:3 * P], N - 1).then_inc(fills, 1)
            dve.memset(base_row[:, 0:1], 0).then_inc(fills, 1)
            dve.memset(ones[:], 1.0)
            dve.memset(zeros[:], 0.0)
            dve.memset(kept[:], 0.0)
            dve.memset(routed[:], 0.0)
            dve.memset(pos_all[:], 0.0)
            dve.memset(exp_all[:], 0.0)
            dve.memset(gaps[:], 0.0)
            dve.memset(base_rowf[:, CH:64], N - 1.0)
            dve.wait_ge(iotas, 5)
            dve.tensor_scalar(ident[:], diff_id[:], 0.0, None, ALU.is_equal)
            dve.tensor_scalar(tri_eye[:, X:2 * X], diff_id[0:X, 0:X], 0.0, None, ALU.is_equal)
            dve.tensor_scalar(tri_eye[:, 0:X], diff_id[0:X, 0:X], 0.0, None, ALU.is_le)
            dve.tensor_scalar(below[:], diff_id[:], 0.0, None, ALU.is_lt)
            dve.drain()
            dve.memset(done[:], 0.0).then_inc(consts_ready, 1)

            def scale_of(small_, mv, r, c0, c1):
                v, sd, a, t, s, z = (small_[0:r, k, c0:c1] for k in range(6))
                dve.reciprocal(a, sd)
                dve.drain()
                dve.tensor_tensor(t, a, a, ALU.mult)
                dve.drain()
                dve.tensor_tensor(t, t, v, ALU.mult)
                dve.drain()
                dve.tensor_scalar(t, t, -0.5, 1.5, ALU.mult, ALU.add)
                dve.drain()
                dve.tensor_tensor(s, a, t, ALU.mult)
                dve.drain()
                return dve.scalar_tensor_tensor(out=z, in0=mv[0:r, c0:c1, 0], scalar=-1.0, in1=s, op0=ALU.mult, op1=ALU.mult)

            def ln_measure(s, b, source, r, n):
                wait(dve, ln_applied, s - 3)
                for k in range(n):
                    dve.bn_stats(ln_stats[0:r, k, :], source[0:r, k, :])
                dve.drain()
                for k in range(n):
                    dve.bn_aggr(ln_mv[b][0:r, k, :], ln_stats[0:r, k, :])
                dve.drain()
                dve.tensor_scalar(ln_small[b][0:r, 0, 0:n], ln_mv[b][0:r, 0:n, 1], EPS, None, ALU.add).then_inc(ln_var, 1)

            def ln_scale(s, b, r, n):
                dve.wait_ge(ln_sd, s + 1)
                scale_of(ln_small[b], ln_mv[b], r, 0, n).then_inc(ln_scaled, 1)

            def ln_group(s, r, g):
                dve.wait_ge(ln_loaded[r], 16 * g + 16)
                ln_measure(s, r, ln_in[r], P, LR)
                if not (isinstance(s, int) and s == 0):
                    ln_scale(s - 1, (r - 1) % 4, P, LR)

            def check_edges():
                dve.wait_ge(base_in, 16)
                dve.tensor_copy(base_rowf[:, 0:CH], base_row[:, 0:CH]).then_inc(base_ready, 1)
                dve.wait_ge(dst_in, 32)
                dve.tensor_tensor(unsorted, dst_all[:, 1:PK + 1], dst_all[:, 0:PK], ALU.is_lt)
                dve.drain()
                dve.tensor_reduce(bad[:, 0:1], unsorted, AX_X, ALU.add)
                dve.wait_ge(base_kept, 1)
                dve.tensor_tensor(delta[:, 1:CH + 1], base[:, 1:CH + 1], base[:, 0:CH], ALU.subtract)
                dve.tensor_tensor(need[:, LAG:CH], base[:, LAG:CH], need[:, LAG:CH], ALU.is_lt)
                dve.drain()
                dve.tensor_scalar(delta[:, CH + 1:64], delta[:, 1:2], 0.0, None, ALU.mult)
                dve.tensor_reduce(bad[:, 1:2], need[:, LAG:CH], AX_X, ALU.add)
                dve.tensor_reduce(bad[:, 2:3], delta[:, 1:CH + 1], AX_X, ALU.max)
                dve.drain()
                dve.memset(delta[:, 0:1], FAR)
                dve.tensor_scalar(bad[:, 2:3], bad[:, 2:3], P - 1.0, None, ALU.is_gt)
                dve.drain()
                dve.tensor_reduce(bad_sum[:], bad[:], AX_X, ALU.add).then_inc(bad_ready, 1)
                dve.wait_ge(bad_summed, 1)
                dve.tensor_scalar(slow_i[:], small[:, 64:65], 0.0, None, ALU.is_gt).then_inc(slow_known, 1)

            ln_groups(dve, ln_group, check_edges)
            dve.wait_ge(tail_loaded, 16)
            ln_measure(LG, 0, tail_in, LTAIL, 1)
            ln_scale(LG - 1, 3, P, LR)
            ln_scale(LG, 0, LTAIL, 1)

            def tok_residual(i, b, m, r):
                dve.drain()
                dve.wait_ge(tok_in[b], 48 * m + 48)
                wait(dve, tok_out[b], 16 * m)
                dve.tensor_tensor(mid_t[0:r, :], x_t[0:r, b, :], bias_sb[0:r, :], ALU.add)
                dve.drain()
                dve.wait_ge(tok_projected, i + 1)
                dve.tensor_tensor(mid_t[0:r, :], mid_t[0:r, :], proj[0][0:r, 0:D], ALU.add)
                dve.drain()
                dve.tensor_tensor(res_t[0:r, b, :], mid_t[0:r, :], beta_sb[0:r, :], ALU.add).then_inc(tok_res, 1)
                dve.bn_stats(tok_stats[0:r, 0, :], mid_t[0:r, :])
                dve.drain()
                dve.bn_aggr(tok_mv[0:r, 0, :], tok_stats[0:r, 0, :])
                dve.drain()
                dve.tensor_scalar(tok_small[0:r, 0, 0:1], tok_mv[0:r, 0:1, 1], EPS, None, ALU.add).then_inc(tok_var, 1)

            def tok_norm(i, b, m, r):
                dve.wait_ge(tok_sd, i + 1)
                scale_of(tok_small, tok_mv, r, 0, 1)
                dve.drain()
                wait(dve, tok_scattered[b], 32 * m)
                dve.tensor_scalar(t_t[0:r, b, :], mid_t[0:r, :], tok_mv[0:r, 0, 0:1], tok_small[0:r, 4, 0:1],
                                  ALU.subtract, ALU.mult).then_inc(tok_t, 1)

            def tok_choose(i, b, m, r):
                dve.wait_ge(tok_gated, i + 1)
                dve.tensor_tensor(logits[0:r, :], small2[0:r, 0:X], gate_b_sb[0:r, :], ALU.add)
                dve.drain()
                dve.max(top_v[0:r, :], logits[0:r, :])
                dve.drain()
                dve.max_index(top_i[0:r, :], top_v[0:r, :], logits[0:r, :])
                dve.tensor_tensor(gaps[0:r, bass.ds(i, 1)], top_v[0:r, 1:2], top_v[0:r, 0:1], ALU.subtract)
                dve.drain()
                dve.tensor_copy(top_f[0:r, :], top_i[0:r, 0:2])
                dve.drain()
                for k in range(2):
                    dve.tensor_scalar(chosen[0:r, k, :], col_id[0:r, 0:X], top_f[0:r, k:k + 1], None, ALU.is_equal)
                dve.drain()
                dve.tensor_tensor(both[0:r, :], chosen[0:r, 0, :], chosen[0:r, 1, :], ALU.add).then_inc(tok_chosen, 1)

            def tok_place(i, b, m, r):
                dve.wait_ge(tok_ranked, i + 1)
                dve.tensor_tensor(place[0:r, :], small2[0:r, X:2 * X], slot_base[0:r, :], ALU.add)
                dve.tensor_tensor(routed[0:r, :], routed[0:r, :], both[0:r, :], ALU.add)
                dve.drain()
                for k in range(2):
                    dve.tensor_tensor(placed[0:r, k, :], chosen[0:r, k, :], place[0:r, :], ALU.mult)
                dve.drain()
                dve.tensor_reduce(pos_f[0:r, :], placed[0:r, :, :], AX_X, ALU.add)
                dve.drain()
                dve.tensor_copy(pos_all[0:r, bass.ds(2 * i, 2)], pos_f[0:r, :])
                dve.tensor_copy(exp_all[0:r, bass.ds(2 * i, 2)], top_f[0:r, :])
                dve.tensor_copy(pos_t[b][0:r, :], pos_f[0:r, :]).then_inc(tok_placed, 1)

            def tokens(i, b, m, r):
                for step in (tok_residual, tok_norm, tok_choose, tok_place):
                    step(i, b, m, r)

            def signal_counted(k):
                dve.drain()
                dve.memset(done[:], 0.0).then_inc(counted, 1)

            def tiles_of(target, counts):
                dve.tensor_scalar(target, counts, 1.0 / P, (P - 1.0) / P - 0.498, ALU.mult, ALU.add)
                dve.drain()
                dve.tensor_scalar(target, target, ROUND, None, ALU.add)
                dve.drain()
                return dve.tensor_scalar(target, target, -ROUND, None, ALU.add)

            def find_tiles(k):
                dve.wait_ge(counted, 2 * k + 2)
                dve.tensor_tensor(zero_f[:], small[:, P:P + X], slot_base[:], ALU.add)
                tiles_of(tiles_T[:, :], small[0:X, 0:P]).then_inc(tiles_ready, 1)
                if k == 0:
                    dve.memset(routed[:], 0.0)
                dve.drain()
                dve.tensor_copy(zero_at[k][:], zero_f[:])

            def find_steps(k):
                dve.wait_ge(cumulated, k + 1)
                dve.tensor_copy(tiles_C[:], small[:, 2 * P:2 * P + 2 * X])
                dve.drain()
                dve.tensor_scalar(step_cmp[:], tiles_C[:, 0:X], row_id[:], None, ALU.is_le)
                dve.drain()
                dve.tensor_tensor(step_cum[:], step_cmp[:], tiles_C[:, X:2 * X], ALU.mult)
                dve.tensor_reduce(step_f[:, 0:1], step_cmp[:], AX_X, ALU.add)
                dve.drain()
                dve.tensor_reduce(step_f[:, 1:2], step_cum[:], AX_X, ALU.add)
                dve.drain()
                dve.tensor_tensor(step_f[:, 2:3], row_id[:], step_f[:, 1:2], ALU.subtract)
                dve.tensor_scalar(step_f[:, 3:4], step_f[:, 0:1], float(CAP), None, ALU.mult)
                dve.drain()
                dve.scalar_tensor_tensor(out=step_f[:, 3:4], in0=step_f[:, 2:3], scalar=float(P), in1=step_f[:, 3:4], op0=ALU.mult, op1=ALU.add)
                dve.tensor_scalar(step_f[:, 0:1], step_f[:, 0:1], X - 1.0, None, ALU.min)
                dve.drain()
                dve.tensor_copy(step_i[k][:, 0:1], step_f[:, 3:4])
                dve.tensor_copy(step_i[k][:, 1:2], step_f[:, 0:1])
                dve.drain()
                dve.memset(done[:], 0.0).then_inc(steps_ready, 1)

            def fix_places(k):
                dve.tensor_tensor(slot_fix[:], tiles_C[:, 0:X], tiles_C[:, X:2 * X], ALU.subtract)
                dve.drain()
                dve.tensor_scalar(slot_fix[:], slot_fix[:], float(P), float(P * STEPS[0] * k), ALU.mult, ALU.add)
                dve.drain()
                dve.tensor_tensor(slot_fix[:], slot_fix[:], slot_base[:], ALU.subtract)
                cols = slice(2 * TE, 2 * TT) if k else slice(0, 2 * TE)
                for e in range(X):
                    dve.drain()
                    dve.tensor_scalar(pos_fix[:, cols], exp_all[:, cols], float(e), slot_fix[:, e:e + 1], ALU.is_equal, ALU.mult)
                    dve.drain()
                    dve.tensor_tensor(pos_all[:, cols], pos_all[:, cols], pos_fix[:, cols], ALU.add)

            table_parts = (signal_counted, find_tiles, find_steps, fix_places)

            def keep_up(f, s, r, g):
                b, u = r % f.depth, r % f.ring
                dve.wait_ge(f.bias_in[u], 16 * uses(r, g, f.ring) + 16)
                wait(dve, f.h_turned, s - f.depth + 1)
                dve.wait_ge(f.up_done, s + 1)
                dve.tensor_tensor(f.hb[b], f.up_out[b], f.bias[u][:, 0:F], ALU.add).then_inc(f.up_kept, 1)

            def keep_down(f, s, r, g):
                b, u = r % f.depth, r % f.ring
                wait(dve, f.y_out[b], 16 * uses(r, g, f.depth))
                dve.wait_ge(f.down_done, s + 1)
                dve.tensor_tensor(f.ys[b], f.down_out[b], f.bias[u][:, F:F + D], ALU.add)
                dve.drain()
                dve.tensor_tensor(f.ys[b], f.ys[b], f.xs[u], ALU.add).then_inc(f.y_kept, 1)

            def early_step(s, r, g):
                keep_up(early, s, r, g)
                keep_down(early, s, r, g)

            def select_chunk(hop, c, b, q, steps=None):
                n = c + CH * hop
                dve.wait_ge(edges_in[b], 48 * (q + CH // 2 * hop) + 48)
                dve.tensor_scalar(dst_rel[b][:], dst_t[b][:], base[:, bass.ds(c, 1)], None, ALU.subtract)
                wait(dve, window_summed, n - 1)
                dve.tensor_scalar(shift[:, b, :], diff_id[:], delta[:, bass.ds(c, 1)], None, ALU.is_equal).then_inc(shift_built, 1)
                dve.drain()
                for j in range(CT):
                    wait(dve, tile_summed, CT * n + j - SR + 1)
                    dve.tensor_scalar(sel[:, j % SR, :], col_id[:], dst_rel[b][:, j:j + 1], w_t[b][:, j:j + 1],
                                      ALU.is_equal, ALU.mult).then_inc(sel_built, 1)
                    if steps and j in steps:
                        steps[j]()

            def with_tokens(i, b, m):
                at = {j: (lambda f=f: f(i, b, m, TR)) for j, f in ((15, tok_residual), (17, tok_norm))}
                if not (isinstance(i, int) and i == 0):
                    at.update({j: (lambda f=f: f(i - 1, 1 - b, None, TR)) for j, f in ((1, tok_choose), (8, tok_place))})
                return at

            def with_steps(g, b):
                at = {}
                for n, r in enumerate((2 * b, 2 * b + 1)):
                    at[SR * n + 6 - n] = lambda r=r: keep_up(early, 4 * g + r, r, g)
                    at[SR * n + 12] = lambda r=r: keep_down(early, 4 * g + r, r, g)
                return at

            def with_table():
                return {j: (lambda f=f: f(0)) for j, f in zip((9, 13, 16, 19), table_parts)}

            dve.wait_ge(slow_known, 1)
            slow = dve.value_load(slow_i[0:1, 0:1], min_val=0, max_val=1)
            with dve.If(slow):
                for hop in range(2):
                    with dve.Fori(0, ETILES) as k:
                        for loaded in slow_loaded[hop][1:]:
                            dve.wait_ge(loaded, 16 * k + 16)
                        dve.tensor_copy(s_dstf[:], s_dst[:])
                        dve.tensor_copy(s_dst_rowf, s_dst_row)
                        dve.drain()
                        dve.tensor_scalar(s_same_w, s_dst_rowf, s_dstf[:], s_w[:], ALU.is_equal, ALU.mult)
                        dve.scalar_tensor_tensor(out=s_same_below, in0=s_dst_rowf, scalar=s_dstf[:, 0:1], in1=below[:],
                                                 op0=ALU.is_equal, op1=ALU.mult)
                        dve.drain()
                        dve.engine_nop().then_inc(slow_sel, 1)
                        dve.wait_ge(slow_rows[hop][1], 16 * k + 16)
                        dve.wait_ge(slow_summed, k + 1 + ETILES * hop)
                        dve.tensor_tensor(s_new, s_old, win[0][:, 0:D], ALU.add)
                        dve.tensor_scalar(s_repf[:], small[:, 0:1], 0.0, OUT, ALU.is_gt, ALU.mult)
                        dve.drain()
                        dve.tensor_tensor(s_rep[:], s_repf[:], s_dstf[:], ALU.add)
                        dve.drain()
                        dve.tensor_copy(s_put[:], s_rep[:]).then_inc(slow_new, 1)
                tokens(0, 0, 0, TR)
                tokens(1, 1, 0, TR)
                with dve.Fori(1, TE // 2) as m:
                    tokens(2 * m, 0, m, TR)
                    tokens(2 * m + 1, 1, m, TR)
                for part_of_table in table_parts:
                    part_of_table(0)
                steps_of_four(dve, early.steps, early_step)
                with dve.Fori(TE // 2, TT // 2) as m:
                    tokens(2 * m, 0, m, TR)
                    tokens(2 * m + 1, 1, m, TR)
                tokens(TT - 1, 0, TT // 2, TLAST)
            with dve.Else():
                select_chunk(0, 0, 0, 0)
                select_chunk(0, 1, 1, 0)
                with dve.Fori(1, CH // 2) as q:
                    select_chunk(0, 2 * q, 0, q)
                    select_chunk(0, 2 * q + 1, 1, q)
                with dve.Fori(0, LAG // 2) as q:
                    select_chunk(1, 2 * q, 0, q)
                    select_chunk(1, 2 * q + 1, 1, q)
                q0 = LAG // 2
                select_chunk(1, LAG, 0, q0, with_tokens(0, 0, 0))
                select_chunk(1, LAG + 1, 1, q0, with_tokens(1, 1, 0))

                def full_chunk(q, b, others):
                    select_chunk(1, 2 * q + b, b, q, {**with_tokens(2 * q + b - LAG, b, q - q0), **others})

                first = EARLY // 2
                with dve.Fori(q0 + 1, first - 1) as q:
                    full_chunk(q, 0, {})
                    full_chunk(q, 1, {})
                full_chunk(first - 1, 0, with_table())
                full_chunk(first - 1, 1, {})
                full_chunk(first, 0, with_steps(0, 0))
                full_chunk(first, 1, with_steps(0, 1))
                with dve.Fori(first + 1, CH // 2 - 1) as q:
                    full_chunk(q, 0, with_steps(q - first, 0))
                    full_chunk(q, 1, with_steps(q - first, 1))
                full_chunk(CH // 2 - 1, 0, with_steps(CH // 2 - 1 - first, 0))
                full_chunk(CH // 2 - 1, 1, {})
                tok_choose(*left_tiles[0])
                tok_place(*left_tiles[0])
                tok_residual(*left_tiles[1])
                tok_norm(*left_tiles[1])
                for n in (1, 2):
                    tok_residual(*left_tiles[n + 1])
                    tok_choose(*left_tiles[n])
                    tok_norm(*left_tiles[n + 1])
                    tok_place(*left_tiles[n])
                tok_choose(*left_tiles[3])
                tok_place(*left_tiles[3])

            for part_of_table in table_parts:
                part_of_table(1)
            dve.wait_ge(gaps_raised, 1)
            dve.tensor_scalar(gaps_sum[:], gaps_exp[:], 1.0, None, ALU.add)
            dve.drain()
            dve.reciprocal(weights_1[:], gaps_sum[:])
            dve.drain()
            dve.tensor_tensor(weights_2[:], gaps_exp[:], weights_1[:], ALU.mult).then_inc(weights_ready, 1)

            def stage_places(f, i, us):
                for b, u in enumerate(us):
                    dve.tensor_copy(f.pos[u][:], pos_all[:, bass.ds(2 * (i + b), 2)]).then_inc(f.pos_staged, 1)

            def final_mix(f, m, i, us, r, next_i, next_us):
                n = len(us)
                dve.wait_ge(f.weighed, m + 1)
                for b, u in enumerate(us):
                    last = dve.scalar_tensor_tensor(out=f.sum[u][0:r, :], in0=f.y_b[u][0:r, :], scalar=weights_2[0:r, bass.ds(i + b, 1)],
                                                    in1=f.y_a[u][0:r, :], op0=ALU.mult, op1=ALU.add)
                last.then_inc(f.mixed, 1)
                dve.drain()
                stage_places(f, next_i, next_us)
                for b, u in enumerate(us):
                    dve.bn_stats(tok_stats[0:r, b, :], f.sum[u][0:r, :])
                dve.drain()
                for b in range(n):
                    dve.bn_aggr(tok_mv[0:r, b, :], tok_stats[0:r, b, :])
                dve.drain()
                dve.tensor_scalar(tok_small[0:r, 0, 0:n], tok_mv[0:r, 0:n, 1], EPS, None, ALU.add).then_inc(f.var, 1)
                for b, u in enumerate(us):
                    dve.scalar_tensor_tensor(out=f.sum[u][0:r, :], in0=f.sum[u][0:r, :], scalar=tok_mv[0:r, b, 0:1],
                                             in1=gamma_sb[0:r, :], op0=ALU.subtract, op1=ALU.mult)

            def final_add(f, m, us, g, r):
                dve.wait_ge(f.sd, m + 1)
                scale_of(tok_small, tok_mv, r, 0, len(us))
                dve.drain()
                dve.wait_ge(f.res_in[us[0] // f.half], 16 * (f.half * g + len(us)))
                for b, u in enumerate(us):
                    last = dve.scalar_tensor_tensor(out=f.res[u][0:r, :], in0=f.sum[u][0:r, :], scalar=tok_small[0:r, 4, b:b + 1],
                                                    in1=f.res[u][0:r, :], op0=ALU.mult, op1=ALU.add)
                last.then_inc(f.ready, 1)

            def late_step(s, r, g, finishing):
                if not (isinstance(s, int) and s == late.steps - 1):
                    keep_up(late, s + 1, (r + 1) % 4, g + (r + 1) // 4)
                keep_down(late, s, r, g)
                i, us = 2 * g + r // 2, [r // 2]
                if finishing and r % 2 == 0:
                    final_mix(fin_early, i, i, us, TR, i + 2, us)
                elif finishing:
                    final_add(fin_early, i, us, g, TR)

            dve.drain()
            stage_places(fin_early, 0, [0, 1])
            stage_places(fin_late, TE, list(range(8)))
            keep_up(late, 0, 0, 0)
            late_steps(dve, late.steps, late_step)

            def finish_group(m, g, h, n, r):
                us = [4 * h + b for b in range(n)]
                after = 4
                if isinstance(m, int) and m >= FOURS - 2:
                    after = (LEFT, 1, 0, 0)[m - FOURS + 2]
                final_mix(fin_late, m, tile_of(m), us, r, tile_of(m + 2), us[:after])
                final_add(fin_late, m, us, g, r)

            wait_all_out(dve)
            late_groups(dve, finish_group)

        @block.tensor
        def _(pe):
            pe.wait_ge(consts_ready, 1)
            pe.wait_ge(base_ready, 1)
            pe.matmul(small[:, 0:64], ones[0:1, :], base_rowf[:, :], start=True, stop=True).then_inc(base_spread, 1)
            pe.wait_ge(bad_ready, 1)
            pe.matmul(small[:, 64:65], ones[:], bad_sum[:], start=True, stop=True).then_inc(bad_summed, 1)
            pe.wait_ge(params_in, 96)

            def tok_turn(i, b, m, r):
                pe.wait_ge(tok_in[b], 48 * m + 48)
                wait(pe, tok_turned_kept, i)
                for k in range(2 * DH):
                    last = pe.transpose(turn[:, k * P:k * P + r], h_t[0:r, b, k * P:(k + 1) * P], ident[0:r, 0:r])
                last.then_inc(tok_turned, 1)

            def tok_project(i, b, m, r):
                wait(pe, tok_res, i)
                pe.wait_ge(tok_turned_kept, i + 1)
                for k in range(2 * DH):
                    last = pe.matmul(proj[0][0:r, 0:D], hT_t[:, k, 0:r], gnn_w_sb[:, k, :], start=(k == 0), stop=(k == 2 * DH - 1))
                last.then_inc(tok_projected, 1)

            def tok_turn_t(i, b, m, r):
                wait(pe, t_turned_kept, i)
                pe.wait_ge(tok_t, i + 1)
                for k in range(DH):
                    last = pe.transpose(turn2[:, k * P:k * P + r], t_t[0:r, b, k * P:(k + 1) * P], ident[0:r, 0:r])
                last.then_inc(t_turned, 1)

            def tok_gate(i, b, m, r):
                wait(pe, tok_placed, i)
                pe.wait_ge(t_turned_kept, i + 1)
                for k in range(DH):
                    last = pe.matmul(small2[0:r, 0:X], tT_t[:, k, 0:r], gate_w_sb[:, k, :], start=(k == 0), stop=(k == DH - 1))
                last.then_inc(tok_gated, 1)

            def tok_rank(i, b, m, r):
                pe.wait_ge(tok_chosen, i + 1)
                pe.matmul(small2[0:r, X:2 * X], below[0:r, 0:r], both[0:r, :], start=True, stop=False)
                pe.matmul(small2[0:r, X:2 * X], ones[:, 0:r], routed[:, :], start=False, stop=True).then_inc(tok_ranked, 1)

            def tokens(i, b, m, r):
                for step in (tok_turn, tok_project, tok_turn_t, tok_gate, tok_rank):
                    step(i, b, m, r)

            def count_tokens(k):
                pe.wait_ge(counted, 2 * k + 1)
                pe.matmul(small[0:X, 0:P], routed[:, :], ones[:], start=True, stop=True)
                pe.matmul(small[:, P:P + X], ones[:], routed[:, :], start=True, stop=True).then_inc(counted, 1)

            def cumulate(k):
                pe.wait_ge(tiles_ready, k + 1)
                pe.matmul(small[:, 2 * P:2 * P + 2 * X], tiles_T[:, :], tri_eye[:, :], start=True, stop=True).then_inc(cumulated, 1)

            def turn_xs(f, s, r, g):
                u = r % f.ring
                pe.wait_ge(f.xs_in[u], 16 * uses(r, g, f.ring) + 16)
                wait(pe, f.xs_kept, s)
                for k in range(DH):
                    last = pe.transpose(f.xs_out[:, k * P:(k + 1) * P], f.xs[u][:, k * P:(k + 1) * P], ident[:])
                last.then_inc(f.xs_turned, 1)

            def expert_of(f, s):
                return pe.value_load(step_row[f.k][0:1, bass.ds(2 * s + 1, 1)], min_val=0, max_val=X - 1)

            def up(f, s, r, g):
                b = r % f.depth
                e = expert_of(f, s)
                wait(pe, f.up_kept if f is late else f.y_kept, s - f.depth + 1)
                pe.wait_ge(f.xs_kept, s + 1)
                for k in range(DH):
                    last = pe.matmul(f.up_out[b], f.xsT[b][:, k, :], w1_sb[:, bass.ds(e * DH + k, 1), :], start=(k == 0), stop=(k == DH - 1))
                last.then_inc(f.up_done, 1)

            def turn_h(f, s, r, g):
                wait(pe, f.h_kept, s)
                pe.wait_ge(f.up_kept, s + 1)
                for k in range(FH):
                    last = pe.transpose(f.h_out[:, k * P:(k + 1) * P], f.hb[r % f.depth][:, k * P:(k + 1) * P], ident[:])
                last.then_inc(f.h_turned, 1)

            def down(f, s, r, g):
                b = r % f.depth
                e = expert_of(f, s)
                wait(pe, f.y_kept, s - f.depth + 1)
                pe.wait_ge(f.h_kept, s + 1)
                for k in range(FH):
                    last = pe.matmul(f.down_out[b], f.hT[b][:, k, :], w2_sb[:, bass.ds(e * FH + k, 1), :], start=(k == 0), stop=(k == FH - 1))
                last.then_inc(f.down_done, 1)

            def early_step(s, r, g):
                for part_of_step in (turn_xs, up, turn_h, down):
                    part_of_step(early, s, r, g)

            def with_tokens(i, b, m, r):
                at = {j: (lambda f=f: f(i, b, m, r)) for j, f in ((8, tok_turn), (11, tok_project), (19, tok_turn_t), (21, tok_gate))}
                if not (isinstance(i, int) and i == 0):
                    at[4] = lambda: tok_rank(i - 1, 1 - b, None, r)
                return at

            def with_table():
                return {10: lambda: count_tokens(0), 14: lambda: cumulate(0)}

            def with_steps(g, b):
                return {j: (lambda f=f, r=2 * b + n: f(early, 4 * g + r, r, g))
                        for n, places in enumerate(((0, 3, 6, 9), (12, 16, 18, 22)))
                        for j, f in zip(places, (turn_xs, up, turn_h, down))}

            def sum_chunk(hop, c, b, others={}):
                n = c + CH * hop
                wait(pe, window_kept, n - 1)
                for j in range(CT):
                    pe.wait_ge(sel_built, CT * n + j + 1)
                    pe.wait_ge(rows_in[j % SR], 16 * (2 * n + j // SR) + 16)
                    pe.matmul(win[b][:, 0:D], sel[:, j % SR, :], rows[:, j % SR, :], start=(j == 0), stop=False).then_inc(tile_summed, 1)
                    if j in others:
                        others[j]()
                pe.wait_ge(shift_built, n + 1)
                wait(pe, window_kept, n)
                pe.matmul(win[b][:, 0:D], shift[:, b, :], kept[:, 1 - b, :], start=False, stop=True).then_inc(window_summed, 1)

            pe.wait_ge(slow_known, 1)
            slow = pe.value_load(slow_i[0:1, 0:1], min_val=0, max_val=1)
            with pe.If(slow):
                for hop in range(2):
                    with pe.Fori(0, ETILES) as k:
                        pe.wait_ge(slow_sel, k + 1 + ETILES * hop)
                        pe.wait_ge(slow_rows[hop][0], 16 * k + 16)
                        pe.matmul(win[0][:, 0:D], s_same_w, s_rows, start=True, stop=True)
                        pe.matmul(small[:, 0:1], s_same_below, ones[:, 0:1], start=True, stop=True).then_inc(slow_summed, 1)
                tokens(0, 0, 0, TR)
                tokens(1, 1, 0, TR)
                with pe.Fori(1, TE // 2) as m:
                    tokens(2 * m, 0, m, TR)
                    tokens(2 * m + 1, 1, m, TR)
                count_tokens(0)
                cumulate(0)
                pe.wait_ge(weights_in, 16 * 2 * X)
                pe.wait_ge(steps_in, 16)
                steps_of_four(pe, early.steps, early_step)
                with pe.Fori(TE // 2, TT // 2) as m:
                    tokens(2 * m, 0, m, TR)
                    tokens(2 * m + 1, 1, m, TR)
                tokens(TT - 1, 0, TT // 2, TLAST)
            with pe.Else():
                sum_chunk(0, 0, 0)
                sum_chunk(0, 1, 1)
                with pe.Fori(1, CH // 2) as q:
                    sum_chunk(0, 2 * q, 0)
                    sum_chunk(0, 2 * q + 1, 1)
                with pe.Fori(0, LAG // 2) as q:
                    sum_chunk(1, 2 * q, 0)
                    sum_chunk(1, 2 * q + 1, 1)
                sum_chunk(1, LAG, 0, with_tokens(0, 0, 0, TR))
                sum_chunk(1, LAG + 1, 1, with_tokens(1, 1, 0, TR))

                def full_chunk(q, b, others):
                    sum_chunk(1, 2 * q + b, b, {**with_tokens(2 * q + b - LAG, b, q - LAG // 2, TR), **others})

                first = EARLY // 2
                with pe.Fori(LAG // 2 + 1, first - 1) as q:
                    full_chunk(q, 0, {})
                    full_chunk(q, 1, {})
                full_chunk(first - 1, 0, with_table())
                full_chunk(first - 1, 1, {})
                pe.wait_ge(weights_in, 16 * 2 * X)
                pe.wait_ge(steps_in, 16)
                full_chunk(first, 0, with_steps(0, 0))
                full_chunk(first, 1, with_steps(0, 1))
                with pe.Fori(first + 1, CH // 2 - 1) as q:
                    full_chunk(q, 0, with_steps(q - first, 0))
                    full_chunk(q, 1, with_steps(q - first, 1))
                full_chunk(CH // 2 - 1, 0, with_steps(CH // 2 - 1 - first, 0))
                full_chunk(CH // 2 - 1, 1, {})
                tok_turn(*left_tiles[1])
                tok_project(*left_tiles[1])
                tok_rank(*left_tiles[0])
                for n in (1, 2, 3):
                    tok_turn_t(*left_tiles[n])
                    if n < 3:
                        tok_turn(*left_tiles[n + 1])
                        tok_project(*left_tiles[n + 1])
                    tok_gate(*left_tiles[n])
                    tok_rank(*left_tiles[n])

            count_tokens(1)
            cumulate(1)

            def late_step(s, r, g):
                known = isinstance(s, int)
                turn_h(late, s, r, g)
                if not (known and s == late.steps - 1):
                    up(late, s + 1, (r + 1) % 4, g + (r + 1) // 4)
                if not (known and s >= late.steps - 2):
                    turn_xs(late, s + 2, (r + 2) % 4, g + (r + 2) // 4)
                down(late, s, r, g)

            pe.wait_ge(steps_in, 32)
            turn_xs(late, 0, 0, 0)
            up(late, 0, 0, 0)
            turn_xs(late, 1, 1, 0)
            steps_of_four(pe, late.steps, late_step)


_INS = ["x", "src", "dst", "edge_weight", "L0_gnn_W", "L0_gnn_bias", "L0_ffn_gate_w", "L0_ffn_gate_b", "L0_ffn_w1",
        "L0_ffn_b1", "L0_ffn_w2", "L0_ffn_b2", "L0_ffn_gamma", "L0_ffn_beta"]


def kernel(**inputs):
    import numpy as np
    import concourse.bacc as bacc
    from concourse.bass_utils import run_bass_kernel_spmd

    nc = bacc.Bacc("TRN2", target_bir_lowering=False, num_devices=1)
    arrays, args = {}, []
    for name in _INS:
        a = np.ascontiguousarray(inputs[name])
        arrays[f"in_{name}"] = a
        args.append(nc.dram_tensor(f"in_{name}", a.shape, mybir.dt.from_np(a.dtype), kind="ExternalInput").ap())
    args.append(nc.dram_tensor("out", (N, D), F32, kind="ExternalOutput").ap())
    build(nc, *args)
    r = run_bass_kernel_spmd(nc, [arrays], core_ids=[0])
    return r.results[0]["out"]
```
